# Optimizing a Trainium2 kernel written in Bass

```python
import numpy as np
import jax
import jax.numpy as jnp

def _softmax(x, axis=-1):
    return jax.nn.softmax(x, axis=axis)

def _gelu(x):
    return jax.nn.gelu(x, approximate=True)

def _silu(x):
    return jax.nn.silu(x)

def _sigmoid(x):
    return jax.nn.sigmoid(x)

def _layernorm(x, axis=-1, eps=1e-05):
    m = jnp.mean(x, axis=axis, keepdims=True)
    v = jnp.var(x, axis=axis, keepdims=True)
    return (x - m) / jnp.sqrt(v + eps)

def _scatter_add(tgt, idx, src, axis=0):
    return tgt.at[idx].add(src)

def _segment_sum(src, seg, n):
    return jax.ops.segment_sum(src, seg, n)
kernel_name = 'mk_adaln_d2_jaxref_r4_688576'

def setup_inputs(seed: int=0):
    np.random.seed(seed)
    _w = jnp.asarray

    def _L0_attn_setup():
        import jax, jax.numpy as jnp
        import numpy as np

        def _logcumsumexp(x, axis):
            return jax.lax.associative_scan(jnp.logaddexp, x, axis=axis)

        def _log_g(x):
            return jnp.where(x >= 0, jnp.log(jax.nn.relu(x) + 0.5), -jax.nn.softplus(-x))

        def _min_gru(x, Wz, bz, Wh, bh):
            k = x @ Wz + bz
            log_z = -jax.nn.softplus(-k)
            log_coeffs = -jax.nn.softplus(k)
            log_tilde_h = _log_g(x @ Wh + bh)
            a_star = jnp.cumsum(log_coeffs, axis=1)
            log_h = a_star + _logcumsumexp(log_z + log_tilde_h - a_star, axis=1)
            return jnp.exp(log_h)
        key = jax.random.key(seed)
        ks = jax.random.split(key, 7)
        B, S, D, H = (4, 1024, 256, 256)
        s_in = 1.0 / np.sqrt(D)
        s_cat = 1.0 / np.sqrt(2 * H)
        return {'x': jax.random.normal(ks[0], (B, S, D), jnp.float32), 'Wz_f': jax.random.normal(ks[1], (D, H), jnp.float32) * s_in, 'bz_f': jnp.zeros((H,), jnp.float32), 'Wh_f': jax.random.normal(ks[2], (D, H), jnp.float32) * s_in, 'bh_f': jnp.zeros((H,), jnp.float32), 'Wz_b': jax.random.normal(ks[3], (D, H), jnp.float32) * s_in, 'bz_b': jnp.zeros((H,), jnp.float32), 'Wh_b': jax.random.normal(ks[4], (D, H), jnp.float32) * s_in, 'bh_b': jnp.zeros((H,), jnp.float32), 'W_out': jax.random.normal(ks[5], (2 * H, H), jnp.float32) * s_cat, 'b_out': jnp.zeros((H,), jnp.float32)}
    _L0_attn_in = _L0_attn_setup()

    def _L0_ffn_setup():
        import jax, jax.numpy as jnp
        import numpy as np
        from jax import lax
        T, B, I, M, O = (64, 64, 256, 256, 256)

        def _xavier(key, shape):
            fan_out, fan_in = shape
            limit = float(np.sqrt(6.0 / (fan_in + fan_out)))
            return jax.random.uniform(key, shape, jnp.float32, -limit, limit)
        key = jax.random.key(seed)
        ks = jax.random.split(key, 9)
        x = jax.random.normal(ks[0], (T, B, I), jnp.float32)
        return {'x': x, 'wf': _xavier(ks[1], (M, I)), 'uf': _xavier(ks[2], (M, M)), 'bf': jnp.zeros((M,), jnp.float32), 'wi': _xavier(ks[3], (M, I)), 'ui': _xavier(ks[4], (M, M)), 'bi': jnp.zeros((M,), jnp.float32), 'wc': _xavier(ks[5], (M, I)), 'uc': _xavier(ks[6], (M, M)), 'bc': jnp.zeros((M,), jnp.float32), 'wo': _xavier(ks[7], (O, I)), 'uo': _xavier(ks[8], (O, M)), 'bo': jnp.zeros((O,), jnp.float32), 'in_c': jnp.zeros((M,), jnp.float32)}
    _L0_ffn_in = _L0_ffn_setup()
    _L0_c = _w((lambda *s: np.random.randn(*s).astype(np.float32) * 0.05)(4, 256))
    _L0_wmod = _w((lambda *s: np.random.randn(*s).astype(np.float32) * 0.05)(256, 6 * 256) * 256 ** (-0.5))

    def _L1_attn_setup():
        import jax, jax.numpy as jnp
        import numpy as np
        B, N, DM, H, FF = (8, 512, 256, 16, 1024)
        D = DM // H // 2
        LAMBDA_INIT = 0.8 - 0.6 * float(np.exp(-0.3 * 1.0))

        def _layernorm(x, g, b, eps=1e-05):
            mu = jnp.mean(x, axis=-1, keepdims=True)
            var = jnp.mean(jnp.square(x - mu), axis=-1, keepdims=True)
            return (x - mu) * jax.lax.rsqrt(var + eps) * g + b

        def _rmsnorm(x, eps=1e-05):
            return x * jax.lax.rsqrt(jnp.mean(x * x, axis=-1, keepdims=True) + eps)

        def _diff_attn(x, Wq, Wk, Wv, lq1, lq2, lk1, lk2, Wo, bo):
            b, n, d = x.shape
            scale = D ** (-0.5)
            q = (x @ Wq.T).reshape(b, n, H, D, 2).transpose(0, 1, 4, 2, 3).reshape(b, n, 2 * H, D) * scale
            k = (x @ Wk.T).reshape(b, n, H, D, 2).transpose(0, 1, 4, 2, 3).reshape(b, n, 2 * H, D)
            v = (x @ Wv.T).reshape(b, n, H, 2 * D).transpose(0, 2, 1, 3)
            att = jnp.einsum('bnqd,bnkd->bnqk', q, k)
            att = jnp.nan_to_num(att)
            att = jax.nn.softmax(att.astype(jnp.float32), axis=-1)
            lam = jnp.exp(jnp.sum(lq1 * lk1)) - jnp.exp(jnp.sum(lq2 * lk2)) + LAMBDA_INIT
            att6 = att.reshape(b, n, 2, H, 2, H)
            att2 = att6[:, :, 0, :, 0, :] - lam * att6[:, :, 1, :, 1, :]
            out = jnp.einsum('bnah,bhnd->bnad', att2, v)
            out = _rmsnorm(out) * (1.0 - LAMBDA_INIT)
            out = out.reshape(b, n, d)
            return out @ Wo.T + bo
        key = jax.random.key(seed)
        ks = jax.random.split(key, 12)
        p = lambda k, sh, s=0.02: jax.random.normal(k, sh, jnp.float32) * s
        return {'x': jax.random.normal(ks[0], (B, N, DM), jnp.float32), 'Wq': p(ks[1], (DM, DM)), 'Wk': p(ks[2], (DM, DM)), 'Wv': p(ks[3], (DM, DM)), 'lq1': p(ks[4], (D,), 0.1), 'lq2': p(ks[5], (D,), 0.1), 'lk1': p(ks[6], (D,), 0.1), 'lk2': p(ks[7], (D,), 0.1), 'Wo': p(ks[8], (DM, DM)), 'bo': jnp.zeros((DM,), jnp.float32), 'ln1_g': jnp.ones((DM,), jnp.float32), 'ln1_b': jnp.zeros((DM,), jnp.float32), 'ln2_g': jnp.ones((DM,), jnp.float32), 'ln2_b': jnp.zeros((DM,), jnp.float32), 'W1': p(ks[9], (FF, DM)), 'b1': jnp.zeros((FF,), jnp.float32), 'W2': p(ks[10], (DM, FF)), 'b2': jnp.zeros((DM,), jnp.float32)}
    _L1_attn_in = _L1_attn_setup()

    def _L1_ffn_setup():
        import jax, jax.numpy as jnp
        import numpy as np
        B, T, E, C, H, G = (2, 512, 8, 256, 512, 16)
        key = jax.random.key(seed)
        ks = jax.random.split(key, 7)
        return {'hidden_states': jax.random.normal(ks[0], (B, T, C), jnp.float32), 'w_red': jax.random.normal(ks[1], (C, G), jnp.float32) * 0.02, 'wg': jax.random.normal(ks[2], (E, G), jnp.float32), 'W1': jax.random.normal(ks[3], (E, C, H), jnp.float32) * 0.02, 'b1': jax.random.normal(ks[4], (E, H), jnp.float32) * 0.02, 'W2': jax.random.normal(ks[5], (E, H, C), jnp.float32) * 0.02, 'b2': jax.random.normal(ks[6], (E, C), jnp.float32) * 0.02}
    _L1_ffn_in = _L1_ffn_setup()
    _L1_c = _w((lambda *s: np.random.randn(*s).astype(np.float32) * 0.05)(4, 256))
    _L1_wmod = _w((lambda *s: np.random.randn(*s).astype(np.float32) * 0.05)(256, 6 * 256) * 256 ** (-0.5))
    _d = {'L0_attn_x': _L0_attn_in['x'], 'L0_attn_Wz_f': _L0_attn_in['Wz_f'], 'L0_attn_bz_f': _L0_attn_in['bz_f'], 'L0_attn_Wh_f': _L0_attn_in['Wh_f'], 'L0_attn_bh_f': _L0_attn_in['bh_f'], 'L0_attn_Wz_b': _L0_attn_in['Wz_b'], 'L0_attn_bz_b': _L0_attn_in['bz_b'], 'L0_attn_Wh_b': _L0_attn_in['Wh_b'], 'L0_attn_bh_b': _L0_attn_in['bh_b'], 'L0_attn_W_out': _L0_attn_in['W_out'], 'L0_attn_b_out': _L0_attn_in['b_out'], 'L0_ffn_wf': _L0_ffn_in['wf'], 'L0_ffn_uf': _L0_ffn_in['uf'], 'L0_ffn_bf': _L0_ffn_in['bf'], 'L0_ffn_wi': _L0_ffn_in['wi'], 'L0_ffn_ui': _L0_ffn_in['ui'], 'L0_ffn_bi': _L0_ffn_in['bi'], 'L0_ffn_wc': _L0_ffn_in['wc'], 'L0_ffn_uc': _L0_ffn_in['uc'], 'L0_ffn_bc': _L0_ffn_in['bc'], 'L0_ffn_wo': _L0_ffn_in['wo'], 'L0_ffn_uo': _L0_ffn_in['uo'], 'L0_ffn_bo': _L0_ffn_in['bo'], 'L0_ffn_in_c': _L0_ffn_in['in_c'], 'L0_c': _L0_c, 'L0_wmod': _L0_wmod, 'L1_attn_Wq': _L1_attn_in['Wq'], 'L1_attn_Wk': _L1_attn_in['Wk'], 'L1_attn_Wv': _L1_attn_in['Wv'], 'L1_attn_lq1': _L1_attn_in['lq1'], 'L1_attn_lq2': _L1_attn_in['lq2'], 'L1_attn_lk1': _L1_attn_in['lk1'], 'L1_attn_lk2': _L1_attn_in['lk2'], 'L1_attn_Wo': _L1_attn_in['Wo'], 'L1_attn_bo': _L1_attn_in['bo'], 'L1_attn_ln1_g': _L1_attn_in['ln1_g'], 'L1_attn_ln1_b': _L1_attn_in['ln1_b'], 'L1_attn_ln2_g': _L1_attn_in['ln2_g'], 'L1_attn_ln2_b': _L1_attn_in['ln2_b'], 'L1_attn_W1': _L1_attn_in['W1'], 'L1_attn_b1': _L1_attn_in['b1'], 'L1_attn_W2': _L1_attn_in['W2'], 'L1_attn_b2': _L1_attn_in['b2'], 'L1_ffn_w_red': _L1_ffn_in['w_red'], 'L1_ffn_wg': _L1_ffn_in['wg'], 'L1_ffn_W1': _L1_ffn_in['W1'], 'L1_ffn_b1': _L1_ffn_in['b1'], 'L1_ffn_W2': _L1_ffn_in['W2'], 'L1_ffn_b2': _L1_ffn_in['b2'], 'L1_c': _L1_c, 'L1_wmod': _L1_wmod}
    _x0 = _d['L0_attn_x']
    _d['L0_attn_x'] = jax.random.normal(jax.random.fold_in(jax.random.key(seed), 1), (4, 1024, 256), dtype=_x0.dtype)
    del _x0
    return _d

def reference(L0_attn_x, L0_attn_Wz_f, L0_attn_bz_f, L0_attn_Wh_f, L0_attn_bh_f, L0_attn_Wz_b, L0_attn_bz_b, L0_attn_Wh_b, L0_attn_bh_b, L0_attn_W_out, L0_attn_b_out, L0_ffn_wf, L0_ffn_uf, L0_ffn_bf, L0_ffn_wi, L0_ffn_ui, L0_ffn_bi, L0_ffn_wc, L0_ffn_uc, L0_ffn_bc, L0_ffn_wo, L0_ffn_uo, L0_ffn_bo, L0_ffn_in_c, L0_c, L0_wmod, L1_attn_Wq, L1_attn_Wk, L1_attn_Wv, L1_attn_lq1, L1_attn_lq2, L1_attn_lk1, L1_attn_lk2, L1_attn_Wo, L1_attn_bo, L1_attn_ln1_g, L1_attn_ln1_b, L1_attn_ln2_g, L1_attn_ln2_b, L1_attn_W1, L1_attn_b1, L1_attn_W2, L1_attn_b2, L1_ffn_w_red, L1_ffn_wg, L1_ffn_W1, L1_ffn_b1, L1_ffn_W2, L1_ffn_b2, L1_c, L1_wmod):

    def _L0_attn_ref(x, Wz_f, bz_f, Wh_f, bh_f, Wz_b, bz_b, Wh_b, bh_b, W_out, b_out):
        import jax, jax.numpy as jnp
        import numpy as np

        def _logcumsumexp(x, axis):
            return jax.lax.associative_scan(jnp.logaddexp, x, axis=axis)

        def _log_g(x):
            return jnp.where(x >= 0, jnp.log(jax.nn.relu(x) + 0.5), -jax.nn.softplus(-x))

        def _min_gru(x, Wz, bz, Wh, bh):
            k = x @ Wz + bz
            log_z = -jax.nn.softplus(-k)
            log_coeffs = -jax.nn.softplus(k)
            log_tilde_h = _log_g(x @ Wh + bh)
            a_star = jnp.cumsum(log_coeffs, axis=1)
            log_h = a_star + _logcumsumexp(log_z + log_tilde_h - a_star, axis=1)
            return jnp.exp(log_h)
        x_rev = jnp.flip(x, axis=1)
        out_fwd = _min_gru(x, Wz_f, bz_f, Wh_f, bh_f)
        out_bwd = _min_gru(x_rev, Wz_b, bz_b, Wh_b, bh_b)
        concat = jnp.concatenate([out_fwd, out_bwd], axis=2)
        return concat @ W_out + b_out

    def _L0_ffn_ref(x, wf, uf, bf, wi, ui, bi, wc, uc, bc, wo, uo, bo, in_c):
        import jax, jax.numpy as jnp
        import numpy as np
        from jax import lax
        T, B, I, M, O = (64, 64, 256, 256, 256)

        def _xavier(key, shape):
            fan_out, fan_in = shape
            limit = float(np.sqrt(6.0 / (fan_in + fan_out)))
            return jax.random.uniform(key, shape, jnp.float32, -limit, limit)
        batch = x.shape[1]
        c0 = jnp.broadcast_to(in_c, (batch, in_c.shape[0]))

        def step(c, xt):
            ft = jax.nn.sigmoid(xt @ wf.T + c @ uf.T + bf)
            it = jax.nn.sigmoid(xt @ wi.T + c @ ui.T + bi)
            gt = jnp.tanh(xt @ wc.T + c @ uc.T + bc)
            c = ft * c + it * gt
            return (c, None)
        c_final, _ = lax.scan(step, c0, x)
        h = jnp.tanh(jnp.einsum('tbi,oi->tbo', x, wo) + c_final @ uo.T + bo)
        return h

    def _L1_attn_ref(x, Wq, Wk, Wv, lq1, lq2, lk1, lk2, Wo, bo, ln1_g, ln1_b, ln2_g, ln2_b, W1, b1, W2, b2):
        import jax, jax.numpy as jnp
        import numpy as np
        B, N, DM, H, FF = (8, 512, 256, 16, 1024)
        D = DM // H // 2
        LAMBDA_INIT = 0.8 - 0.6 * float(np.exp(-0.3 * 1.0))

        def _layernorm(x, g, b, eps=1e-05):
            mu = jnp.mean(x, axis=-1, keepdims=True)
            var = jnp.mean(jnp.square(x - mu), axis=-1, keepdims=True)
            return (x - mu) * jax.lax.rsqrt(var + eps) * g + b

        def _rmsnorm(x, eps=1e-05):
            return x * jax.lax.rsqrt(jnp.mean(x * x, axis=-1, keepdims=True) + eps)

        def _diff_attn(x, Wq, Wk, Wv, lq1, lq2, lk1, lk2, Wo, bo):
            b, n, d = x.shape
            scale = D ** (-0.5)
            q = (x @ Wq.T).reshape(b, n, H, D, 2).transpose(0, 1, 4, 2, 3).reshape(b, n, 2 * H, D) * scale
            k = (x @ Wk.T).reshape(b, n, H, D, 2).transpose(0, 1, 4, 2, 3).reshape(b, n, 2 * H, D)
            v = (x @ Wv.T).reshape(b, n, H, 2 * D).transpose(0, 2, 1, 3)
            att = jnp.einsum('bnqd,bnkd->bnqk', q, k)
            att = jnp.nan_to_num(att)
            att = jax.nn.softmax(att.astype(jnp.float32), axis=-1)
            lam = jnp.exp(jnp.sum(lq1 * lk1)) - jnp.exp(jnp.sum(lq2 * lk2)) + LAMBDA_INIT
            att6 = att.reshape(b, n, 2, H, 2, H)
            att2 = att6[:, :, 0, :, 0, :] - lam * att6[:, :, 1, :, 1, :]
            out = jnp.einsum('bnah,bhnd->bnad', att2, v)
            out = _rmsnorm(out) * (1.0 - LAMBDA_INIT)
            out = out.reshape(b, n, d)
            return out @ Wo.T + bo
        skip = x
        h = _layernorm(x, ln1_g, ln1_b)
        src2 = _diff_attn(h, Wq, Wk, Wv, lq1, lq2, lk1, lk2, Wo, bo)
        conn = skip + src2
        skip2 = conn
        h2 = _layernorm(conn, ln2_g, ln2_b)
        src3 = jax.nn.relu(h2 @ W1.T + b1) @ W2.T + b2
        return skip2 + src3

    def _L1_ffn_ref(hidden_states, w_red, wg, W1, b1, W2, b2):
        import jax, jax.numpy as jnp
        import numpy as np
        B, T, E, C, H, G = (2, 512, 8, 256, 512, 16)
        b, t, c = hidden_states.shape
        x = hidden_states.reshape(-1, c)
        x_red = x @ w_red
        wg_n = wg / jnp.maximum(jnp.linalg.norm(wg, axis=1, keepdims=True), 0.0001)
        logits = x_red @ wg_n.T
        gates = jax.nn.softmax(logits, axis=1)
        scores = jnp.max(gates, axis=1)
        idx = jnp.argmax(gates, axis=1)
        h = jnp.einsum('nc,ech->neh', x, W1) + b1[None]
        h = jnp.take_along_axis(h, idx[:, None, None], axis=1)[:, 0, :]
        h = jax.nn.gelu(h, approximate=False)
        o = jnp.einsum('nh,ehc->nec', h, W2) + b2[None]
        o = jnp.take_along_axis(o, idx[:, None, None], axis=1)[:, 0, :]
        o = o * scores[:, None]
        return o.reshape(b, t, c)
    x = L0_attn_x
    mod = (_silu(L0_c) @ L0_wmod).reshape(L0_c.shape[0], 6, 1, -1)
    sa, ca, ga, sb, cb, gb = (mod[:, 0], mod[:, 1], mod[:, 2], mod[:, 3], mod[:, 4], mod[:, 5])
    ga = (2 * (ga >= 0) - 1) * jnp.maximum(jnp.abs(ga), 0.25)
    gb = (2 * (gb >= 0) - 1) * jnp.maximum(jnp.abs(gb), 0.25)
    h = _layernorm(x, axis=-1) * (1 + ca) + sa
    x = x + ga * _L0_attn_ref(h, L0_attn_Wz_f, L0_attn_bz_f, L0_attn_Wh_f, L0_attn_bh_f, L0_attn_Wz_b, L0_attn_bz_b, L0_attn_Wh_b, L0_attn_bh_b, L0_attn_W_out, L0_attn_b_out)
    h = _layernorm(x, axis=-1) * (1 + cb) + sb
    x = x + gb * _L0_ffn_ref(h, L0_ffn_wf, L0_ffn_uf, L0_ffn_bf, L0_ffn_wi, L0_ffn_ui, L0_ffn_bi, L0_ffn_wc, L0_ffn_uc, L0_ffn_bc, L0_ffn_wo, L0_ffn_uo, L0_ffn_bo, L0_ffn_in_c)
    mod = (_silu(L1_c) @ L1_wmod).reshape(L1_c.shape[0], 6, 1, -1)
    sa, ca, ga, sb, cb, gb = (mod[:, 0], mod[:, 1], mod[:, 2], mod[:, 3], mod[:, 4], mod[:, 5])
    ga = (2 * (ga >= 0) - 1) * jnp.maximum(jnp.abs(ga), 0.25)
    gb = (2 * (gb >= 0) - 1) * jnp.maximum(jnp.abs(gb), 0.25)
    h = _layernorm(x, axis=-1) * (1 + ca) + sa
    x = x + ga * _L1_attn_ref(h, L1_attn_Wq, L1_attn_Wk, L1_attn_Wv, L1_attn_lq1, L1_attn_lq2, L1_attn_lk1, L1_attn_lk2, L1_attn_Wo, L1_attn_bo, L1_attn_ln1_g, L1_attn_ln1_b, L1_attn_ln2_g, L1_attn_ln2_b, L1_attn_W1, L1_attn_b1, L1_attn_W2, L1_attn_b2)
    h = _layernorm(x, axis=-1) * (1 + cb) + sb
    x = x + gb * _L1_ffn_ref(h, L1_ffn_w_red, L1_ffn_wg, L1_ffn_W1, L1_ffn_b1, L1_ffn_W2, L1_ffn_b2)
    return x

_drawn_inputs = setup_inputs


def setup_inputs(seed=0):
    import zlib

    import numpy as np

    out = dict(_drawn_inputs(seed))
    spreads = {'L0_attn_bz_f': (0.0, 0.8),
     'L0_attn_bh_f': (0.0, 0.701),
     'L0_attn_bz_b': (0.0, 0.8),
     'L0_attn_bh_b': (0.0, 0.662),
     'L0_attn_b_out': (0.0, 0.346),
     'L0_ffn_bf': (0.0, 0.8),
     'L0_ffn_bi': (0.0, 0.8),
     'L0_ffn_bc': (0.0, 0.772),
     'L0_ffn_bo': (0.0, 0.493),
     'L0_ffn_in_c': (0.0, 0.8),
     'L1_attn_bo': (0.0, 0.352),
     'L1_attn_ln1_g': (1.0, 0.6),
     'L1_attn_ln1_b': (0.0, 0.8),
     'L1_attn_ln2_g': (1.0, 0.6),
     'L1_attn_ln2_b': (0.0, 0.8),
     'L1_attn_b1': (0.0, 0.722),
     'L1_attn_b2': (0.0, 0.353)}
    factors = {'L0_ffn_wf': 3.351,
     'L0_ffn_uf': 6.989,
     'L0_ffn_ui': 4.871,
     'L1_attn_Wq': 6.633,
     'L1_attn_Wk': 6.528,
     'L1_attn_lq1': 8.0,
     'L1_attn_lq2': 8.0,
     'L1_attn_lk1': 8.0,
     'L1_attn_lk2': 8.0,
     'L1_ffn_w_red': 8.0,
     'L1_ffn_wg': 8.0,
     'L1_ffn_W1': 8.0,
     'L1_ffn_b1': 8.0,
     'L1_ffn_W2': 8.0,
     'L1_ffn_b2': 26.035}
    for name, (base, spread) in spreads.items():
        noise = np.random.default_rng([zlib.crc32(name.encode()), seed]).standard_normal(out[name].shape)
        drawn = base * np.exp(spread * noise) if base else spread * noise
        out[name] = jnp.asarray(drawn.astype(out[name].dtype))
    for name, factor in factors.items():
        out[name] = (out[name] * factor).astype(out[name].dtype)
    return out
```

```python
from contextlib import ExitStack

import numpy as np

import concourse.bass as bass
from concourse import mybir

F32 = mybir.dt.float32
U32 = mybir.dt.uint32
I32 = mybir.dt.int32
ALU = mybir.AluOpType
ACT = mybir.ActivationFunctionType
AX = mybir.AxisListType

P = 128
B, S, DM = 4, 1024, 256
TILES = B * S // P
TB = S // P
HALVES = 2
TJ = TB // HALVES
TH = B * TJ
KD = DM // P
EPS = 1e-5
LAMBDA_INIT = 0.8 - 0.6 * float(np.exp(-0.3 * 1.0))
FMAX = float(np.finfo(np.float32).max)

COL = {}
_n = 0
for _name, _blocks in (("bz_f", 2), ("bh_f", 2), ("bz_b", 2), ("bh_b", 2), ("bf", 2), ("bi", 2), ("bc", 2),
                       ("in_c", 2), ("ln1_g", 2), ("ln1_b", 2), ("ln2_g", 2), ("ln2_b", 2), ("b1", 8)):
    COL[_name] = _n
    _n += _blocks
NCOL = _n
ROW = {n: i for i, n in enumerate(("b_out", "bo_ffn", "bo_attn", "b2_attn"))}
NROW = len(ROW)


class Steps:

    def __init__(self, eng, sem, base=0):
        self.eng, self.sem, self.base, self.n = eng, sem, base, 0

    def did(self, ins):
        ins.then_inc(self.sem, 1)
        self.n += 1
        return self.base + self.n

    def then(self, ins):
        self.eng.wait_ge(self.sem, self.did(ins))


class Core:

    def __init__(self, nc, ctx, d):
        self.nc, self.ctx, self.d = nc, ctx, d
        self.phase = ""
        self.clamped, self.summed = self.sem("attn_clamped"), self.sem("attn_summed")
        self.updated = self.sem("updated")
        self.passed = self.sem("passed")

    def hold(self, eng, sem, value):
        eng.wait_ge(sem, value)
        eng.sem_inc(self.passed, 1)

    def sem(self, name):
        return self.ctx.enter_context(self.nc.semaphore(name))

    def sb(self, name, shape, dt=F32, ctx=None):
        return (ctx or self.ctx).enter_context(self.nc.sbuf_tensor(self.phase + name, shape, dt))

    def ps(self, name, shape, dt=F32, ctx=None):
        return (ctx or self.ctx).enter_context(self.nc.psum_tensor(self.phase + name, shape, dt))


def setup(c):
    nc, d = c.nc, c.d
    c.X = c.sb("X", [P, TILES, DM])
    c.cols = c.sb("cols", [P, NCOL])
    c.nbz = c.sb("nbz", [P, 2, KD])
    c.ident = c.sb("ident", [P, P])
    c.ones = c.sb("ones", [1, P])
    c.mhalf = c.sb("mhalf", [P, P])
    c.modT = [c.sb(f"modT{l}", [P, 6 * KD, B]) for l in range(2)]
    c.rows1 = c.sb("rows1", [P, B, 6, DM])
    c.rows0 = c.sb("rows0", [P, B, 2, DM], ctx=c.layer0)
    c.x_loaded = c.sem("x_loaded")

    with ExitStack() as own:
        wmod = [c.sb(f"wmod{l}", [P, KD, 6 * DM], ctx=own) for l in range(2)]
        cT = c.sb("cT", [P, 2, KD, B], ctx=own)
        sT = c.sb("sT", [P, 2, KD, B], ctx=own)
        sB = c.sb("sB", [P, 2, KD, B, P], ctx=own)
        mag = c.sb("mag", [P, B, 2, DM], ctx=own)
        sgn = c.sb("sgn", [P, B, 2, DM], ctx=own)
        colp = c.ps("colp", [P, 2, 6 * KD, B], ctx=own)
        rowp = c.ps("rowp", [P, 4, 512], ctx=own)
        mod_loaded, silu_ready = c.sem("mod_loaded"), c.sem("silu_ready")
        spread_ready, colp_ready = c.sem("spread_ready"), c.sem("colp_ready")
        rowp_ready, rowp_free = c.sem("rowp_ready"), c.sem("rowp_free")
        dve_order, ident_clear = c.sem("dve_order0"), c.sem("ident_clear")

        with nc.Block() as block:

            @block.sync
            def _(sp):
                sp.dma_start(cT[:], d["cT"].rearrange("l (k p) b -> p l k b", p=P)).then_inc(mod_loaded, 16)
                for l in range(2):
                    sp.dma_start(wmod[l][:], d["wmod"][l].rearrange("(k p) n -> p k n", p=P)).then_inc(mod_loaded, 16)
                sp.dma_start(c.cols[:], d["cols"]).then_inc(mod_loaded, 16)
                for b in range(B):
                    for h in range(HALVES):
                        at = h * TH + b * TJ
                        sp.dma_start(c.X[:, at:at + TJ, :], d["x"][b, h * TJ * P:(h + 1) * TJ * P, :].rearrange(
                            "(t p) n -> p t n", p=P)).then_inc(c.x_loaded, 16)

            @block.gpsimd
            def _(pool):
                pool.memset(c.ones[:], 1.0)
                pool.memset(c.mhalf[:], -0.5)
                pool.memset(c.ident[:], 0.0).then_inc(ident_clear, 1)
                pool.wait_ge(ident_clear, 1)
                pool.affine_select(out=c.ident[:], in_=c.ident[:], compare_op=ALU.not_equal, fill=1.0,
                                   base=0, pattern=[[-1, P]], channel_multiplier=1)

            @block.scalar
            def _(act):
                act.wait_ge(mod_loaded, 64)
                act.activation(sT[:], cT[:], ACT.Silu).then_inc(silu_ready, 1)

            @block.tensor
            def _(pe):
                pe.wait_ge(mod_loaded, 64)
                pe.wait_ge(silu_ready, 1)
                for l in range(2):
                    for j in range(6 * KD):
                        for k in range(KD):
                            last = pe.matmul(colp[:, l, j, :], wmod[l][:, k, j * P:(j + 1) * P], sT[:, l, k, :],
                                             start=(k == 0), stop=(k == KD - 1))
                last.then_inc(colp_ready, 1)
                pe.wait_ge(spread_ready, 1)
                for n in range(4 * B):
                    l, b, j = (0, n, 0) if n < B else (1, (n - B) // 3, (n - B) % 3)
                    if n >= 4:
                        pe.wait_ge(rowp_free, n - 3)
                    for q in range(2):
                        src = (2, 5)[q] if l == 0 else 2 * j + q
                        for k in range(KD):
                            last = pe.matmul(rowp[:, n % 4, q * DM:(q + 1) * DM], sB[:, l, k, b, :],
                                             wmod[l][:, k, src * DM:(src + 1) * DM], start=(k == 0), stop=(k == KD - 1))
                    last.then_inc(rowp_ready, 1)

            def clamp_gate(dve, order, gate):
                order.then(dve.tensor_scalar(mag[:], gate, -1.0, None, ALU.mult))
                for b in range(B):
                    order.did(dve.scalar_tensor_tensor(mag[:, b], gate[:, b], 0.25, mag[:, b], ALU.max, ALU.max))
                order.then(dve.tensor_scalar(sgn[:], gate, 0.0, 2.0, ALU.is_ge, ALU.mult))
                for b in range(B):
                    order.then(dve.scalar_tensor_tensor(gate[:, b], sgn[:, b], 1.0, mag[:, b],
                                                        ALU.subtract, ALU.mult))

            @block.vector
            def _(dve):
                order = Steps(dve, dve_order)
                dve.wait_ge(mod_loaded, 64)
                for q, name in enumerate(("bz_f", "bz_b")):
                    dve.tensor_scalar(c.nbz[:, q, :], c.cols[:, COL[name]:COL[name] + KD], -1.0, None, ALU.mult)
                dve.wait_ge(silu_ready, 1)
                dve.tensor_copy(sB[:].rearrange("p l k b m -> p (l k b) m"),
                                sT[:].rearrange("p l k b -> p (l k b)").unsqueeze(2).broadcast_to([P, 2 * KD * B, P])
                                ).then_inc(spread_ready, 1)
                dve.wait_ge(colp_ready, 1)
                for l in range(2):
                    order.then(dve.tensor_copy(c.modT[l][:], colp[:, l]))
                    for j in (1, 4):
                        part = c.modT[l][:, j * KD:(j + 1) * KD, :]
                        dve.tensor_scalar(part, part, 1.0, None, ALU.add)
                for n in range(4 * B):
                    dve.wait_ge(rowp_ready, n + 1)
                    b, j = (n, 0) if n < B else ((n - B) // 3, (n - B) % 3)
                    dst = c.rows0[:, b] if n < B else c.rows1[:, b, 2 * j:2 * j + 2]
                    dve.tensor_copy(dst, rowp[:, n % 4, :].rearrange("p (q n) -> p q n", q=2)).then_inc(rowp_free, 1)
                dve.wait_ge(rowp_free, 4 * B)
                for j in (1, 4):
                    part = c.rows1[:, :, j, :]
                    dve.tensor_scalar(part, part, 1.0, None, ALU.add)
                clamp_gate(dve, order, c.rows0[:])
                dve.wait_ge(dve_order, order.n)
                clamp_gate(dve, order, c.rows1[:, :, 2::3, :])


def gru(c):
    nc, d = c.nc, c.d
    c.phase = "gru_"
    with ExitStack() as own:
        wg = c.sb("wg", [P, 4, KD, DM], ctx=own)
        wo = c.sb("wo", [P, 5, DM], ctx=own)
        wo_b = c.sb("wo_b", [P, 5, DM], ctx=own)
        stats = c.sb("stats", [P, TB, 6], ctx=own)
        mv = c.sb("mv", [P, TB, 2], ctx=own)
        ve = c.sb("ve", [P, TB], ctx=own)
        rs = c.sb("rs", [P, TB], ctx=own)
        xhat = c.sb("xhat", [P, TB, DM], ctx=own)
        hT = c.sb("hT", [P, KD, S], ctx=own)
        Z = c.sb("Z", [P, 2, S], ctx=own)
        A = c.sb("A", [P, 2, S], ctx=own)
        SG = c.sb("SG", [P, 2, S], ctx=own)
        R = c.sb("R", [P, 2, S], ctx=own)
        H = c.sb("H", [P, 4, S], ctx=own)
        tp = c.ps("tp", [P, 2, 512], ctx=own)
        gp = c.ps("gp", [P, 4, 512], ctx=own)
        op = c.ps("op", [P, 2, 2, DM], ctx=own)
        w_loaded = c.sem("gru_w_loaded")
        stats_ready, rstd_ready = c.sem("gru_stats_ready"), c.sem("gru_rstd_ready")
        xhat_ready = c.sem("gru_xhat_ready")
        tp_ready, hT_ready = c.sem("gru_tp_ready"), c.sem("gru_hT_ready")
        gp_ready, gates_ready = c.sem("gru_gp_ready"), c.sem("gru_gates_ready")
        scan_ready, wo_ready = c.sem("gru_scan_ready"), c.sem("gru_wo_ready")
        op_ready, op_free = c.sem("gru_op_ready"), c.sem("gru_op_free")
        dve_order, pool_order = c.sem("gru_dve_order"), c.sem("gru_pool_order")

        with nc.Block() as block:

            @block.sync
            def _(sp):
                sp.dma_start(wg[:], d["wg"].rearrange("w (k p) n -> p w k n", p=P)).then_inc(w_loaded, 16)
                sp.dma_start(wo[:, 0:4, :], d["wo0"].rearrange("(k p) n -> p k n", p=P)).then_inc(w_loaded, 16)
                r = d["rows"][ROW["b_out"]:ROW["b_out"] + 1, :]
                sp.dma_start(wo[:, 4, :], r.broadcast_to([P, DM])).then_inc(w_loaded, 16)

            @block.gpsimd
            def _(pool):
                pool.wait_ge(w_loaded, 48)
                with pool.Fori(0, B) as b:
                    order = Steps(pool, pool_order, b * 1)
                    c.hold(pool, stats_ready, b + 1)
                    order.then(pool.tensor_scalar(ve[:], mv[:, :, 1], EPS, None, ALU.add))
                    pool.tensor_tensor(rs[:], ve[:], c.mhalf[:, 0:TB], ALU.pow).then_inc(rstd_ready, 1)
                    pool.wait_ge(op_free, b * 4 + 2)
                    pool.tensor_tensor(wo_b[:], wo[:], c.rows0[:, bass.ds(b, 1), 0, :].broadcast_to([P, 5, DM]),
                                       ALU.mult).then_inc(wo_ready, 1)

            @block.scalar
            def _(act):
                act.sem_inc(gates_ready, 4)
                with act.Fori(0, B) as b:
                    for n in range(4):
                        k, q = n // 2, n % 2
                        c.hold(act, tp_ready, b * 4 + n + 2)
                        act.activation(hT[:, k, q * 512:(q + 1) * 512], tp[:, n % 2, :], ACT.Identity,
                                       bias=c.modT[0][:, 0 * KD + k, bass.ds(b, 1)],
                                       scale=c.modT[0][:, 1 * KD + k, bass.ds(b, 1)]).then_inc(hT_ready, 1)
                    for u in range(4):
                        dr, m, s = u // 2, u % 2, u % 2
                        bz, bh = COL[("bz_f", "bz_b")[dr]] + m, COL[("bh_f", "bh_b")[dr]] + m
                        act.wait_ge(scan_ready, b * 4 + u + 1)
                        for n in range(2):
                            cs = slice(n * 512, (n + 1) * 512)
                            act.wait_ge(gp_ready, b * 16 + u * 4 + n * 2 + 1)
                            act.activation(Z[:, s, cs], gp[:, 2 * n, :], ACT.Sigmoid, bias=c.cols[:, bz:bz + 1])
                            act.activation(A[:, s, cs], gp[:, 2 * n, :], ACT.Sigmoid, bias=c.nbz[:, dr, m:m + 1],
                                           scale=-1.0).then_inc(gates_ready, 1)
                            act.wait_ge(gp_ready, b * 16 + u * 4 + n * 2 + 2)
                            act.activation(SG[:, s, cs], gp[:, 2 * n + 1, :], ACT.Sigmoid, bias=c.cols[:, bh:bh + 1])
                            act.activation(R[:, s, cs], gp[:, 2 * n + 1, :], ACT.Relu, bias=c.cols[:, bh:bh + 1]
                                           ).then_inc(gates_ready, 1)

            @block.tensor
            def _(pe):
                pe.sem_inc(tp_ready, 1)
                pe.wait_ge(w_loaded, 48)
                with pe.Fori(0, B) as b:
                    for n in range(4):
                        k, q = n // 2, n % 2
                        if n < 2:
                            pe.wait_ge(xhat_ready, b * 8 + 4 * q + 4)
                        else:
                            pe.wait_ge(hT_ready, b * 4 + n - 1)
                        for t in range(4):
                            last = pe.transpose(tp[:, n % 2, t * P:(t + 1) * P],
                                                xhat[:, 4 * q + t, k * P:(k + 1) * P], c.ident[:])
                        last.then_inc(tp_ready, 1)
                    pe.wait_ge(hT_ready, b * 4 + 4)
                    for u in range(4):
                        dr, m = u // 2, u % 2
                        for n in range(2):
                            for w in range(2):
                                pe.wait_ge(gates_ready, b * 16 + u * 4 + n * 2 + w + 1)
                                for k in range(KD):
                                    last = pe.matmul(gp[:, 2 * n + w, :], wg[:, 2 * dr + w, k, m * P:(m + 1) * P],
                                                     hT[:, k, n * 512:(n + 1) * 512], start=(k == 0), stop=(k == KD - 1))
                                last.then_inc(gp_ready, 1)
                    pe.wait_ge(scan_ready, b * 4 + 6)
                    pe.wait_ge(wo_ready, b + 1)
                    for n in range(4):
                        pe.wait_ge(op_free, b * 4 + n + 1)
                        for q in range(2):
                            t = 2 * n + q
                            for k in range(4):
                                pe.matmul(op[:, n % 2, q, :], H[:, k, t * P:(t + 1) * P], wo_b[:, k, :],
                                          start=(k == 0), stop=False)
                            last = pe.matmul(op[:, n % 2, q, :], c.ones[:], wo_b[0:1, 4, :], start=False, stop=True)
                        last.then_inc(op_ready, 1)

            @block.vector
            def _(dve):
                dve.sem_inc(scan_ready, 2)
                dve.sem_inc(op_free, 2)
                dve.wait_ge(c.x_loaded, 16 * B * HALVES)
                with dve.Fori(0, B) as b:
                    order = Steps(dve, dve_order, b * 16)
                    for t in range(TB):
                        order.did(dve.bn_stats(stats[:, t, :], c.X[:, b * TJ + (t // TJ * TH + t % TJ), :]))
                    for t in range(TB):
                        c.hold(dve, dve_order, order.base + t + 1)
                        last = dve.bn_aggr(mv[:, t, :], stats[:, t, :])
                    last.then_inc(stats_ready, 1)
                    dve.wait_ge(rstd_ready, b + 1)
                    dve.wait_ge(tp_ready, b * 4 + 1)
                    for t in range(TB):
                        dve.tensor_scalar(xhat[:, t, :], c.X[:, b * TJ + (t // TJ * TH + t % TJ), :], mv[:, t, 0:1],
                                          rs[:, t:t + 1], ALU.subtract, ALU.mult).then_inc(xhat_ready, 1)
                    for u in range(4):
                        s = u % 2
                        dve.wait_ge(gates_ready, 4 + b * 16 + u * 4 + 4)
                        order.then(dve.scalar_tensor_tensor(SG[:, s, :], SG[:, s, :], 0.5, R[:, s, :], ALU.min, ALU.add))
                        order.then(dve.tensor_tensor(SG[:, s, :], SG[:, s, :], Z[:, s, :], ALU.mult))
                        a, v = A[:, s, :], SG[:, s, :]
                        if u >= 2:
                            a, v = a[:, ::-1], v[:, ::-1]
                        dve.tensor_tensor_scan(H[:, u, :], a, v, 0.0, ALU.mult, ALU.add).then_inc(scan_ready, 1)
                    for n in range(4):
                        dve.wait_ge(op_ready, b * 4 + n + 1)
                        xs = c.X[:, bass.ds(b * TJ + (2 * n // TJ * TH + 2 * n % TJ), 2), :]
                        dve.tensor_tensor(xs, op[:, n % 2], xs, ALU.add).then_inc(op_free, 1)


def ffn(c):
    nc, d = c.nc, c.d
    c.phase = "ffn_"
    CH = TJ * P // 2
    with ExitStack() as own:
        w = c.sb("w_ffn", [P, 8, KD, DM], ctx=own)
        bo = c.sb("bo_row", [1, DM], ctx=own)
        stats = c.sb("stats", [P, TJ, 6], ctx=own)
        mv = c.sb("mv", [P, TJ, 2], ctx=own)
        ve = c.sb("ve", [P, TJ], ctx=own)
        rs = c.sb("rs", [P, TJ], ctx=own)
        xhat = c.sb("xhat", [P, TJ, DM], ctx=own)
        hT = c.sb("hT", [P, B, KD, TJ * P], ctx=own)
        cT = c.sb("cT_state", [P, KD, TJ * P], ctx=own)
        G = c.sb("G", [P, 2, 3, KD, CH], ctx=own)
        Y = c.sb("Y", [P, 2, 2, DM], ctx=own)
        zero = c.sb("zero", [P, DM], ctx=own)
        zero_ready, cleared = c.sem("zero_ready"), c.sem("cleared")
        tp = c.ps("tp", [P, KD, 512], ctx=own)
        gp = c.ps("gp", [P, 6, 512], ctx=own)
        w_loaded, stats_ready = c.sem("ffn_w_loaded"), c.sem("ffn_stats_ready")
        rstd_ready, xhat_ready = c.sem("ffn_rstd_ready"), c.sem("ffn_xhat_ready")
        tp_ready, hT_ready = c.sem("ffn_tp_ready"), c.sem("ffn_hT_ready")
        gp_ready, gates_ready, c_ready = c.sem("ffn_gp_ready"), c.sem("ffn_gates_ready"), c.sem("ffn_c_ready")
        y_ready, tanh_ready = c.sem("ffn_y_ready"), c.sem("ffn_tanh_ready")
        scaled_ready, y_free = c.sem("ffn_scaled_ready"), c.sem("ffn_y_free")
        dve_order, pool_order = c.sem("ffn_dve_order"), c.sem("ffn_pool_order")

        with nc.Block() as block:

            @block.sync
            def _(sp):
                sp.dma_start(w[:], d["w_ffn"].rearrange("w (k p) n -> p w k n", p=P)).then_inc(w_loaded, 16)
                sp.dma_start(bo[:], d["rows"][ROW["bo_ffn"]:ROW["bo_ffn"] + 1, :]).then_inc(w_loaded, 16)
                sp.wait_ge(zero_ready, 1)
                sp.dma_start(c.sorted_h.rearrange("(n p) m -> p n m", p=P),
                             zero[:].unsqueeze(1).broadcast_to([P, NT, DM])).then_inc(cleared, 16)
                sp.wait_ge(cleared, 16)

            @block.gpsimd
            def _(pool):
                pool.memset(zero[:], 0.0).then_inc(zero_ready, 1)

                def rstd(it):
                    c.hold(pool, stats_ready, it + 1)
                    pool.tensor_scalar(ve[:], mv[:, :, 1], EPS, None, ALU.add).then_inc(pool_order, 1)
                    pool.wait_ge(pool_order, it + 1)
                    pool.tensor_tensor(rs[:], ve[:], c.mhalf[:, 0:TJ], ALU.pow).then_inc(rstd_ready, 1)

                with pool.Fori(0, HALVES) as h:
                    rstd(h * B)
                    with pool.Fori(0, B - 1) as b:
                        rstd(h * B + b + 1)
                    for n in range(8):
                        pool.wait_ge(tanh_ready, h * 8 + n + 1)
                        pool.tensor_tensor(Y[:, n % 2], Y[:, n % 2],
                                           c.rows0[:, n // 2, 1:2, :].broadcast_to([P, 2, DM]),
                                           ALU.mult).then_inc(scaled_ready, 1)

            @block.scalar
            def _(act):

                def evacuate(it, b):
                    for k in range(KD):
                        c.hold(act, tp_ready, it * 2 + k + 2)
                        act.activation(hT[:, b, k, :], tp[:, k, :], ACT.Identity,
                                       bias=c.modT[0][:, 3 * KD + k, bass.ds(b, 1)],
                                       scale=c.modT[0][:, 4 * KD + k, bass.ds(b, 1)]).then_inc(hT_ready, 1)

                def gates(it, ch):
                    for g, (name, f) in enumerate((("bf", ACT.Sigmoid), ("bi", ACT.Sigmoid), ("bc", ACT.Tanh))):
                        act.wait_ge(gp_ready, it * 6 + ch * 3 + g + 1)
                        for m in range(KD):
                            col = COL[name] + m
                            last = act.activation(G[:, ch, g, m, :], gp[:, ch * 3 + g, m * CH:(m + 1) * CH], f,
                                                  bias=c.cols[:, col:col + 1])
                    last.then_inc(gates_ready, 1)

                with act.Fori(0, HALVES) as h:
                    evacuate(h * B, 0)
                    with act.Fori(0, B - 1) as b:
                        gates(h * B + b, 0)
                        evacuate(h * B + b + 1, b + 1)
                        gates(h * B + b, 1)
                    gates(h * B + B - 1, 0)
                    gates(h * B + B - 1, 1)
                    for n in range(8):
                        act.wait_ge(y_ready, h * 8 + n + 1)
                        act.wait_ge(y_free, h * 8 + n + 1)
                        act.activation(Y[:, n % 2], gp[:, n % 6, :].rearrange("p (q n) -> p q n", q=2),
                                       ACT.Tanh).then_inc(tanh_ready, 1)

            @block.tensor
            def _(pe):

                def transposes(it):
                    pe.wait_ge(xhat_ready, it + 1)
                    for k in range(KD):
                        for t in range(TJ):
                            last = pe.transpose(tp[:, k, t * P:(t + 1) * P], xhat[:, t, k * P:(k + 1) * P], c.ident[:])
                        last.then_inc(tp_ready, 1)

                def gates(h, b, ch):
                    pe.wait_ge(hT_ready, h * 2 * B + b * 2 + 2)
                    pe.wait_ge(c_ready, h * 10 + b * 2 + ch + 1)
                    for g in range(3):
                        for m in range(KD):
                            out = gp[:, ch * 3 + g, m * CH:(m + 1) * CH]
                            for k in range(KD):
                                pe.matmul(out, w[:, 2 * g, k, m * P:(m + 1) * P], hT[:, b, k, ch * CH:(ch + 1) * CH],
                                          start=(k == 0), stop=False)
                            for k in range(KD):
                                last = pe.matmul(out, w[:, 2 * g + 1, k, m * P:(m + 1) * P],
                                                 cT[:, k, ch * CH:(ch + 1) * CH], start=False, stop=(k == KD - 1))
                        last.then_inc(gp_ready, 1)

                pe.sem_inc(tp_ready, 1)
                pe.wait_ge(w_loaded, 32)
                with pe.Fori(0, HALVES) as h:
                    transposes(h * B)
                    with pe.Fori(0, B - 1) as b:
                        gates(h, b, 0)
                        transposes(h * B + b + 1)
                        gates(h, b, 1)
                    gates(h, B - 1, 0)
                    gates(h, B - 1, 1)
                    pe.wait_ge(c_ready, h * 10 + 10)
                    for n in range(8):
                        if n >= 6:
                            pe.wait_ge(tanh_ready, h * 8 + n - 5)
                        for q in range(2):
                            out = gp[:, n % 6, q * DM:(q + 1) * DM]
                            b, t = n // 2, 2 * (n % 2) + q
                            for k in range(KD):
                                pe.matmul(out, hT[:, b, k, t * P:(t + 1) * P], w[:, 6, k, :],
                                          start=(k == 0), stop=False)
                            for k in range(KD):
                                pe.matmul(out, cT[:, k, t * P:(t + 1) * P], w[:, 7, k, :], start=False, stop=False)
                            last = pe.matmul(out, c.ones[:], bo[:], start=False, stop=True)
                        last.then_inc(y_ready, 1)

            @block.vector
            def _(dve):

                def layernorm(it):
                    for t in range(TJ):
                        dve.bn_stats(stats[:, t, :], c.X[:, it * TJ + t, :]).then_inc(dve_order, 1)
                    c.hold(dve, dve_order, it * TJ + TJ)
                    for t in range(TJ):
                        last = dve.bn_aggr(mv[:, t, :], stats[:, t, :])
                    last.then_inc(stats_ready, 1)
                    dve.wait_ge(rstd_ready, it + 1)
                    dve.wait_ge(tp_ready, it * 2 + 1)
                    for t in range(TJ):
                        last = dve.tensor_scalar(xhat[:, t, :], c.X[:, it * TJ + t, :], mv[:, t, 0:1],
                                                 rs[:, t:t + 1], ALU.subtract, ALU.mult)
                    last.then_inc(xhat_ready, 1)

                def update(h, b, ch):
                    state = cT[:, :, ch * CH:(ch + 1) * CH]
                    dve.wait_ge(gates_ready, h * 2 * B + b * 2 + ch + 1)
                    dve.tensor_tensor(G[:, ch, 2], G[:, ch, 1], G[:, ch, 2], ALU.mult)
                    dve.tensor_tensor(state, G[:, ch, 0], state, ALU.mult).then_inc(c.updated, 1)
                    dve.wait_ge(c.updated, h * 2 * B + b * 2 + ch + 1)
                    dve.tensor_tensor(state, state, G[:, ch, 2], ALU.add).then_inc(c_ready, 1)

                dve.sem_inc(y_free, 2)
                with dve.Fori(0, HALVES) as h:
                    for ch in range(2):
                        dve.tensor_copy(cT[:, :, ch * CH:(ch + 1) * CH],
                                        c.cols[:, COL["in_c"]:COL["in_c"] + KD].unsqueeze(2).broadcast_to([P, KD, CH])
                                        ).then_inc(c_ready, 1)
                    layernorm(h * B)
                    with dve.Fori(0, B - 1) as b:
                        layernorm(h * B + b + 1)
                        update(h, b, 0)
                        update(h, b, 1)
                    update(h, B - 1, 0)
                    update(h, B - 1, 1)
                    for n in range(8):
                        xs = c.X[:, bass.ds(h * TH + 2 * n, 2), :]
                        dve.wait_ge(scaled_ready, h * 8 + n + 1)
                        dve.tensor_tensor(xs, xs, Y[:, n % 2], ALU.add).then_inc(y_free, 1)


H_, D_, DV = 16, 8, 16
NH = 2 * H_
GB = 16
G8 = P // GB


def attention_setup(c):
    nc, d = c.nc, c.d
    c.phase = "as_"
    own = c.layer1
    c.w_qk = c.sb("w_qk", [P, KD, 2 * DM], ctx=own)
    c.w_v = c.sb("w_v", [P, KD, DM], ctx=own)
    c.w_o = c.sb("w_o", [P, KD, DM], ctx=own)
    c.bo1 = c.sb("bo1", [1, DM], ctx=own)
    c.maskK = c.sb("maskK", [P, 4], ctx=own)
    c.maskV = c.sb("maskV", [P, G8], ctx=own)
    c.combine = c.sb("combine", [P, 2, 64], ctx=own)
    lam_in = c.sb("lam_in", [P, 2, 2, D_], ctx=own)
    lam = c.sb("lam", [P, 4], ctx=own)
    loaded, dve_order, exp_ready = c.sem("as_loaded"), c.sem("as_dve_order"), c.sem("as_exp_ready")
    c.credit = {n: c.sem("attn_" + n) for n in ("norm1_ready", "cp_ready")}

    with nc.Block() as block:

        @block.sync
        def _(sp):
            sp.dma_start(c.w_qk[:], d["w_qk"].rearrange("(k p) n -> p k n", p=P)).then_inc(loaded, 16)
            sp.dma_start(c.w_v[:], d["w_v"].rearrange("(k p) n -> p k n", p=P)).then_inc(loaded, 16)
            sp.dma_start(c.w_o[:], d["w_o"].rearrange("(k p) n -> p k n", p=P)).then_inc(loaded, 16)
            sp.dma_start(c.bo1[:], d["rows"][ROW["bo_attn"]:ROW["bo_attn"] + 1, :]).then_inc(loaded, 16)
            sp.dma_start(c.maskK[:], d["maskK"]).then_inc(loaded, 16)
            sp.dma_start(c.maskV[:], d["maskV"]).then_inc(loaded, 16)
            sp.dma_start(c.combine[:], d["combine"]).then_inc(loaded, 16)
            sp.dma_start(lam_in[:].rearrange("p a b n -> p (a b n)"),
                         d["lam"].rearrange("a n -> (a n)").unsqueeze(0).broadcast_to([P, 4 * D_])).then_inc(loaded, 16)
            sp.wait_ge(loaded, 16 * 8)

        @block.scalar
        def _(act):
            act.wait_ge(dve_order, 2)
            act.activation(lam[:, 2:4], lam[:, 0:2], ACT.Exp).then_inc(exp_ready, 1)

        @block.vector
        def _(dve):
            order = Steps(dve, dve_order)
            dve.sem_inc(c.credit["norm1_ready"], 2)
            dve.sem_inc(c.credit["cp_ready"], 2)
            dve.wait_ge(loaded, 16 * 8)
            order.then(dve.tensor_tensor(lam_in[:, 0], lam_in[:, 0], lam_in[:, 1], ALU.mult))
            order.then(dve.tensor_reduce(lam[:, 0:2], lam_in[:, 0], AX.X, ALU.add))
            dve.wait_ge(exp_ready, 1)
            order.then(dve.scalar_tensor_tensor(lam[:, 0:1], lam[:, 3:4], LAMBDA_INIT, lam[:, 2:3],
                                                ALU.subtract, ALU.subtract))
            dve.tensor_scalar(c.combine[:, 1, :], c.combine[:, 1, :], lam[:, 0:1], None, ALU.mult)


def attention(c, h, own):
    nc = c.nc
    c.phase = "at_"
    AREA = TH * DM
    area0 = c.sb("area0", [P, AREA], ctx=own)
    area1 = c.sb("area1", [P, 2 * AREA], ctx=own)
    area2 = c.sb("area2", [P, 2 * AREA], ctx=own)
    tok = area0[:].rearrange("p (k t r g) -> p k t r g", k=KD, t=TJ, r=B)
    OT = area0[:].rearrange("p (a r g j) -> p a r g j", a=H_, r=4, g=GB)
    QK = area1[:].rearrange("p (n t d) -> p n t d", n=2 * NH, t=TH)
    VS = area1[:, 0:AREA].rearrange("p (u G n) -> p u G n", u=2, G=G8)
    VT = area1[:, AREA:].rearrange("p (g t d) -> p g t d", g=GB, t=TH)
    PN = area1[:, 0:AREA // 2].rearrange("p (s k n a) -> p s k n a", s=2, k=2, a=H_)
    OK = area1[:, 0:AREA].rearrange("p (u G a d) -> p u G a d", u=2, G=G8, a=H_)
    QT = area2[:, 0:AREA].rearrange("p (g n) -> p g n", n=NH)
    KT = area2[:, AREA:].rearrange("p (g n) -> p g n", n=NH)
    oT = area2[:, 0:AREA].rearrange("p (k t r n g) -> p k t r n g", k=KD, t=4, r=4, g=2)
    SQ = area2[:, AREA:].rearrange("p (u n) -> p u n", u=2)

    stats = c.sb("stats", [P, 2, TJ, 6], ctx=own)
    mv = c.sb("mv", [P, 2, TJ, 2], ctx=own)
    ve = c.sb("ve", [P, 2, TJ], ctx=own)
    rs = c.sb("rs", [P, 2, TJ], ctx=own)
    xhat = area2[:, 0:TJ * DM].rearrange("p (t n) -> p t n", t=TJ)
    Kbd = c.sb("Kbd", [P, 2, G8, P], ctx=own)
    Qs = c.sb("Qs", [P, 2, G8, NH], ctx=own)
    Vbd = c.sb("Vbd", [P, 2, TH, P], ctx=own)
    T = c.sb("T", [P, 2, 4 * G8, NH], ctx=own)
    mx = c.sb("mx", [P, 2, 4 * G8], ctx=own)
    Z = c.sb("Z", [P, 2, 2, 4 * G8], ctx=own)
    attT = c.sb("attT", [P, 2, 4, 64], ctx=own)
    ss = c.sb("ss", [P, 2, P], ctx=own)
    rr = c.sb("rr", [P, 2, P], ctx=own)
    work = c.ps("work", [P, 6, 512], ctx=own)
    tp = c.ps("tp", [P, KD, 512], ctx=own)
    SC = work[:, 0:4, 0:G8 * NH]
    CP = [work[:, 4, 0:4 * 64], tp[:, 0, 0:4 * 64]]
    PV = [bank[:, 0:TH * H_].rearrange("p (r j a) -> p r j a", r=4, j=4) for bank in (work[:, 5], tp[:, 1])]

    QK0, HD0, V0, VT0, O0, F0, P0, JOBS = 0, 16, 32, 40, 48, 56, 64, 72
    by_act = [n < HD0 or (n % 2 == 0 and n < P0) for n in range(JOBS)]
    ACTS, DVES = sum(by_act), JOBS - sum(by_act)

    def emptied(n):
        return sum(1 for m in range(n + 1) if by_act[m] == by_act[n])

    sem = lambda n: c.sem("attn_" + n)
    stats_ready, rstd_ready = sem("stats_ready"), sem("rstd_ready")
    xn_ready, h1_ready, xhat_ready = sem("xn_ready"), sem("h1_ready"), sem("xhat_ready")
    tp_ready, hT_ready = sem("tp_ready"), sem("hT_ready")
    full, empty_a, empty_d = sem("bank_full"), sem("bank_empty_act"), sem("bank_empty_dve")
    kbd_ready, q_ready, vbd_ready = sem("kbd_ready"), sem("q_ready"), sem("vbd_ready")
    s_ready, s_free, t_ready, e_ready, rz_ready = sem("s_ready"), sem("s_free"), sem("t_ready"), sem("e_ready"), sem("rz_ready")
    norm0_ready, norm1_ready, cp_ready = sem("norm0_ready"), c.credit["norm1_ready"], c.credit["cp_ready"]
    att_ready, pv_ready, o_ready = sem("att_ready"), sem("pv_ready"), sem("o_ready")
    sq_ready, ss_ready, rr_ready, ok_ready = sem("sq_ready"), sem("ss_ready"), sem("rr_ready"), sem("ok_ready")
    dve_order, pool_order = sem("dve_order"), sem("pool_order")

    def emptied_wait(eng, n, hh):
        if by_act[n]:
            eng.wait_ge(empty_a, hh * ACTS + emptied(n))
        else:
            eng.wait_ge(empty_d, hh * DVES + emptied(n))

    def rounds(eng, do_round):
        with eng.Fori(0, GB // 2 - 1) as i2:
            for s in range(2):
                do_round(i2 * 2 + s, s, True)
        for s in range(2):
            do_round(GB - 2 + s, s, False)

    LN = [(0, 0), (0, 1), (1, 0), (0, 2), (1, 1), (0, 3), (1, 2), (1, 3)]

    with nc.Block() as block:

        def empty(n, copy):
            bank = work[:, n % 6, :]
            if n < V0:
                q, j = ((QT, n - HD0) if n < HD0 + 8 else (KT, n - HD0 - 8))
                return copy(q[:, :, 4 * j:4 * j + 4].rearrange("p g n -> p n g"),
                            bank.rearrange("p (n g) -> p n g", n=4))
            if n < VT0:
                u, G = (n - V0) // 4, 2 * ((n - V0) % 4)
                return copy(VS[:, u, G:G + 2, :], bank.rearrange("p (G n) -> p G n", G=2))
            if n < O0:
                u, d0 = (n - VT0) // 4, 4 * ((n - VT0) % 4)
                v = bank.rearrange("p (d r g j) -> p d r g j", d=4, r=2, g=GB)
                for r in range(2):
                    at = 8 * u + 4 * r
                    last = copy(VT[:, :, at:at + 4, d0:d0 + 4].rearrange("p g j d -> p d g j"), v[:, :, r])
                return last
            if n < F0:
                u, a = (n - O0) // 4, 4 * ((n - O0) % 4)
                return copy(OK[:, u, :, a:a + 4, :].rearrange("p G a d -> p a G d"),
                            bank.rearrange("p (a G d) -> p a G d", a=4, G=G8))
            u, k, g2 = (n - F0) // 4, (n - F0) // 2 % 2, (n - F0) % 2
            return copy(oT[:, k, :, 2 * u:2 * u + 2, :, g2], bank.rearrange("p (t r n) -> p t r n", t=4, r=2))

        @block.gpsimd
        def _(pool):
            order = Steps(pool, pool_order, h * 16)

            def rstd(n):
                kind, b = LN[n]
                c.hold(pool, stats_ready, h * 8 + n + 1)
                order.then(pool.tensor_scalar(ve[:, kind], mv[:, kind, :, 1], EPS, None, ALU.add))
                pool.tensor_tensor(rs[:, kind], ve[:, kind], c.mhalf[:, 0:TJ], ALU.pow).then_inc(rstd_ready, 1)

            def affine(b):
                part = c.H1[:, b * TJ:(b + 1) * TJ, :]
                pool.wait_ge(xn_ready, h * B + b + 1)
                order.then(pool.tensor_tensor(part, part, c.rows1[:, b, 1:2, :].broadcast_to([P, TJ, DM]), ALU.mult))
                pool.tensor_tensor(part, part, c.rows1[:, b, 0:1, :].broadcast_to([P, TJ, DM]),
                                   ALU.add).then_inc(h1_ready, 1)

            rstd(0)
            affine(0)
            rstd(1)
            affine(1)
            rstd(2)
            rstd(3)
            affine(2)
            rstd(4)
            rstd(5)
            affine(3)
            rstd(6)
            rstd(7)

            def spread_v(i, s):
                pool.tensor_tensor(Vbd[:, s].rearrange("p t (G d) -> p t G d", d=DV),
                                   VT[:, bass.ds(i, 1), :, :].rearrange("p g t d -> p (g t) d").unsqueeze(2).broadcast_to([P, TH, G8, DV]),
                                   c.maskV[:].unsqueeze(1).unsqueeze(3).broadcast_to([P, TH, G8, DV]),
                                   ALU.mult).then_inc(vbd_ready, 1)

            emptied_wait(pool, O0 - 2, h)
            emptied_wait(pool, O0 - 1, h)
            for i in range(2):
                spread_v(i, i)

            def do_round(i, s, more):
                pool.wait_ge(vbd_ready, h * GB + (i + 2 if more else GB))
                pool.wait_ge(rz_ready, h * GB + i + 1)
                pool.wait_ge(cp_ready, h * GB + i + 1)
                pool.tensor_tensor(PN[:, s, 1], T[:, s, :, H_:NH],
                                   Z[:, s, 1, :].unsqueeze(2).broadcast_to([P, 4 * G8, H_]),
                                   ALU.mult).then_inc(norm1_ready, 1)
                if more:
                    pool.wait_ge(pv_ready, h * GB + i + 1)
                    pool.wait_ge(norm1_ready, h * GB + i + 3)
                    spread_v(i + 2, s)

            rounds(pool, do_round)
            pool.wait_ge(norm1_ready, h * GB + GB + 2)
            for u in range(2):
                c.hold(pool, ss_ready, h * 2 + u + 1)
                order.then(pool.tensor_scalar(ss[:, u], ss[:, u], 1.0 / DV, EPS, ALU.mult, ALU.add))
                c.hold(pool, pool_order, order.did(pool.tensor_tensor(rr[:, u], ss[:, u], c.mhalf[:], ALU.pow)))
                pool.tensor_scalar(rr[:, u], rr[:, u], 1.0 - LAMBDA_INIT, 0.0, ALU.mult, ALU.add).then_inc(rr_ready, 1)

        @block.scalar
        def _(act):

            def to_hT(b):
                for k in range(KD):
                    act.wait_ge(tp_ready, h * 2 * B + 2 * b + k + 1)
                    g, o = COL["ln1_g"] + k, COL["ln1_b"] + k
                    act.activation(tok[:, k, :, b, :], tp[:, k, :].rearrange("p (t g) -> p t g", t=TJ), ACT.Identity,
                                   bias=c.cols[:, o:o + 1], scale=c.cols[:, g:g + 1]).then_inc(hT_ready, 1)

            def copy(out, in_):
                return act.copy(out, in_)

            for b in range(B):
                to_hT(b)
                for t in range(TJ):
                    n = QK0 + b * TJ + t
                    act.wait_ge(full, h * JOBS + n + 1)
                    copy(QK[:, :, n, :], work[:, n % 6, :].rearrange("p (n d) -> p n d", d=D_)).then_inc(empty_a, 1)
            for n in range(HD0, O0):
                if by_act[n]:
                    act.wait_ge(full, h * JOBS + n + 1)
                    empty(n, copy).then_inc(empty_a, 1)

            def take_q(i, s):
                c.hold(act, empty_d, h * DVES + emptied(V0 - 1))
                copy(Qs[:, s], QT[:, bass.ds(i * G8, G8), :]).then_inc(q_ready, 1)

            for i in range(2):
                take_q(i, i)

            def exponent(i, s):
                act.wait_ge(t_ready, h * GB + i + 1)
                act.activation(T[:, s], T[:, s], ACT.Exp).then_inc(e_ready, 1)

            def do_round(i, s, more):
                if more:
                    c.hold(act, s_ready, h * GB + i + 1)
                    take_q(i + 2, s)
                act.wait_ge(cp_ready, h * GB + i + 3)
                copy(attT[:, s].rearrange("p r n -> p (r n)"), CP[s]).then_inc(att_ready, 1)
                if more or s == 0:
                    exponent(i + 1, 1 - s)
                c.hold(act, pv_ready, h * GB + i + 1)
                copy(OT[:, :, :, bass.ds(i, 1), :].rearrange("p a r g j -> p (r g) j a"), PV[s]).then_inc(o_ready, 1)

            exponent(0, 0)
            rounds(act, do_round)
            for u in range(2):
                for n in range(O0 + 4 * u, O0 + 4 * u + 4):
                    if by_act[n]:
                        act.wait_ge(full, h * JOBS + n + 1)
                        empty(n, copy).then_inc(empty_a, 1)
                emptied_wait(act, O0 + 4 * u + 2, h)
                emptied_wait(act, O0 + 4 * u + 3, h)
                act.activation(SQ[:, u], OK[:, u].rearrange("p G a d -> p (G a d)"), ACT.Square).then_inc(sq_ready, 1)
            for n in range(F0, P0):
                if by_act[n]:
                    act.wait_ge(full, h * JOBS + n + 1)
                    empty(n, copy).then_inc(empty_a, 1)

        @block.tensor
        def _(pe):

            def bank_free(n):
                if n >= 6:
                    emptied_wait(pe, n - 6, h)

            for b in range(B):
                pe.wait_ge(xhat_ready, h * B + b + 1)
                if b:
                    pe.wait_ge(hT_ready, h * 2 * B + 2 * b)
                for k in range(KD):
                    for t in range(TJ):
                        last = pe.transpose(tp[:, k, t * P:(t + 1) * P], xhat[:, t, k * P:(k + 1) * P], c.ident[:])
                    last.then_inc(tp_ready, 1)
                pe.wait_ge(hT_ready, h * 2 * B + 2 * b + 2)
                for t in range(TJ):
                    n = QK0 + b * TJ + t
                    bank_free(n)
                    for k in range(KD):
                        last = pe.matmul(work[:, n % 6, :], tok[:, k, t, b, :], c.w_qk[:, k, :],
                                         start=(k == 0), stop=(k == KD - 1))
                    last.then_inc(full, 1)
            emptied_wait(pe, HD0 - 1, h)
            for n in range(HD0, V0):
                bank_free(n)
                for q in range(4):
                    hd = 4 * (n - HD0) + q
                    last = pe.transpose(work[:, n % 6, q * P:(q + 1) * P], QK[:, hd].rearrange("p t d -> p (t d)"), c.ident[:])
                last.then_inc(full, 1)
            eight = tok.rearrange("p k t (u r) (n g) -> p k t u (r n) g", u=2, g=2)
            for n in range(V0, VT0):
                u, G = (n - V0) // 4, 2 * ((n - V0) % 4)
                bank_free(n)
                for q in range(2):
                    for k in range(KD):
                        last = pe.matmul(work[:, n % 6, q * DM:(q + 1) * DM], eight[:, k, (G + q) % 4, u, :, (G + q) // 4],
                                         c.w_v[:, k, :], start=(k == 0), stop=(k == KD - 1))
                last.then_inc(full, 1)
            for n in range(VT0, O0):
                u, d0 = (n - VT0) // 4, 4 * ((n - VT0) % 4)
                if n in (VT0, VT0 + 4):
                    emptied_wait(pe, V0 + 4 * u + 2, h)
                    emptied_wait(pe, V0 + 4 * u + 3, h)
                bank_free(n)
                v = VS[:, u].rearrange("p G (n d) -> p (G n) d", d=DV)
                for q in range(4):
                    last = pe.transpose(work[:, n % 6, q * P:(q + 1) * P], v[:, :, d0 + q], c.ident[:])
                last.then_inc(full, 1)
            emptied_wait(pe, O0 - 2, h)
            emptied_wait(pe, O0 - 1, h)

            def scores(i, s):
                pe.wait_ge(kbd_ready, h * GB + i + 1)
                c.hold(pe, q_ready, h * GB + i + 1)
                for g in range(G8):
                    for q in range(4):
                        rows = slice(32 * q, 32 * q + 32)
                        j, g2 = g // 2, g % 2
                        last = pe.matmul(SC[NH * j:NH * (j + 1), q, g2 * P:(g2 + 1) * P], Qs[rows, s, g, :],
                                         Kbd[rows, s, g, :], start=True, stop=True)
                last.then_inc(s_ready, 1)

            def do_round(i, s, more):
                if more or s == 0:
                    pe.wait_ge(s_free, h * GB + i + 1)
                    scores(i + 1, 1 - s)
                pe.wait_ge(norm0_ready, h * GB + i + 1)
                pe.wait_ge(norm1_ready, h * GB + i + 3)
                for q in range(4):
                    for g2 in range(2):
                        for kind in range(2):
                            at = 4 * (2 * q + g2)
                            last = pe.matmul(CP[s][64 * g2:64 * g2 + 64, q * 64:(q + 1) * 64],
                                             PN[:, s, kind, at:at + 4, :].rearrange("p t n -> p (t n)"),
                                             c.combine[:, kind, :], start=(kind == 0), stop=(kind == 1))
                last.then_inc(cp_ready, 1)
                pe.wait_ge(vbd_ready, h * GB + i + 1)
                pe.wait_ge(att_ready, h * GB + i + 1)
                for t in range(TH):
                    last = pe.matmul(PV[s][:, t // 4, t % 4, :], Vbd[:, s, t, :], attT[:, s, t // 4, t % 4 * H_:(t % 4 + 1) * H_],
                                     start=True, stop=True)
                last.then_inc(pv_ready, 1)

            scores(0, 0)
            rounds(pe, do_round)
            pe.wait_ge(o_ready, h * GB + GB)
            for n in range(O0, F0):
                u, a = (n - O0) // 4, 4 * ((n - O0) % 4)
                if n >= O0 + 6:
                    bank_free(n)
                for q in range(4):
                    last = pe.transpose(work[:, n % 6, q * P:(q + 1) * P],
                                        OT[:, a + q, 2 * u:2 * u + 2].rearrange("p r g j -> p (r g j)"), c.ident[:])
                last.then_inc(full, 1)
            for n in range(F0, P0):
                u, k, G = (n - F0) // 4, (n - F0) // 2 % 2, 4 * ((n - F0) % 2)
                bank_free(n)
                pe.wait_ge(ok_ready, h * 2 + u + 1)
                for q in range(4):
                    last = pe.transpose(work[:, n % 6, q * P:(q + 1) * P],
                                        OK[:, u, G + q, 8 * k:8 * k + 8, :].rearrange("p a d -> p (a d)"), c.ident[:])
                last.then_inc(full, 1)
            for n in range(P0, JOBS):
                bank_free(n)
                if n in (P0, P0 + 4):
                    u = (n - P0) // 4
                    emptied_wait(pe, F0 + 4 * u + 2, h)
                    emptied_wait(pe, F0 + 4 * u + 3, h)
                for q in range(2):
                    t = 2 * (n - P0) + q
                    for k in range(KD):
                        o = oT[:, k, t % 4, t // 4].rearrange("p n g -> p (n g)")
                        pe.matmul(work[:, n % 6, q * DM:(q + 1) * DM], o, c.w_o[:, k, :],
                                  start=(k == 0), stop=False)
                    last = pe.matmul(work[:, n % 6, q * DM:(q + 1) * DM], c.ones[:], c.bo1[:], start=False, stop=True)
                last.then_inc(full, 1)

        @block.vector
        def _(dve):
            order = Steps(dve, dve_order, h * (8 + 2 * GB))

            def layernorm(n):
                kind, b = LN[n]
                if kind == 1:
                    dve.wait_ge(h1_ready, h * B + b + 1)
                src = [c.X[:, h * TH + (b * TJ + t), :] if kind == 0 else c.H1[:, b * TJ + t, :] for t in range(TJ)]
                for t in range(TJ):
                    last = dve.bn_stats(stats[:, kind, t, :], src[t])
                c.hold(dve, dve_order, order.did(last))
                for t in range(TJ):
                    last = dve.bn_aggr(mv[:, kind, t, :], stats[:, kind, t, :])
                last.then_inc(stats_ready, 1)
                dve.wait_ge(rstd_ready, h * 8 + n + 1)
                if kind == 1 and b:
                    dve.wait_ge(tp_ready, h * 2 * B + 2 * b)
                for t in range(TJ):
                    dst = c.H1[:, b * TJ + t, :] if kind == 0 else xhat[:, t, :]
                    last = dve.tensor_scalar(dst, src[t], mv[:, kind, t, 0:1], rs[:, kind, t:t + 1],
                                             ALU.subtract, ALU.mult)
                last.then_inc(xn_ready if kind == 0 else xhat_ready, 1)

            for n in range(8):
                layernorm(n)
            for n in range(HD0, O0):
                if not by_act[n]:
                    dve.wait_ge(full, h * JOBS + n + 1)
                    empty(n, dve.tensor_copy).then_inc(empty_d, 1)

            def spread_k(i, s):
                dve.tensor_tensor(Kbd[:, s].rearrange("p g (t n) -> p g t n", t=4),
                                  KT[:, bass.ds(i * G8, G8), :].unsqueeze(2).broadcast_to([P, G8, 4, NH]),
                                  c.maskK[:].unsqueeze(1).unsqueeze(3).broadcast_to([P, G8, 4, NH]),
                                  ALU.mult).then_inc(kbd_ready, 1)

            emptied_wait(dve, V0 - 2, h)
            for i in range(2):
                spread_k(i, i)

            def do_round(i, s, more):
                flat = T[:, s].rearrange("p (r g) n -> p r (g n)", r=4)
                at = h * (8 + 2 * GB) + 8 + 2 * i
                dve.wait_ge(s_ready, h * GB + i + 1)
                dve.wait_ge(norm1_ready, h * GB + i + 1)
                dve.tensor_scalar(flat, SC, 0.0, -FMAX, ALU.min, ALU.max).then_inc(dve_order, 1)
                dve.wait_ge(dve_order, at + 1)
                dve.scalar_tensor_tensor(flat, SC, 0.0, flat, ALU.max, ALU.add).then_inc(s_free, 1)
                dve.wait_ge(s_free, h * GB + i + 1)
                dve.tensor_reduce(mx[:, s], T[:, s], AX.X, ALU.max).then_inc(dve_order, 1)
                dve.wait_ge(dve_order, at + 2)
                dve.tensor_scalar(mx[:, s], mx[:, s], FMAX, None, ALU.min).then_inc(c.clamped, 1)
                dve.wait_ge(c.clamped, h * GB + i + 1)
                dve.scalar_tensor_tensor(T[:, s], T[:, s], FMAX, mx[:, s].unsqueeze(2).broadcast_to([P, 4 * G8, NH]),
                                         ALU.min, ALU.subtract).then_inc(t_ready, 1)
                if more:
                    spread_k(i + 2, s)
                dve.wait_ge(e_ready, h * GB + i + 1)
                dve.tensor_reduce(Z[:, s, 0], T[:, s], AX.X, ALU.add).then_inc(c.summed, 1)
                dve.wait_ge(c.summed, h * GB + i + 1)
                dve.reciprocal(Z[:, s, 1], Z[:, s, 0]).then_inc(rz_ready, 1)
                dve.wait_ge(rz_ready, h * GB + i + 1)
                dve.wait_ge(cp_ready, h * GB + i + 1)
                dve.tensor_tensor(PN[:, s, 0], T[:, s, :, 0:H_],
                                  Z[:, s, 1, :].unsqueeze(2).broadcast_to([P, 4 * G8, H_]),
                                  ALU.mult).then_inc(norm0_ready, 1)

            rounds(dve, do_round)
            for u in range(2):
                for n in range(O0 + 4 * u, O0 + 4 * u + 4):
                    if not by_act[n]:
                        dve.wait_ge(full, h * JOBS + n + 1)
                        empty(n, dve.tensor_copy).then_inc(empty_d, 1)
                dve.wait_ge(sq_ready, h * 2 + u + 1)
                dve.tensor_reduce(ss[:, u], SQ[:, u].rearrange("p (n d) -> p n d", d=DV), AX.X,
                                  ALU.add).then_inc(ss_ready, 1)
            for u in range(2):
                dve.wait_ge(rr_ready, h * 2 + u + 1)
                o = OK[:, u].rearrange("p G a d -> p (G a) d")
                dve.tensor_tensor(o, o, rr[:, u].unsqueeze(2).broadcast_to([P, P, DV]), ALU.mult).then_inc(ok_ready, 1)
            for n in range(F0, P0):
                if not by_act[n]:
                    dve.wait_ge(full, h * JOBS + n + 1)
                    empty(n, dve.tensor_copy).then_inc(empty_d, 1)
            for n in range(P0, JOBS):
                m = 2 * (n - P0)
                dve.wait_ge(full, h * JOBS + n + 1)
                dve.tensor_tensor(c.H1[:, m:m + 2, :], c.H1[:, m:m + 2, :],
                                  work[:, n % 6, :].rearrange("p (q n) -> p q n", q=2), ALU.add).then_inc(empty_d, 1)


FF = 1024


def mlp(c, h, own):
    nc, d = c.nc, c.d
    c.phase = "ml_"
    MF = FF // P
    w1 = c.sb("w1", [P, KD, FF], ctx=own)
    w2 = c.sb("w2", [P, MF, DM], ctx=own)
    b2 = c.sb("b2", [1, DM], ctx=own)
    stats = c.sb("stats", [P, TJ, 6], ctx=own)
    mv = c.sb("mv", [P, TJ, 2], ctx=own)
    ve = c.sb("ve", [P, TJ], ctx=own)
    rs = c.sb("rs", [P, TJ], ctx=own)
    xhat = c.sb("xhat", [P, 2, TJ, DM], ctx=own)
    hT = c.sb("hT", [P, 2, KD, TJ * P], ctx=own)
    rT = c.sb("rT", [P, 2, MF, TJ * P], ctx=own)
    tp = c.ps("tp", [P, KD, 512], ctx=own)
    f1 = c.ps("f1", [P, 4, 512], ctx=own)
    f2 = c.ps("f2", [P, 2, 2, DM], ctx=own)
    sem = lambda n: c.sem("mlp_" + n)
    w_loaded, stats_ready, rstd_ready, xhat_ready = sem("w_loaded"), sem("stats"), sem("rstd"), sem("xhat")
    tp_ready, hT_ready, f1_ready, rT_ready = sem("tp"), sem("hT"), sem("f1"), sem("rT")
    f2_ready, f2_free = sem("f2"), sem("f2_free")
    dve_order, pool_order, sum_order = sem("dve_order"), sem("pool_order"), sem("sum_order")

    with nc.Block() as block:

        @block.sync
        def _(sp):
            sp.dma_start(w1[:], d["w1"].rearrange("(k p) n -> p k n", p=P)).then_inc(w_loaded, 16)
            sp.dma_start(w2[:], d["w2"].rearrange("(k p) n -> p k n", p=P)).then_inc(w_loaded, 16)
            sp.dma_start(b2[:], d["rows"][ROW["b2_attn"]:ROW["b2_attn"] + 1, :]).then_inc(w_loaded, 16)

        @block.gpsimd
        def _(pool):
            for b in range(B):
                c.hold(pool, stats_ready, h * B + b + 1)
                pool.tensor_scalar(ve[:], mv[:, :, 1], EPS, None, ALU.add).then_inc(pool_order, 1)
                pool.wait_ge(pool_order, h * B + b + 1)
                pool.tensor_tensor(rs[:], ve[:], c.mhalf[:, 0:TJ], ALU.pow).then_inc(rstd_ready, 1)

        @block.scalar
        def _(act):
            for b in range(B):
                for k in range(KD):
                    act.wait_ge(tp_ready, h * 2 * B + 2 * b + k + 1)
                    g, o = COL["ln2_g"] + k, COL["ln2_b"] + k
                    act.activation(hT[:, b % 2, k, :], tp[:, k, :], ACT.Identity,
                                   bias=c.cols[:, o:o + 1], scale=c.cols[:, g:g + 1]).then_inc(hT_ready, 1)
                if b >= 2:
                    act.wait_ge(f2_ready, h * 2 * B + 2 * (b - 1))
                for m in range(MF):
                    act.wait_ge(f1_ready, h * B * MF + b * MF + m + 1)
                    col = COL["b1"] + m
                    act.activation(rT[:, b % 2, m, :], f1[:, m % 4, :], ACT.Relu,
                                   bias=c.cols[:, col:col + 1]).then_inc(rT_ready, 1)

        @block.tensor
        def _(pe):

            def up(b):
                pe.wait_ge(xhat_ready, h * B + b + 1)
                if b:
                    pe.wait_ge(hT_ready, h * 2 * B + 2 * b)
                for k in range(KD):
                    for t in range(TJ):
                        last = pe.transpose(tp[:, k, t * P:(t + 1) * P], xhat[:, b % 2, t, k * P:(k + 1) * P], c.ident[:])
                    last.then_inc(tp_ready, 1)
                pe.wait_ge(hT_ready, h * 2 * B + 2 * b + 2)
                for m in range(MF):
                    if b * MF + m >= 4:
                        pe.wait_ge(rT_ready, h * B * MF + b * MF + m - 3)
                    for k in range(KD):
                        last = pe.matmul(f1[:, m % 4, :], w1[:, k, m * P:(m + 1) * P], hT[:, b % 2, k, :],
                                         start=(k == 0), stop=(k == KD - 1))
                    last.then_inc(f1_ready, 1)

            def down(b):
                pe.wait_ge(rT_ready, h * B * MF + (b + 1) * MF)
                for n in range(2):
                    if 2 * b + n >= 2:
                        pe.wait_ge(f2_free, h * 2 * B + 2 * b + n - 1)
                    for q in range(2):
                        t = 2 * n + q
                        for m in range(MF):
                            pe.matmul(f2[:, n, q, :], rT[:, b % 2, m, t * P:(t + 1) * P], w2[:, m, :],
                                      start=(m == 0), stop=False)
                        last = pe.matmul(f2[:, n, q, :], c.ones[:], b2[:], start=False, stop=True)
                    last.then_inc(f2_ready, 1)

            pe.wait_ge(w_loaded, h * 48 + 48)
            up(0)
            for b in range(B - 1):
                up(b + 1)
                down(b)
            down(B - 1)

        @block.vector
        def _(dve):

            def layernorm(b):
                for t in range(TJ):
                    last = dve.bn_stats(stats[:, t, :], c.H1[:, b * TJ + t, :])
                last.then_inc(dve_order, 1)
                c.hold(dve, dve_order, h * B + b + 1)
                for t in range(TJ):
                    last = dve.bn_aggr(mv[:, t, :], stats[:, t, :])
                last.then_inc(stats_ready, 1)
                dve.wait_ge(rstd_ready, h * B + b + 1)
                if b >= 2:
                    dve.wait_ge(tp_ready, h * 2 * B + 2 * (b - 1))
                for t in range(TJ):
                    last = dve.tensor_scalar(xhat[:, b % 2, t, :], c.H1[:, b * TJ + t, :], mv[:, t, 0:1],
                                             rs[:, t:t + 1], ALU.subtract, ALU.mult)
                last.then_inc(xhat_ready, 1)

            layernorm(0)
            layernorm(1)
            for b in range(B):
                if b + 2 < B:
                    layernorm(b + 2)
                for n in range(2):
                    m = 2 * b + n
                    y = c.H1[:, 2 * m:2 * m + 2, :]
                    xs = c.X[:, bass.ds(h * TH + 2 * m, 2), :]
                    dve.wait_ge(f2_ready, h * 2 * B + m + 1)
                    dve.tensor_tensor(y, y, f2[:, n], ALU.add).then_inc(f2_free, 1)
                    dve.wait_ge(f2_free, h * 2 * B + m + 1)
                    dve.tensor_tensor(y, y, c.rows1[:, b, 2:3, :].broadcast_to([P, 2, DM]), ALU.mult
                                      ).then_inc(sum_order, 1)
                    dve.wait_ge(sum_order, h * 2 * B + m + 1)
                    dve.tensor_tensor(xs, xs, y, ALU.add)


E_, HM, GR = 8, 512, 16
NT = TILES + E_ - 1


def moe(c, out):
    nc, d = c.nc, c.d
    c.phase = "moe_"
    sorted_h = c.sorted_h
    sorted_y = nc.dram_tensor("sorted_y", (NT * P, DM), F32, kind="Internal").ap()
    sem = lambda n: c.sem("moe_" + n)
    with ExitStack() as own:
        sb = lambda name, shape, dt=F32: c.sb(name, shape, dt, ctx=own)
        w1 = sb("w1", [P, E_, KD, HM])
        w2 = sb("w2", [P, E_, HM // P, DM])
        b1 = sb("b1", [P, E_, HM])
        b2 = sb("b2", [P, E_, DM])
        pos = sb("pos", [P, TILES], U32)
        expert = sb("expert", [1, NT], U32)
        score = sb("score", [P, TILES])
        w_loaded = sem("w_loaded")

        with ExitStack() as st:
            sb1 = lambda name, shape, dt=F32: c.sb(name, shape, dt, ctx=st)
            hrow = sb1("hrow", [P, TILES, DM])
            w_red = sb1("w_red", [P, KD, GR])
            wgT = sb1("wgT", [GR, E_])
            wsq = sb1("wsq", [GR, E_])
            stats = sb1("stats", [P, 2, TJ, 6])
            mv = sb1("mv", [P, 2, TJ, 2])
            ve = sb1("ve", [P, 2, TJ])
            rs = sb1("rs", [P, 2, TJ])
            xhat = sb1("xhat", [P, 2, TJ, DM])
            rows_scaled, rows_ready = sem("rows_scaled"), sem("rows_ready")
            hT = sb1("hT", [P, KD, TJ * P])
            xr = sb1("xr", [GR, TJ * P])
            full1 = sb1("full1", [P, P])
            upper = sb1("upper", [P, P])
            L = sb1("L", [P, TILES, E_])
            O = sb1("O", [P, TILES, E_])
            W = sb1("W", [P, TILES, E_])
            iota = sb1("iota", [P, E_])
            tile_no = sb1("tile_no", [P, NT])
            ends = sb1("ends", [P, NT, E_])
            mx = sb1("mx", [P, TILES])
            tmp = sb1("tmp", [P, TILES])
            cnt = sb1("cnt", [P, 8, E_])
            cnt_i = sb1("cnt_i", [P, E_], I32)
            tp = c.ps("tp", [P, KD, 512], ctx=st)
            rp = c.ps("rp", [P, 512], ctx=st)
            lp = c.ps("lp", [P, 512], ctx=st)
            pre = c.ps("pre", [P, 512], ctx=st)
            tot = c.ps("tot", [P, 512], ctx=st)
            np_ = c.ps("np", [P, 512], ctx=st)
            r_loaded, stats_ready, rstd_ready, xhat_ready = sem("r_loaded"), sem("stats"), sem("rstd"), sem("xhat")
            tp_ready, hT_ready, rp_ready, xr_ready = sem("tp"), sem("hT"), sem("rp"), sem("xr")
            lp_ready, lp_free, l_done = sem("lp"), sem("lp_free"), sem("l_done")
            ln_order = sem("ln_order")
            dve_order, pool_order, sent = sem("dve_order"), sem("pool_order"), sem("sent")
            wsq_ready, norm_ready, sqrt_ready, wg_ready = sem("wsq"), sem("norm"), sem("sqrt"), sem("wg")
            m_ready, exp_ready, o_ready, count_ready, pos_ready = (sem("m"), sem("exp"), sem("o"), sem("count"),
                                                                   sem("pos"))
            const_ready = sem("const")

            with nc.Block() as block:

                @block.sync
                def _(sp):
                    sp.dma_start(w_red[:], d["w_red"].rearrange("(k p) n -> p k n", p=P)).then_inc(r_loaded, 16)
                    sp.dma_start(wgT[:], d["wgT"]).then_inc(r_loaded, 16)
                    for e in range(E_):
                        sp.dma_start(w1[:, e], d["moe_w1"][e].rearrange("(k p) n -> p k n", p=P)).then_inc(w_loaded, 16)
                        sp.dma_start(w2[:, e], d["moe_w2"][e].rearrange("(k p) n -> p k n", p=P)).then_inc(w_loaded, 16)
                    sp.dma_start(b1[:].rearrange("p e n -> p (e n)"), d["moe_b1"].rearrange("e n -> (e n)").unsqueeze(0)
                                 .broadcast_to([P, E_ * HM])).then_inc(w_loaded, 16)
                    sp.dma_start(b2[:].rearrange("p e n -> p (e n)"), d["moe_b2"].rearrange("e n -> (e n)").unsqueeze(0)
                                 .broadcast_to([P, E_ * DM])).then_inc(w_loaded, 16)

                @block.gpsimd
                def _(pool):
                    pool.memset(full1[:], 1.0).then_inc(const_ready, 1)
                    pool.memset(upper[:], 1.0).then_inc(pool_order, 1)
                    pool.iota(iota[:], pattern=[[1, E_]], base=0, channel_multiplier=0,
                              allow_small_or_imprecise_dtypes=True)
                    pool.iota(tile_no[:], pattern=[[1, NT]], base=0, channel_multiplier=0,
                              allow_small_or_imprecise_dtypes=True)
                    pool.wait_ge(pool_order, 1)
                    pool.affine_select(out=upper[:], in_=upper[:], compare_op=ALU.is_gt, fill=0.0,
                                       base=0, pattern=[[1, P]], channel_multiplier=-1).then_inc(const_ready, 1)
                    def rstd(q, s):
                        c.hold(pool, stats_ready, q + 1)
                        pool.tensor_scalar(ve[:, s], mv[:, s, :, 1], EPS, None, ALU.add).then_inc(pool_order, 1)
                        pool.wait_ge(pool_order, q + 2)
                        pool.tensor_tensor(rs[:, s], ve[:, s], c.mhalf[:, 0:TJ], ALU.pow).then_inc(rstd_ready, 1)

                    with pool.Fori(0, HALVES) as hh:
                        rstd(hh * B, 0)
                        for b in range(B):
                            if b + 1 < B:
                                rstd(hh * B + b + 1, (b + 1) % 2)
                            rows = hrow[:, bass.ds(hh * TH + b * TJ, TJ), :]
                            c.hold(pool, xhat_ready, hh * B + b + 1)
                            pool.tensor_tensor(rows, xhat[:, b % 2], c.rows1[:, b, 4:5, :].broadcast_to([P, TJ, DM]),
                                               ALU.mult).then_inc(rows_scaled, 1)
                            c.hold(pool, rows_scaled, hh * B + b + 3)
                            pool.tensor_tensor(rows, rows, c.rows1[:, b, 3:4, :].broadcast_to([P, TJ, DM]),
                                               ALU.add).then_inc(rows_ready, 1)
                    pool.wait_ge(pos_ready, 1)
                    pool.wait_ge(rows_ready, 2 * B)
                    for t in range(TILES):
                        pool.indirect_dma_start(sorted_h, bass.IndirectOffsetOnAxis(ap=pos[:, t:t + 1], axis=0),
                                                hrow[:, t, :], None).then_inc(sent, 16)
                    pool.wait_ge(sent, 16 * TILES)

                @block.scalar
                def _(act):
                    act.wait_ge(norm_ready, 1)
                    act.activation(wsq[:], np_[0:GR, 0:E_], ACT.Sqrt).then_inc(sqrt_ready, 1)
                    with act.Fori(0, HALVES) as hh:
                        for b in range(B):
                            q = hh * B + b
                            for k in range(KD):
                                act.wait_ge(tp_ready, q * 2 + k + 1)
                                act.activation(hT[:, k, :], tp[:, k, :], ACT.Identity,
                                               bias=c.modT[1][:, 3 * KD + k, b:b + 1],
                                               scale=c.modT[1][:, 4 * KD + k, b:b + 1]).then_inc(hT_ready, 1)
                            act.wait_ge(rp_ready, q + 1)
                            act.copy(xr[:], rp[0:GR, :]).then_inc(xr_ready, 1)
                    act.wait_ge(m_ready, 1)
                    act.activation(W[:], W[:], ACT.Exp).then_inc(exp_ready, 1)

                @block.tensor
                def _(pe):
                    pe.wait_ge(wsq_ready, 1)
                    pe.wait_ge(const_ready, 2)
                    pe.matmul(np_[0:GR, 0:E_], full1[0:GR, 0:GR], wsq[:], start=True, stop=True).then_inc(norm_ready, 1)
                    pe.wait_ge(wg_ready, 1)

                    def turn(q, s):
                        pe.wait_ge(xhat_ready, q + 1)
                        for k in range(KD):
                            for t in range(TJ):
                                last = pe.transpose(tp[:, k, t * P:(t + 1) * P], xhat[:, s, t, k * P:(k + 1) * P],
                                                    c.ident[:])
                            last.then_inc(tp_ready, 1)

                    with pe.Fori(0, HALVES) as hh:
                        turn(hh * B, 0)
                        for b in range(B):
                            q = hh * B + b
                            pe.wait_ge(hT_ready, q * 2 + 2)
                            for k in range(KD):
                                last = pe.matmul(rp[0:GR, :], w_red[:, k, :], hT[:, k, :], start=(k == 0),
                                                 stop=(k == KD - 1))
                            last.then_inc(rp_ready, 1)
                            if b + 1 < B:
                                turn(q + 1, (b + 1) % 2)
                            pe.wait_ge(xr_ready, q + 1)
                            pe.wait_ge(lp_free, q + 1)
                            for t in range(TJ):
                                last = pe.matmul(lp[:, t * E_:(t + 1) * E_], xr[:, t * P:(t + 1) * P], wgT[:],
                                                 start=True, stop=True)
                            last.then_inc(lp_ready, 1)
                    pe.wait_ge(o_ready, 1)
                    o = O[:].rearrange("p t e -> p (t e)")
                    pe.matmul(pre[:, 0:TILES * E_], upper[:], o, start=True, stop=True)
                    pe.matmul(tot[:, 0:TILES * E_], full1[:], o, start=True, stop=True).then_inc(count_ready, 1)

                @block.vector
                def _(dve):
                    order = Steps(dve, dve_order)
                    dve.wait_ge(r_loaded, 32)
                    dve.tensor_tensor(wsq[:], wgT[:], wgT[:], ALU.mult).then_inc(wsq_ready, 1)
                    dve.wait_ge(sqrt_ready, 1)
                    order.then(dve.tensor_scalar(wsq[:], wsq[:], 1e-4, None, ALU.max))
                    order.then(dve.reciprocal(wsq[:], wsq[:]))
                    dve.tensor_tensor(wgT[:], wgT[:], wsq[:], ALU.mult).then_inc(wg_ready, 1)
                    dve.sem_inc(lp_free, 1)

                    dve.sem_inc(rows_scaled, 2)

                    def layernorm(q, s):
                        for t in range(TJ):
                            last = dve.bn_stats(stats[:, s, t, :], c.X[:, q * TJ + t, :])
                        last.then_inc(ln_order, 1)
                        c.hold(dve, ln_order, q + 1)
                        for t in range(TJ):
                            last = dve.bn_aggr(mv[:, s, t, :], stats[:, s, t, :])
                        last.then_inc(stats_ready, 1)
                        dve.wait_ge(rstd_ready, q + 1)
                        dve.wait_ge(rows_scaled, q + 1)
                        for t in range(TJ):
                            last = dve.tensor_scalar(xhat[:, s, t, :], c.X[:, q * TJ + t, :],
                                                     mv[:, s, t, 0:1], rs[:, s, t:t + 1], ALU.subtract, ALU.mult)
                        last.then_inc(xhat_ready, 1)

                    with dve.Fori(0, HALVES) as hh:
                        layernorm(hh * B, 0)
                        for b in range(B):
                            q = hh * B + b
                            if b + 1 < B:
                                layernorm(q + 1, (b + 1) % 2)
                            dve.wait_ge(lp_ready, q + 1)
                            dve.tensor_copy(L[:, bass.ds(q * TJ, TJ), :],
                                            lp[:, 0:TJ * E_].rearrange("p (t e) -> p t e", e=E_)).then_inc(lp_free, 1)
                    dve.wait_ge(lp_free, 2 * B + 1)

                    def over_e(x):
                        return x.unsqueeze(2).broadcast_to([P, TILES, E_])

                    def over_t(x):
                        return x.unsqueeze(1).broadcast_to([P, TILES, E_])

                    order.then(dve.tensor_reduce(mx[:], L[:], AX.X, ALU.max))
                    dve.tensor_tensor(W[:], L[:], over_e(mx[:]), ALU.subtract).then_inc(m_ready, 1)
                    order.then(dve.tensor_tensor(L[:], L[:], over_e(mx[:]), ALU.is_equal))
                    order.then(dve.scalar_tensor_tensor(L[:], L[:], -float(E_), over_t(iota[:]), ALU.mult, ALU.add))
                    order.then(dve.tensor_reduce(mx[:], L[:], AX.X, ALU.min))
                    dve.tensor_tensor(O[:], L[:], over_e(mx[:]), ALU.is_equal).then_inc(o_ready, 1)
                    dve.wait_ge(exp_ready, 1)
                    order.then(dve.tensor_reduce(tmp[:], W[:], AX.X, ALU.add))
                    order.then(dve.reciprocal(score[:], tmp[:]))
                    dve.wait_ge(count_ready, 1)
                    order.then(dve.tensor_copy(W[:], tot[:, 0:TILES * E_].rearrange("p (t e) -> p t e", e=E_)))
                    dve.wait_ge(o_ready, 1)
                    for e in range(E_):
                        order.did(dve.tensor_tensor_scan(L[:, :, e], full1[:, 0:TILES], W[:, :, e], 0.0,
                                                           ALU.mult, ALU.add))
                    dve.wait_ge(dve_order, order.n)
                    order.then(dve.tensor_scalar(cnt[:, 0, :], L[:, TILES - 1, :], float(P - 1), None, ALU.add))
                    order.then(dve.tensor_tensor(L[:], L[:], W[:], ALU.subtract))
                    order.then(dve.tensor_tensor(L[:], L[:], pre[:, 0:TILES * E_].rearrange("p (t e) -> p t e", e=E_),
                                                 ALU.add))
                    order.then(dve.tensor_copy(cnt_i[:], cnt[:, 0, :]))
                    order.then(dve.tensor_scalar(cnt_i[:], cnt_i[:], 7, None, ALU.arith_shift_right))
                    order.then(dve.tensor_copy(cnt[:, 1, :], cnt_i[:]))
                    order.then(dve.tensor_tensor_scan(cnt[:, 2, :], full1[:, 0:E_], cnt[:, 1, :], 0.0, ALU.mult, ALU.add))
                    order.then(dve.tensor_tensor(cnt[:, 3, :], cnt[:, 2, :], cnt[:, 1, :], ALU.subtract))
                    order.then(dve.scalar_tensor_tensor(L[:], over_t(cnt[:, 3, :]), float(P), L[:], ALU.mult, ALU.add))
                    order.then(dve.tensor_tensor(L[:], L[:], O[:], ALU.mult))
                    order.then(dve.tensor_reduce(tmp[:], L[:], AX.X, ALU.add))
                    dve.tensor_copy(pos[:], tmp[:]).then_inc(pos_ready, 1)
                    order.then(dve.tensor_tensor(ends[:], cnt[:, 2, :].unsqueeze(1).broadcast_to([P, NT, E_]),
                                                 tile_no[:].unsqueeze(2).broadcast_to([P, NT, E_]), ALU.is_le))
                    order.then(dve.tensor_reduce(tile_no[:], ends[:], AX.X, ALU.add))
                    order.then(dve.tensor_scalar(tile_no[:], tile_no[:], float(E_ - 1), None, ALU.min))
                    dve.tensor_copy(expert[:], tile_no[0:1, :])

        with ExitStack() as st:
            sb2 = lambda name, shape, dt=F32: c.sb(name, shape, dt, ctx=st)
            hs = sb2("hs", [P, 3, DM])
            hsT = sb2("hsT", [P, 2, KD, P])
            a = sb2("a", [P, 2, HM])
            aT = sb2("aT", [P, 2, HM // P, P])
            ys = sb2("ys", [P, 3, DM])
            tp = c.ps("tp2", [P, 2, 512], ctx=st)
            up = c.ps("up", [P, 2, HM], ctx=st)
            ap = c.ps("ap", [P, 2, 512], ctx=st)
            dn = c.ps("dn", [P, 2, 512], ctx=st)
            hs_loaded = [sem(f"hs_loaded{i}") for i in range(3)]
            ys_stored = [sem(f"ys_stored{i}") for i in range(3)]
            tp_ready, hsT_ready, up_ready, up_free = sem("tp2"), sem("hsT"), sem("up"), sem("up_free")
            a_ready, ap_ready, aT_ready, dn_ready, ys_ready = sem("a"), sem("ap"), sem("aT"), sem("dn"), sem("ys")

            def tiles(eng, do_tile):
                with eng.Fori(0, NT // 6) as i6:
                    for j in range(6):
                        do_tile(i6 * 6 + j, i6 * 2 + j // 3, j)
                for n in range(NT // 6 * 6, NT):
                    do_tile(n, n // 3, n)

            with nc.Block() as block:

                @block.gpsimd
                def _(pool):
                    def do_tile(n, turn, j):
                        pool.wait_ge(hsT_ready, n + 1)
                        pool.dma_start(hs[:, j % 3, :], sorted_h[bass.ds(n * P, P), :]).then_inc(hs_loaded[j % 3], 16)
                    tiles(pool, do_tile)

                @block.sync
                def _(sp):
                    def do_tile(n, turn, j):
                        sp.wait_ge(ys_ready, n + 4)
                        sp.dma_start(sorted_y[bass.ds(n * P, P), :], ys[:, j % 3, :]).then_inc(ys_stored[j % 3], 16)
                    tiles(sp, do_tile)
                    for i in range(3):
                        sp.wait_ge(ys_stored[i], 16 * (NT // 3) + 16)

                @block.tensor
                def _(pe):
                    pe.wait_ge(w_loaded, 16 * (2 * E_ + 2))

                    def expert_of(n):
                        return pe.value_load(expert[0:1, bass.ds(n, 1)], min_val=0, max_val=E_ - 1)

                    def turn_h(n, turn, j):
                        pe.wait_ge(hs_loaded[j % 3], turn * 16 + 16)
                        for k in range(KD):
                            last = pe.transpose(tp[:, j % 2, k * P:(k + 1) * P], hs[:, j % 3, k * P:(k + 1) * P], c.ident[:])
                        last.then_inc(tp_ready, 1)

                    def go_up(n, j, e):
                        pe.wait_ge(hsT_ready, n + 4)
                        pe.wait_ge(up_free, n + 1)
                        for k in range(KD):
                            last = pe.matmul(up[:, j % 2, :], hsT[:, j % 2, k, :], w1[:, bass.ds(e, 1), k, :],
                                             start=(k == 0), stop=(k == KD - 1))
                        last.then_inc(up_ready, 1)

                    def do_tile(n, turn, j):
                        e = expert_of(n)
                        e_next = expert_of(n + 1) if not isinstance(n, int) or n + 1 < NT else None
                        pe.wait_ge(a_ready, n + 1)
                        for m in range(HM // P):
                            last = pe.transpose(ap[:, j % 2, m * P:(m + 1) * P], a[:, j % 2, m * P:(m + 1) * P], c.ident[:])
                        last.then_inc(ap_ready, 1)
                        if not isinstance(n, int) or n + 2 < NT:
                            turn_h(n + 2, turn + (2 + j % 3) // 3, j + 2)
                        if e_next is not None:
                            go_up(n + 1, j + 1, e_next)
                        pe.wait_ge(aT_ready, n + 1)
                        for m in range(HM // P):
                            last = pe.matmul(dn[:, j % 2, 0:DM], aT[:, j % 2, m, :], w2[:, bass.ds(e, 1), m, :],
                                             start=(m == 0), stop=(m == HM // P - 1))
                        last.then_inc(dn_ready, 1)

                    turn_h(0, 0, 0)
                    turn_h(1, 0, 1)
                    go_up(0, 0, expert_of(0))
                    tiles(pe, do_tile)

                @block.scalar
                def _(act):
                    act.sem_inc(hsT_ready, 3)

                    def turned(n, j):
                        act.wait_ge(tp_ready, n + 1)
                        act.copy(hsT[:, j % 2].rearrange("p k n -> p (k n)"), tp[:, j % 2, 0:DM]).then_inc(hsT_ready, 1)

                    def gelu(n, j):
                        act.wait_ge(up_free, n + 3)
                        act.activation(a[:, j % 2, :], a[:, j % 2, :], ACT.Gelu).then_inc(a_ready, 1)

                    def do_tile(n, turn, j):
                        act.wait_ge(ap_ready, n + 1)
                        act.copy(aT[:, j % 2].rearrange("p m n -> p (m n)"), ap[:, j % 2, :]).then_inc(aT_ready, 1)
                        if not isinstance(n, int) or n + 2 < NT:
                            turned(n + 2, j)
                        if not isinstance(n, int) or n + 1 < NT:
                            gelu(n + 1, j + 1)

                    turned(0, 0)
                    turned(1, 1)
                    gelu(0, 0)
                    tiles(act, do_tile)

                @block.vector
                def _(dve):
                    dve.sem_inc(up_free, 2)
                    dve.sem_inc(ys_ready, 3)
                    for i in range(3):
                        dve.sem_inc(ys_stored[i], 16)

                    def expert_of(n):
                        return dve.value_load(expert[0:1, bass.ds(n, 1)], min_val=0, max_val=E_ - 1)

                    def add_b1(n, j):
                        e = expert_of(n)
                        dve.wait_ge(up_ready, n + 1)
                        dve.tensor_tensor(a[:, j % 2, :], up[:, j % 2, :], b1[:, bass.ds(e, 1), :].rearrange(
                            "p o n -> p (o n)"), ALU.add).then_inc(up_free, 1)

                    def do_tile(n, turn, j):
                        if not isinstance(n, int) or n + 1 < NT:
                            add_b1(n + 1, j + 1)
                        e = expert_of(n)
                        dve.wait_ge(dn_ready, n + 1)
                        dve.wait_ge(ys_stored[j % 3], turn * 16 + 16)
                        dve.tensor_tensor(ys[:, j % 3, :], dn[:, j % 2, 0:DM], b2[:, bass.ds(e, 1), :].rearrange(
                            "p o n -> p (o n)"), ALU.add).then_inc(ys_ready, 1)

                    add_b1(0, 0)
                    tiles(dve, do_tile)

        with ExitStack() as st:
            y = c.sb("y", [P, 8, DM], ctx=st)
            taken, gated, x_ready, stored = ([sem(f"taken{i}") for i in range(8)], sem("gated"),
                                             sem("x_ready"), sem("stored"))
            with nc.Block() as block:

                @block.gpsimd
                def _(pool):
                    for t in range(TILES):
                        if t >= 8:
                            pool.wait_ge(x_ready, t - 7)
                        pool.indirect_dma_start(y[:, t % 8, :], None, sorted_y,
                                                bass.IndirectOffsetOnAxis(ap=pos[:, t:t + 1], axis=0)
                                                ).then_inc(taken[t % 8], 16)

                @block.vector
                def _(dve):
                    for t in range(TILES):
                        b = t % TH // TJ
                        dve.wait_ge(taken[t % 8], 16 * (t // 8) + 16)
                        dve.scalar_tensor_tensor(y[:, t % 8, :], y[:, t % 8, :], score[:, t:t + 1], c.rows1[:, b, 5, :],
                                                 ALU.mult, ALU.mult).then_inc(gated, 1)
                        dve.wait_ge(gated, t + 1)
                        dve.tensor_tensor(c.X[:, t, :], c.X[:, t, :], y[:, t % 8, :], ALU.add).then_inc(x_ready, 1)

                @block.sync
                def _(sp):
                    for h in range(HALVES):
                        for b in range(B):
                            at = h * TH + b * TJ
                            sp.wait_ge(x_ready, at + TJ)
                            sp.dma_start(out[b, h * TJ * P:(h + 1) * TJ * P, :].rearrange("(t p) n -> p t n", p=P),
                                         c.X[:, at:at + TJ, :]).then_inc(stored, 16)
                    sp.wait_ge(stored, 16 * B * HALVES)


def program(nc, d, out):
    with ExitStack() as ctx:
        c = Core(nc, ctx, d)
        c.layer0 = ctx.enter_context(ExitStack())
        c.sorted_h = nc.dram_tensor("sorted_h", (NT * P, DM), F32, kind="Internal").ap()
        setup(c)
        gru(c)
        ffn(c)
        c.layer0.close()
        c.layer1 = ctx.enter_context(ExitStack())
        attention_setup(c)
        c.H1 = c.sb("H1", [P, TH, DM], ctx=c.layer1)
        with nc.Fori(0, HALVES) as h:
            with ExitStack() as own:
                attention(c, h, own)
            with ExitStack() as own:
                mlp(c, h, own)
        c.layer1.close()
        moe(c, out)


def lay_out(inputs):
    g = {k: np.asarray(v) for k, v in inputs.items()}
    a = {}
    a["x"] = g["L0_attn_x"]
    a["cT"] = np.stack([g["L0_c"].T, g["L1_c"].T])
    a["wmod"] = np.stack([g["L0_wmod"], g["L1_wmod"]])
    cols = np.zeros((P, NCOL), np.float32)
    src = {"bz_f": "L0_attn_bz_f", "bh_f": "L0_attn_bh_f", "bz_b": "L0_attn_bz_b", "bh_b": "L0_attn_bh_b",
           "bf": "L0_ffn_bf", "bi": "L0_ffn_bi", "bc": "L0_ffn_bc", "in_c": "L0_ffn_in_c",
           "ln1_g": "L1_attn_ln1_g", "ln1_b": "L1_attn_ln1_b", "ln2_g": "L1_attn_ln2_g",
           "ln2_b": "L1_attn_ln2_b", "b1": "L1_attn_b1"}
    for name, key in src.items():
        v = g[key].reshape(-1, P).T
        cols[:, COL[name]:COL[name] + v.shape[1]] = v
    a["cols"] = cols
    a["rows"] = np.stack([g["L0_attn_b_out"], g["L0_ffn_bo"], g["L1_attn_bo"], g["L1_attn_b2"]])
    a["wg"] = np.stack([g["L0_attn_Wz_f"], g["L0_attn_Wh_f"], g["L0_attn_Wz_b"], g["L0_attn_Wh_b"]])
    a["wo0"] = g["L0_attn_W_out"]
    l1 = "L1_attn_"
    heads = lambda w: w.T.reshape(DM, H_, D_, 2).transpose(0, 3, 1, 2).reshape(DM, DM)
    a["w_qk"] = np.concatenate([heads(g[l1 + "Wq"]), heads(g[l1 + "Wk"])], axis=1)
    a["w_v"], a["w_o"] = g[l1 + "Wv"].T, g[l1 + "Wo"].T
    a["lam"] = np.stack([g[l1 + n] for n in ("lq1", "lq2", "lk1", "lk2")])
    a["w1"], a["w2"] = g[l1 + "W1"].T, g[l1 + "W2"].T
    f1 = "L1_ffn_"
    a["w_red"], a["wgT"] = g[f1 + "w_red"], g[f1 + "wg"].T
    a["moe_w1"], a["moe_w2"], a["moe_b1"], a["moe_b2"] = (g[f1 + n] for n in ("W1", "W2", "b1", "b2"))
    p = np.arange(P)[:, None]
    a["maskK"] = np.where(p // D_ % 4 == np.arange(4), D_ ** -0.5, 0.0).astype(np.float32)
    j, kind, head = p // NH, p // H_ % 2, p % H_
    col = np.arange(64)
    a["combine"] = np.stack([(kind == n) & (j == col // H_) & (head == col % H_) for n in range(2)], 1
                            ).astype(np.float32)
    a["maskV"] = (p // H_ == np.arange(G8)).astype(np.float32)
    f = "L0_ffn_"
    a["w_ffn"] = np.stack([g[f + n].T for n in ("wf", "uf", "wi", "ui", "wc", "uc", "wo", "uo")])
    return a


def kernel(**inputs):
    import concourse.bacc as bacc
    from concourse.bass_utils import run_bass_kernel_spmd

    arrays = {f"in_{n}": np.ascontiguousarray(a) for n, a in lay_out(inputs).items()}
    nc = bacc.Bacc("TRN2", target_bir_lowering=False, num_devices=1)
    d = {n[3:]: nc.dram_tensor(n, a.shape, mybir.dt.from_np(a.dtype), kind="ExternalInput").ap()
         for n, a in arrays.items()}
    out = nc.dram_tensor("out", (B, S, DM), F32, kind="ExternalOutput").ap()
    program(nc, d, out)
    r = run_bass_kernel_spmd(nc, [arrays], core_ids=[0])
    return r.results[0]["out"]
```

```python
from contextlib import ExitStack

import numpy as np

import concourse.bass as bass
from concourse import mybir

F32 = mybir.dt.float32
U32 = mybir.dt.uint32
I32 = mybir.dt.int32
ALU = mybir.AluOpType
ACT = mybir.ActivationFunctionType
AX = mybir.AxisListType

P = 128
B, S, DM = 4, 1024, 256
TILES = B * S // P
TB = S // P
HALVES = 2
TJ = TB // HALVES
TH = B * TJ
KD = DM // P
EPS = 1e-5
LAMBDA_INIT = 0.8 - 0.6 * float(np.exp(-0.3 * 1.0))
FMAX = float(np.finfo(np.float32).max)

COL = {}
_n = 0
for _name, _blocks in (("bz_f", 2), ("bh_f", 2), ("bz_b", 2), ("bh_b", 2), ("bf", 2), ("bi", 2), ("bc", 2),
                       ("in_c", 2), ("ln1_g", 2), ("ln1_b", 2), ("ln2_g", 2), ("ln2_b", 2), ("b1", 8)):
    COL[_name] = _n
    _n += _blocks
NCOL = _n
ROW = {n: i for i, n in enumerate(("b_out", "bo_ffn", "bo_attn", "b2_attn"))}
NROW = len(ROW)


class Steps:

    def __init__(self, eng, sem, base=0):
        self.eng, self.sem, self.base, self.n = eng, sem, base, 0

    def did(self, ins):
        ins.then_inc(self.sem, 1)
        self.n += 1
        return self.base + self.n

    def then(self, ins):
        self.eng.wait_ge(self.sem, self.did(ins))


class Core:

    def __init__(self, nc, ctx, d):
        self.nc, self.ctx, self.d = nc, ctx, d
        self.phase = ""
        self.clamped, self.summed = self.sem("attn_clamped"), self.sem("attn_summed")
        self.updated = self.sem("updated")
        self.passed = self.sem("passed")

    def hold(self, eng, sem, value):
        eng.wait_ge(sem, value)
        eng.sem_inc(self.passed, 1)

    def sem(self, name):
        return self.ctx.enter_context(self.nc.semaphore(name))

    def sb(self, name, shape, dt=F32, ctx=None):
        return (ctx or self.ctx).enter_context(self.nc.sbuf_tensor(self.phase + name, shape, dt))

    def ps(self, name, shape, dt=F32, ctx=None):
        return (ctx or self.ctx).enter_context(self.nc.psum_tensor(self.phase + name, shape, dt))


COL_PARTS = (tuple((0, j) for j in (0, 1, 3, 4)) + tuple((1, j) for j in (3, 4)))


def gru_stats(c, dve, order, b):
    for t in range(TB):
        last = order.did(dve.bn_stats(c.gru_stats[:, t, :], x_tile(c, b, t)))
    c.hold(dve, order.sem, last)
    for t in range(TB):
        last = dve.bn_aggr(c.gru_mv[:, t, :], c.gru_stats[:, t, :])
    last.then_inc(c.gru_stats_ready, 1)


def gru_normalize(c, dve, b):
    dve.wait_ge(c.gru_rstd_ready, b + 1)
    for t in range(TB):
        last = dve.tensor_scalar(c.gru_xhat[:, t, :], x_tile(c, b, t), c.gru_mv[:, t, 0:1], c.gru_rs[:, t:t + 1],
                                 ALU.subtract, ALU.mult)
        if t % TJ == TJ - 1:
            last.then_inc(c.gru_xhat_ready, 1)


def gru_rstd(c, pool, b):
    c.hold(pool, c.gru_stats_ready, b + 1)
    pool.tensor_scalar(c.gru_ve[:], c.gru_mv[:, :, 1], EPS, None, ALU.add).then_inc(c.gru_pool_order, 1)
    pool.wait_ge(c.gru_pool_order, b + 1)
    pool.tensor_tensor(c.gru_rs[:], c.gru_ve[:], c.mhalf[:, 0:TB], ALU.pow).then_inc(c.gru_rstd_ready, 1)


def x_tile(c, b, t):
    return c.X[:, b * TJ + (t // TJ * TH + t % TJ), :]


def lasting(c):
    c.X = c.sb("X", [P, TILES, DM])
    c.cols = c.sb("cols", [P, NCOL])
    c.nbz = c.sb("nbz", [P, 2, KD])
    c.ident = c.sb("ident", [P, P])
    c.ones = c.sb("ones", [1, P])
    c.mhalf = c.sb("mhalf", [P, TB])
    c.modT = [c.sb(f"modT{l}", [P, 6 * KD, B]) for l in range(2)]
    c.rows1 = c.sb("rows1", [P, B, 6, DM])


def setup(c):
    nc, d = c.nc, c.d
    c.rows0 = c.sb("rows0", [P, B, 2, DM], ctx=c.layer0)
    c.w_ffn = c.sb("w_ffn", [P, 8, KD, DM], ctx=c.layer0)
    c.ffn_w_loaded = c.sem("ffn_w_loaded")
    g = c.gru_own
    c.wg = c.sb("wg", [P, 4, KD, DM], ctx=g)
    c.wo = c.sb("wo", [P, 5, DM], ctx=g)
    c.gru_stats, c.gru_mv = c.sb("gru_stats", [P, TB, 6], ctx=g), c.sb("gru_mv", [P, TB, 2], ctx=g)
    c.gru_ve, c.gru_rs = c.sb("gru_ve", [P, TB], ctx=g), c.sb("gru_rs", [P, TB], ctx=g)
    c.gru_xhat = c.sb("gru_xhat", [P, TB, DM], ctx=g)
    c.gru_stats_ready, c.gru_rstd_ready = c.sem("gru_stats_ready"), c.sem("gru_rstd_ready")
    c.gru_xhat_ready, c.gru_pool_order = c.sem("gru_xhat_ready"), c.sem("gru_pool_order")
    c.gru_w_loaded, c.rows_loaded = c.sem("gru_w_loaded"), c.sem("rows_loaded")
    x_first, c.x_loaded = c.sem("x_first"), c.sem("x_loaded")
    rows_dram = nc.dram_tensor("mod_rows", (B, 8, DM), F32, kind="Internal").ap()

    with ExitStack() as own:
        wmod = [c.sb(f"wmod{l}", [P, KD, 6 * DM], ctx=own) for l in range(2)]
        cT = c.sb("cT", [P, 2, KD, B], ctx=own)
        sT = c.sb("sT", [P, 2, KD, B], ctx=own)
        rows = c.sb("rows", [B, 8, DM], ctx=own)
        mag = c.sb("mag", [B, 2, DM], ctx=own)
        sgn = c.sb("sgn", [B, 2, DM], ctx=own)
        colp = c.ps("colp", [P, len(COL_PARTS), KD, B], ctx=own)
        rowp = c.ps("rowp", [P, 4, 512], ctx=own)
        mod_loaded, silu_ready = c.sem("mod_loaded"), c.sem("silu_ready")
        colp_ready, rowp_ready, rows_ready = c.sem("colp_ready"), c.sem("rowp_ready"), c.sem("rows_ready")
        rows_stored, dve_order, ident_clear = c.sem("rows_stored"), c.sem("dve_order0"), c.sem("ident_clear")

        with nc.Block() as block:

            def load_x(eng, b, sem):
                for h in range(HALVES):
                    at = h * TH + b * TJ
                    eng.dma_start(c.X[:, at:at + TJ, :], d["x"][b, h * TJ * P:(h + 1) * TJ * P, :].rearrange(
                        "(t p) n -> p t n", p=P)).then_inc(sem, 16)

            @block.sync
            def _(sp):
                sp.dma_start(cT[:], d["cT"].rearrange("l (k p) b -> p l k b", p=P)).then_inc(mod_loaded, 16)
                sp.dma_start(c.cols[:], d["cols"]).then_inc(mod_loaded, 16)
                for l in range(2):
                    sp.dma_start(wmod[l][:], d["wmod"][l].rearrange("(k p) n -> p k n", p=P)).then_inc(mod_loaded, 16)
                sp.dma_start(c.wg[:], d["wg"].rearrange("w (k p) n -> p w k n", p=P)).then_inc(c.gru_w_loaded, 16)
                sp.dma_start(c.wo[:, 0:4, :], d["wo0"].rearrange("(k p) n -> p k n", p=P)).then_inc(c.gru_w_loaded, 16)
                r = d["rows"][ROW["b_out"]:ROW["b_out"] + 1, :]
                sp.dma_start(c.wo[:, 4, :], r.broadcast_to([P, DM])).then_inc(c.gru_w_loaded, 16)
                for b in range(1, B):
                    load_x(sp, b, c.x_loaded)
                sp.dma_start(c.w_ffn[:], d["w_ffn"].rearrange("w (k p) n -> p w k n", p=P)).then_inc(c.ffn_w_loaded, 16)
                load_attention_constants(c, sp)
                sp.wait_ge(rows_ready, 3)
                sp.dma_start(rows_dram, rows[:]).then_inc(rows_stored, 16)
                sp.wait_ge(rows_stored, 16)
                sp.dma_start(c.rows0[:], rows_dram[:, 0:2, :].unsqueeze(0).broadcast_to([P, B, 2, DM])
                             ).then_inc(c.rows_loaded, 16)
                sp.dma_start(c.rows1[:], rows_dram[:, 2:8, :].unsqueeze(0).broadcast_to([P, B, 6, DM])
                             ).then_inc(c.rows_loaded, 16)

            @block.gpsimd
            def _(pool):
                pool.memset(c.ones[:], 1.0)
                pool.memset(c.mhalf[:], -0.5)
                pool.memset(c.ident[:], 0.0).then_inc(ident_clear, 1)
                pool.wait_ge(ident_clear, 1)
                pool.affine_select(out=c.ident[:], in_=c.ident[:], compare_op=ALU.not_equal, fill=1.0,
                                   base=0, pattern=[[-1, P]], channel_multiplier=1)
                gru_rstd(c, pool, 0)

            @block.scalar
            def _(act):
                load_x(act, 0, x_first)
                act.wait_ge(mod_loaded, 64)
                act.activation(sT[:], cT[:], ACT.Silu).then_inc(silu_ready, 1)
                lambda_on_act(c, act)

            @block.tensor
            def _(pe):
                pe.wait_ge(mod_loaded, 64)
                pe.wait_ge(silu_ready, 1)
                for n, (l, j) in enumerate(COL_PARTS):
                    for m in range(KD):
                        for k in range(KD):
                            at = (j * KD + m) * P
                            last = pe.matmul(colp[:, n, m, :], wmod[l][:, k, at:at + P], sT[:, l, k, :],
                                             start=(k == 0), stop=(k == KD - 1))
                last.then_inc(colp_ready, 1)
                for n in range(4):
                    for q in range(2):
                        l, src = (0, (2, 5)[q]) if n == 0 else (1, 2 * (n - 1) + q)
                        for k in range(KD):
                            last = pe.matmul(rowp[0:B, n, q * DM:(q + 1) * DM], sT[:, l, k, :],
                                             wmod[l][:, k, src * DM:(src + 1) * DM], start=(k == 0), stop=(k == KD - 1))
                    last.then_inc(rowp_ready, 1)

            def clamp_gate(dve, order, gate):
                order.then(dve.tensor_scalar(mag[:], gate, -1.0, None, ALU.mult))
                order.did(dve.scalar_tensor_tensor(mag[:], gate, 0.25, mag[:], ALU.max, ALU.max))
                order.then(dve.tensor_scalar(sgn[:], gate, 0.0, 2.0, ALU.is_ge, ALU.mult))
                order.then(dve.scalar_tensor_tensor(gate, sgn[:], 1.0, mag[:], ALU.subtract, ALU.mult)
                           )

            @block.vector
            def _(dve):
                order = Steps(dve, dve_order)
                dve.wait_ge(x_first, 16 * HALVES)
                gru_stats(c, dve, order, 0)
                gru_normalize(c, dve, 0)
                dve.wait_ge(mod_loaded, 64)
                for q, name in enumerate(("bz_f", "bz_b")):
                    dve.tensor_scalar(c.nbz[:, q, :], c.cols[:, COL[name]:COL[name] + KD], -1.0, None, ALU.mult)
                dve.wait_ge(colp_ready, 1)
                for n, (l, j) in enumerate(COL_PARTS):
                    dve.tensor_scalar(c.modT[l][:, j * KD:(j + 1) * KD, :], colp[:, n], float(j in (1, 4)), None, ALU.add)
                for n in range(4):
                    dve.wait_ge(rowp_ready, n + 1)
                    order.then(dve.tensor_copy(rows[:, 2 * n:2 * n + 2, :],
                                               rowp[0:B, n, :].rearrange("p (q n) -> p q n", q=2)))
                    if n == 0:
                        clamp_gate(dve, order, rows[:, 0:2, :])
                for j in (3, 6):
                    dve.tensor_scalar(rows[:, j, :], rows[:, j, :], 1.0, None, ALU.add).then_inc(rows_ready, 1)
                clamp_gate(dve, order, rows[:, 4:8:3, :])
                dve.wait_ge(dve_order, order.n)
                dve.sem_inc(rows_ready, 1)
                lambda_on_dve(c, dve)


def gru(c):
    nc, d = c.nc, c.d
    c.phase = "gru_"
    with ExitStack() as own:
        wg, wo, xhat = c.wg, c.wo, c.gru_xhat
        wo_b = c.sb("wo_b", [P, 5, DM], ctx=own)
        hT = c.sb("hT", [P, KD, S], ctx=own)
        Z = c.sb("Z", [P, 2, S], ctx=own)
        A = c.sb("A", [P, 2, S], ctx=own)
        SG = c.sb("SG", [P, 2, S], ctx=own)
        R = c.sb("R", [P, 2, S], ctx=own)
        H = c.sb("H", [P, 4, S], ctx=own)
        tp = c.ps("tp", [P, 2, 512], ctx=own)
        gp = c.ps("gp", [P, 4, 512], ctx=own)
        op = c.ps("op", [P, 2, 2, DM], ctx=own)
        tp_ready, hT_ready = c.sem("gru_tp_ready"), c.sem("gru_hT_ready")
        gp_ready, gates_ready = c.sem("gru_gp_ready"), c.sem("gru_gates_ready")
        scan_ready, wo_ready = c.sem("gru_scan_ready"), c.sem("gru_wo_ready")
        op_ready, op_free = c.sem("gru_op_ready"), c.sem("gru_op_free")
        dve_order, bias_added = c.sem("gru_dve_order"), c.sem("gru_bias_added")

        def batch_rows(eng, do_row):
            with eng.Fori(0, B - 1) as b:
                do_row(b, True)
            do_row(B - 1, False)

        with nc.Block() as block:

            @block.gpsimd
            def _(pool):
                pool.wait_ge(c.gru_w_loaded, 48)
                pool.wait_ge(c.rows_loaded, 32)

                def do_row(b, more):
                    if more:
                        gru_rstd(c, pool, b + 1)
                    pool.wait_ge(op_free, b * 4 + 2)
                    ga = c.rows0[:, bass.ds(b, 1), 0, :]
                    pool.tensor_tensor(wo_b[:], wo[:], ga.broadcast_to([P, 5, DM]), ALU.mult).then_inc(wo_ready, 1)
                    c.hold(pool, wo_ready, b + 1)
                    c.hold(pool, c.gru_xhat_ready, b * 2 + 2)
                    for h in range(HALVES):
                        xs = c.X[:, bass.ds(b * TJ + h * TH, TJ), :]
                        pool.tensor_tensor(xs, xs, wo_b[:, 4:5, :].broadcast_to([P, TJ, DM]), ALU.add
                                           ).then_inc(bias_added, 1)

                batch_rows(pool, do_row)

            @block.scalar
            def _(act):

                def by_feature(b):
                    for n in range(4):
                        k, q = n // 2, n % 2
                        c.hold(act, tp_ready, b * 4 + n + 1)
                        act.activation(hT[:, k, q * 512:(q + 1) * 512], tp[:, n % 2, :], ACT.Identity,
                                       bias=c.modT[0][:, 0 * KD + k, bass.ds(b, 1)],
                                       scale=c.modT[0][:, 1 * KD + k, bass.ds(b, 1)]).then_inc(hT_ready, 1)

                def do_row(b, more):
                    for u in range(4):
                        dr, m, s = u // 2, u % 2, u % 2
                        bz, bh = COL[("bz_f", "bz_b")[dr]] + m, COL[("bh_f", "bh_b")[dr]] + m
                        act.wait_ge(scan_ready, b * 4 + u + 1)
                        for n in range(2):
                            cs = slice(n * 512, (n + 1) * 512)
                            act.wait_ge(gp_ready, b * 16 + u * 4 + n * 2 + 1)
                            act.activation(Z[:, s, cs], gp[:, 2 * n, :], ACT.Sigmoid, bias=c.cols[:, bz:bz + 1])
                            act.activation(A[:, s, cs], gp[:, 2 * n, :], ACT.Sigmoid, bias=c.nbz[:, dr, m:m + 1],
                                           scale=-1.0).then_inc(gates_ready, 1)
                            act.wait_ge(gp_ready, b * 16 + u * 4 + n * 2 + 2)
                            act.activation(SG[:, s, cs], gp[:, 2 * n + 1, :], ACT.Sigmoid, bias=c.cols[:, bh:bh + 1])
                            act.activation(R[:, s, cs], gp[:, 2 * n + 1, :], ACT.Relu, bias=c.cols[:, bh:bh + 1]
                                           ).then_inc(gates_ready, 1)
                    if more:
                        by_feature(b + 1)

                act.sem_inc(gates_ready, 4)
                by_feature(0)
                batch_rows(act, do_row)

            @block.tensor
            def _(pe):

                def turn(b, half):
                    for n in (2 * half, 2 * half + 1):
                        k, q = n // 2, n % 2
                        if half == 0:
                            pe.wait_ge(c.gru_xhat_ready, b * 2 + q + 1)
                        else:
                            pe.wait_ge(hT_ready, b * 4 + n - 1)
                        for t in range(4):
                            last = pe.transpose(tp[:, n % 2, t * P:(t + 1) * P],
                                                xhat[:, 4 * q + t, k * P:(k + 1) * P], c.ident[:])
                        last.then_inc(tp_ready, 1)

                def do_row(b, more):
                    pe.wait_ge(hT_ready, b * 4 + 4)
                    for u in range(4):
                        dr, m = u // 2, u % 2
                        for n in range(2):
                            for w in range(2):
                                pe.wait_ge(gates_ready, b * 16 + u * 4 + n * 2 + w + 1)
                                for k in range(KD):
                                    last = pe.matmul(gp[:, 2 * n + w, :], wg[:, 2 * dr + w, k, m * P:(m + 1) * P],
                                                     hT[:, k, n * 512:(n + 1) * 512], start=(k == 0), stop=(k == KD - 1))
                                last.then_inc(gp_ready, 1)
                    if more:
                        turn(b + 1, 0)
                    pe.wait_ge(scan_ready, b * 4 + 6)
                    pe.wait_ge(wo_ready, b + 1)
                    for n in range(4):
                        if more and n == 2:
                            turn(b + 1, 1)
                        pe.wait_ge(op_free, b * 4 + n + 1)
                        for q in range(2):
                            t = 2 * n + q
                            for k in range(4):
                                last = pe.matmul(op[:, n % 2, q, :], H[:, k, t * P:(t + 1) * P], wo_b[:, k, :],
                                                 start=(k == 0), stop=(k == 3))
                        last.then_inc(op_ready, 1)

                pe.wait_ge(c.gru_w_loaded, 48)
                turn(0, 0)
                turn(0, 1)
                batch_rows(pe, do_row)

            @block.vector
            def _(dve):
                dve.sem_inc(scan_ready, 2)
                dve.sem_inc(op_free, 2)
                dve.wait_ge(c.x_loaded, 16 * (B - 1) * HALVES)

                def do_row(b, more):
                    order = Steps(dve, dve_order, b * 16)
                    for u in range(4):
                        s = u % 2
                        dve.wait_ge(gates_ready, 4 + b * 16 + u * 4 + 4)
                        order.then(dve.scalar_tensor_tensor(SG[:, s, :], SG[:, s, :], 0.5, R[:, s, :], ALU.min, ALU.add))
                        order.then(dve.tensor_tensor(SG[:, s, :], SG[:, s, :], Z[:, s, :], ALU.mult))
                        a, v = A[:, s, :], SG[:, s, :]
                        if u >= 2:
                            a, v = a[:, ::-1], v[:, ::-1]
                        dve.tensor_tensor_scan(H[:, u, :], a, v, 0.0, ALU.mult, ALU.add).then_inc(scan_ready, 1)
                        if more and u == 0:
                            gru_stats(c, dve, order, b + 1)
                        if more and u == 1:
                            dve.wait_ge(tp_ready, b * 4 + 4)
                            gru_normalize(c, dve, b + 1)
                    dve.wait_ge(bias_added, b * 2 + 2)
                    for n in range(4):
                        dve.wait_ge(op_ready, b * 4 + n + 1)
                        xs = c.X[:, bass.ds(b * TJ + (2 * n // TJ * TH + 2 * n % TJ), 2), :]
                        dve.tensor_tensor(xs, op[:, n % 2], xs, ALU.add).then_inc(op_free, 1)

                batch_rows(dve, do_row)


def ffn(c):
    nc, d = c.nc, c.d
    c.phase = "ffn_"
    CH = TJ * P // 2
    with ExitStack() as own:
        w = c.w_ffn
        bo = c.sb("bo_row", [1, DM], ctx=own)
        stats = c.sb("stats", [P, TJ, 6], ctx=own)
        mv = c.sb("mv", [P, TJ, 2], ctx=own)
        ve = c.sb("ve", [P, TJ], ctx=own)
        rs = c.sb("rs", [P, TJ], ctx=own)
        xhat = c.sb("xhat", [P, TJ, DM], ctx=own)
        hT = c.sb("hT", [P, B, KD, TJ * P], ctx=own)
        cT = c.sb("cT_state", [P, KD, TJ * P], ctx=own)
        G = c.sb("G", [P, 2, 3, KD, CH], ctx=own)
        Y = c.sb("Y", [P, 2, 2, DM], ctx=own)
        tp = c.ps("tp", [P, KD, 512], ctx=own)
        gp = c.ps("gp", [P, 6, 512], ctx=own)
        w_loaded, stats_ready = c.ffn_w_loaded, c.sem("ffn_stats_ready")
        rstd_ready, xhat_ready = c.sem("ffn_rstd_ready"), c.sem("ffn_xhat_ready")
        tp_ready, hT_ready = c.sem("ffn_tp_ready"), c.sem("ffn_hT_ready")
        gp_ready, gates_ready, c_ready = c.sem("ffn_gp_ready"), c.sem("ffn_gates_ready"), c.sem("ffn_c_ready")
        y_ready, tanh_ready = c.sem("ffn_y_ready"), c.sem("ffn_tanh_ready")
        scaled_ready, y_free = c.sem("ffn_scaled_ready"), c.sem("ffn_y_free")
        dve_order, pool_order = c.sem("ffn_dve_order"), c.sem("ffn_pool_order")

        with nc.Block() as block:

            @block.sync
            def _(sp):
                sp.dma_start(bo[:], d["rows"][ROW["bo_ffn"]:ROW["bo_ffn"] + 1, :]).then_inc(w_loaded, 16)

            @block.gpsimd
            def _(pool):

                def rstd(it):
                    c.hold(pool, stats_ready, it + 1)
                    pool.tensor_scalar(ve[:], mv[:, :, 1], EPS, None, ALU.add).then_inc(pool_order, 1)
                    pool.wait_ge(pool_order, it + 1)
                    pool.tensor_tensor(rs[:], ve[:], c.mhalf[:, 0:TJ], ALU.pow).then_inc(rstd_ready, 1)

                with pool.Fori(0, HALVES) as h:
                    rstd(h * B)
                    with pool.Fori(0, B - 1) as b:
                        rstd(h * B + b + 1)
                    for n in range(8):
                        pool.wait_ge(tanh_ready, h * 8 + n + 1)
                        pool.tensor_tensor(Y[:, n % 2], Y[:, n % 2],
                                           c.rows0[:, n // 2, 1:2, :].broadcast_to([P, 2, DM]),
                                           ALU.mult).then_inc(scaled_ready, 1)

            @block.scalar
            def _(act):

                def evacuate(it, b):
                    for k in range(KD):
                        c.hold(act, tp_ready, it * 2 + k + 2)
                        act.activation(hT[:, b, k, :], tp[:, k, :], ACT.Identity,
                                       bias=c.modT[0][:, 3 * KD + k, bass.ds(b, 1)],
                                       scale=c.modT[0][:, 4 * KD + k, bass.ds(b, 1)]).then_inc(hT_ready, 1)

                def gates(it, ch):
                    for g, (name, f) in enumerate((("bf", ACT.Sigmoid), ("bi", ACT.Sigmoid), ("bc", ACT.Tanh))):
                        act.wait_ge(gp_ready, it * 6 + ch * 3 + g + 1)
                        for m in range(KD):
                            col = COL[name] + m
                            last = act.activation(G[:, ch, g, m, :], gp[:, ch * 3 + g, m * CH:(m + 1) * CH], f,
                                                  bias=c.cols[:, col:col + 1])
                    last.then_inc(gates_ready, 1)

                with act.Fori(0, HALVES) as h:
                    evacuate(h * B, 0)
                    with act.Fori(0, B - 1) as b:
                        gates(h * B + b, 0)
                        evacuate(h * B + b + 1, b + 1)
                        gates(h * B + b, 1)
                    gates(h * B + B - 1, 0)
                    gates(h * B + B - 1, 1)
                    for n in range(8):
                        act.wait_ge(y_ready, h * 8 + n + 1)
                        act.wait_ge(y_free, h * 8 + n + 1)
                        act.activation(Y[:, n % 2], gp[:, n % 6, :].rearrange("p (q n) -> p q n", q=2),
                                       ACT.Tanh).then_inc(tanh_ready, 1)

            @block.tensor
            def _(pe):

                def transposes(it):
                    pe.wait_ge(xhat_ready, it + 1)
                    for k in range(KD):
                        for t in range(TJ):
                            last = pe.transpose(tp[:, k, t * P:(t + 1) * P], xhat[:, t, k * P:(k + 1) * P], c.ident[:])
                        last.then_inc(tp_ready, 1)

                def gates(h, b, ch):
                    pe.wait_ge(hT_ready, h * 2 * B + b * 2 + 2)
                    pe.wait_ge(c_ready, h * 10 + b * 2 + ch + 1)
                    for g in range(3):
                        for m in range(KD):
                            out = gp[:, ch * 3 + g, m * CH:(m + 1) * CH]
                            for k in range(KD):
                                pe.matmul(out, w[:, 2 * g, k, m * P:(m + 1) * P], hT[:, b, k, ch * CH:(ch + 1) * CH],
                                          start=(k == 0), stop=False)
                            for k in range(KD):
                                last = pe.matmul(out, w[:, 2 * g + 1, k, m * P:(m + 1) * P],
                                                 cT[:, k, ch * CH:(ch + 1) * CH], start=False, stop=(k == KD - 1))
                        last.then_inc(gp_ready, 1)

                pe.sem_inc(tp_ready, 1)
                pe.wait_ge(w_loaded, 32)
                with pe.Fori(0, HALVES) as h:
                    transposes(h * B)
                    with pe.Fori(0, B - 1) as b:
                        gates(h, b, 0)
                        transposes(h * B + b + 1)
                        gates(h, b, 1)
                    gates(h, B - 1, 0)
                    gates(h, B - 1, 1)
                    pe.wait_ge(c_ready, h * 10 + 10)
                    for n in range(8):
                        if n >= 6:
                            pe.wait_ge(tanh_ready, h * 8 + n - 5)
                        for q in range(2):
                            out = gp[:, n % 6, q * DM:(q + 1) * DM]
                            b, t = n // 2, 2 * (n % 2) + q
                            for k in range(KD):
                                pe.matmul(out, hT[:, b, k, t * P:(t + 1) * P], w[:, 6, k, :],
                                          start=(k == 0), stop=False)
                            for k in range(KD):
                                pe.matmul(out, cT[:, k, t * P:(t + 1) * P], w[:, 7, k, :], start=False, stop=False)
                            last = pe.matmul(out, c.ones[:], bo[:], start=False, stop=True)
                        last.then_inc(y_ready, 1)

            @block.vector
            def _(dve):

                def layernorm(it):
                    for t in range(TJ):
                        dve.bn_stats(stats[:, t, :], c.X[:, it * TJ + t, :]).then_inc(dve_order, 1)
                    c.hold(dve, dve_order, it * TJ + TJ)
                    for t in range(TJ):
                        last = dve.bn_aggr(mv[:, t, :], stats[:, t, :])
                    last.then_inc(stats_ready, 1)
                    dve.wait_ge(rstd_ready, it + 1)
                    dve.wait_ge(tp_ready, it * 2 + 1)
                    for t in range(TJ):
                        last = dve.tensor_scalar(xhat[:, t, :], c.X[:, it * TJ + t, :], mv[:, t, 0:1],
                                                 rs[:, t:t + 1], ALU.subtract, ALU.mult)
                    last.then_inc(xhat_ready, 1)

                def update(h, b, ch):
                    state = cT[:, :, ch * CH:(ch + 1) * CH]
                    dve.wait_ge(gates_ready, h * 2 * B + b * 2 + ch + 1)
                    dve.tensor_tensor(G[:, ch, 2], G[:, ch, 1], G[:, ch, 2], ALU.mult)
                    dve.tensor_tensor(state, G[:, ch, 0], state, ALU.mult).then_inc(c.updated, 1)
                    dve.wait_ge(c.updated, h * 2 * B + b * 2 + ch + 1)
                    dve.tensor_tensor(state, state, G[:, ch, 2], ALU.add).then_inc(c_ready, 1)

                dve.sem_inc(y_free, 2)
                with dve.Fori(0, HALVES) as h:
                    for ch in range(2):
                        dve.tensor_copy(cT[:, :, ch * CH:(ch + 1) * CH],
                                        c.cols[:, COL["in_c"]:COL["in_c"] + KD].unsqueeze(2).broadcast_to([P, KD, CH])
                                        ).then_inc(c_ready, 1)
                    layernorm(h * B)
                    with dve.Fori(0, B - 1) as b:
                        layernorm(h * B + b + 1)
                        update(h, b, 0)
                        update(h, b, 1)
                    update(h, B - 1, 0)
                    update(h, B - 1, 1)
                    for n in range(8):
                        xs = c.X[:, bass.ds(h * TH + 2 * n, 2), :]
                        dve.wait_ge(scaled_ready, h * 8 + n + 1)
                        dve.tensor_tensor(xs, xs, Y[:, n % 2], ALU.add).then_inc(y_free, 1)


H_, D_, DV = 16, 8, 16
NH = 2 * H_
GB = 16
G8 = P // GB


def attention_constants(c):
    c.w_qk = c.sb("w_qk", [P, KD, 2 * DM], ctx=c.layer1)
    c.w_v = c.sb("w_v", [P, KD, DM], ctx=c.layer1)
    c.w_o = c.sb("w_o", [P, KD, DM], ctx=c.layer1)
    c.bo1 = c.sb("bo1", [P, DM], ctx=c.layer1)
    c.maskK = c.sb("maskK", [P, 4], ctx=c.layer1)
    c.maskV = c.sb("maskV", [P, G8], ctx=c.layer1)
    c.combine = c.sb("combine", [P, 2, 64], ctx=c.layer1)
    c.lam_in = c.sb("lam_in", [P, 2, 2, D_], ctx=c.layer1)
    c.lam = c.sb("lam", [P, 4], ctx=c.layer1)
    c.at_loaded, c.lam_order, c.lam_exp = c.sem("at_loaded"), c.sem("lam_order"), c.sem("lam_exp")
    c.credit = {n: c.sem("attn_" + n) for n in ("norm1_ready", "cp_ready")}


def load_attention_constants(c, sp):
    d = c.d
    for dst, src in ((c.w_qk, d["w_qk"].rearrange("(k p) n -> p k n", p=P)),
                     (c.w_v, d["w_v"].rearrange("(k p) n -> p k n", p=P)),
                     (c.w_o, d["w_o"].rearrange("(k p) n -> p k n", p=P)),
                     (c.bo1, d["rows"][ROW["bo_attn"]:ROW["bo_attn"] + 1, :].broadcast_to([P, DM])),
                     (c.maskK, d["maskK"]), (c.maskV, d["maskV"]), (c.combine, d["combine"])):
        sp.dma_start(dst[:], src).then_inc(c.at_loaded, 16)
    sp.dma_start(c.lam_in[:].rearrange("p a b n -> p (a b n)"),
                 d["lam"].rearrange("a n -> (a n)").unsqueeze(0).broadcast_to([P, 4 * D_])).then_inc(c.at_loaded, 16)


def lambda_on_act(c, act):
    act.wait_ge(c.lam_order, 2)
    act.activation(c.lam[:, 2:4], c.lam[:, 0:2], ACT.Exp).then_inc(c.lam_exp, 1)


def lambda_on_dve(c, dve):
    order = Steps(dve, c.lam_order)
    dve.sem_inc(c.credit["norm1_ready"], 2)
    dve.sem_inc(c.credit["cp_ready"], 2)
    dve.wait_ge(c.at_loaded, 16 * 8)
    order.then(dve.tensor_tensor(c.lam_in[:, 0], c.lam_in[:, 0], c.lam_in[:, 1], ALU.mult))
    order.then(dve.tensor_reduce(c.lam[:, 0:2], c.lam_in[:, 0], AX.X, ALU.add))
    dve.wait_ge(c.lam_exp, 1)
    order.then(dve.scalar_tensor_tensor(c.lam[:, 0:1], c.lam[:, 3:4], LAMBDA_INIT, c.lam[:, 2:3],
                                        ALU.subtract, ALU.subtract))
    dve.tensor_scalar(c.combine[:, 1, :], c.combine[:, 1, :], c.lam[:, 0:1], None, ALU.mult)


def attention(c, h, own):
    nc = c.nc
    c.phase = "at_"
    AREA = TH * DM
    area0 = c.sb("area0", [P, AREA], ctx=own)
    area1 = c.sb("area1", [P, 2 * AREA], ctx=own)
    area2 = c.sb("area2", [P, 2 * AREA], ctx=own)
    tok = area0[:].rearrange("p (k t r g) -> p k t r g", k=KD, t=TJ, r=B)
    OT = area0[:].rearrange("p (a r g j) -> p a r g j", a=H_, r=4, g=GB)
    QK = area1[:].rearrange("p (n t d) -> p n t d", n=2 * NH, t=TH)
    VS = area1[:, 0:AREA].rearrange("p (u G n) -> p u G n", u=2, G=G8)
    VT = area1[:, AREA:].rearrange("p (g t d) -> p g t d", g=GB, t=TH)
    PN = area1[:, 0:AREA // 2].rearrange("p (s k n a) -> p s k n a", s=2, k=2, a=H_)
    attT = area1[:, AREA // 2:AREA * 3 // 4].rearrange("p (s t a) -> p s t a", s=2, t=TH)
    O = area1[:, AREA * 3 // 4:AREA].rearrange("p (s n) -> p s n", s=2)
    OK = area1[:, 0:AREA].rearrange("p (u G a d) -> p u G a d", u=2, G=G8, a=H_)
    QT = area2[:, 0:AREA].rearrange("p (g n) -> p g n", n=NH)
    KT = area2[:, AREA:].rearrange("p (g n) -> p g n", n=NH)
    oT = area2[:, 0:AREA].rearrange("p (k t r n g) -> p k t r n g", k=KD, t=4, r=4, g=2)
    SQ = area2[:, AREA:].rearrange("p (u n) -> p u n", u=2)

    stats = c.sb("stats", [P, 2, TJ, 6], ctx=own)
    mv = c.sb("mv", [P, 2, TJ, 2], ctx=own)
    ve = c.sb("ve", [P, 2, TJ], ctx=own)
    rs = c.sb("rs", [P, 2, TJ], ctx=own)
    xhat = area2[:, 0:TJ * DM].rearrange("p (t n) -> p t n", t=TJ)
    Kbd = c.sb("Kbd", [P, 2, G8, P], ctx=own)
    Qs = c.sb("Qs", [P, 2, G8, NH], ctx=own)
    Vbd = c.sb("Vbd", [P, 2, TH, P], ctx=own)
    T = c.sb("T", [P, 2, 4 * G8, NH], ctx=own)
    mx = c.sb("mx", [P, 2, 4 * G8], ctx=own)
    Z = c.sb("Z", [P, 2, 2, 4 * G8], ctx=own)
    ss = c.sb("ss", [P, 2, P], ctx=own)
    rr = c.sb("rr", [P, 2, P], ctx=own)
    work = c.ps("work", [P, 6, 512], ctx=own)
    tp = c.ps("tp", [P, KD, 512], ctx=own)
    SC = work[:, 0:4, 0:G8 * NH]
    CP = [work[:, 4, 0:4 * 64], tp[:, 0, 0:4 * 64]]
    PV = [work[:, 5], tp[:, 1]]

    QK0, HD0, V0, VT0, O0, F0, P0, JOBS = 0, 16, 32, 40, 48, 56, 64, 72
    by_act = [n < HD0 or (n % 2 == 0 and n < P0) for n in range(JOBS)]
    ACTS, DVES = sum(by_act), JOBS - sum(by_act)

    def emptied(n):
        return sum(1 for m in range(n + 1) if by_act[m] == by_act[n])

    sem = lambda n: c.sem("attn_" + n)
    stats_ready, rstd_ready = sem("stats_ready"), sem("rstd_ready")
    xn_ready, h1_ready, xhat_ready = sem("xn_ready"), sem("h1_ready"), sem("xhat_ready")
    xa_order, bias_added = sem("xa_order"), sem("bias_added")
    tp_ready, hT_ready = sem("tp_ready"), sem("hT_ready")
    full, empty_a, empty_d = sem("bank_full"), sem("bank_empty_act"), sem("bank_empty_dve")
    kbd_ready, q_ready, vbd_ready = sem("kbd_ready"), sem("q_ready"), sem("vbd_ready")
    s_ready, s_free, t_ready, e_ready, rz_ready = sem("s_ready"), sem("s_free"), sem("t_ready"), sem("e_ready"), sem("rz_ready")
    norm0_ready, norm1_ready, cp_ready = sem("norm0_ready"), c.credit["norm1_ready"], c.credit["cp_ready"]
    att_ready, pv_ready, o_ready = sem("att_ready"), sem("pv_ready"), sem("o_ready")
    padded, o_copied, o_turned = sem("padded"), sem("o_copied"), sem("o_turned")
    sq_ready, ss_ready, rr_ready, ok_ready = sem("sq_ready"), sem("ss_ready"), sem("rr_ready"), sem("ok_ready")
    dve_order, pool_order, tail_order = sem("dve_order"), sem("pool_order"), sem("tail_order")

    def emptied_by(n, hh):
        return (empty_a, hh * ACTS + emptied(n)) if by_act[n] else (empty_d, hh * DVES + emptied(n))

    def emptied_wait(eng, n, hh):
        eng.wait_ge(*emptied_by(n, hh))

    def rounds(eng, do_round):
        with eng.Fori(0, GB // 2 - 1) as i2:
            for s in range(2):
                do_round(i2 * 2 + s, s, True)
        for s in range(2):
            do_round(GB - 2 + s, s, False)

    LN = [(0, 0), (1, 0), (0, 1), (1, 1), (0, 2), (1, 2), (0, 3), (1, 3)]

    with nc.Block() as block:

        def empty(n, copy):
            bank = work[:, n % 6, :]
            if n < V0:
                q, j = ((QT, n - HD0) if n < HD0 + 8 else (KT, n - HD0 - 8))
                return copy(q[:, :, 4 * j:4 * j + 4].rearrange("p g n -> p n g"),
                            bank.rearrange("p (n g) -> p n g", n=4))
            if n < VT0:
                u, G = (n - V0) // 4, 2 * ((n - V0) % 4)
                return copy(VS[:, u, G:G + 2, :], bank.rearrange("p (G n) -> p G n", G=2))
            if n < O0:
                u, d0 = (n - VT0) // 4, 4 * ((n - VT0) % 4)
                v = bank.rearrange("p (d r g j) -> p d r g j", d=4, r=2, g=GB)
                for r in range(2):
                    at = 8 * u + 4 * r
                    last = copy(VT[:, :, at:at + 4, d0:d0 + 4].rearrange("p g j d -> p d g j"), v[:, :, r])
                return last
            if n < F0:
                u, a = (n - O0) // 4, 4 * ((n - O0) % 4)
                return copy(OK[:, u, :, a:a + 4, :].rearrange("p G a d -> p a G d"),
                            bank.rearrange("p (a G d) -> p a G d", a=4, G=G8))
            u, k, g2 = (n - F0) // 4, (n - F0) // 2 % 2, (n - F0) % 2
            return copy(oT[:, k, :, 2 * u:2 * u + 2, :, g2], bank.rearrange("p (t r n) -> p t r n", t=4, r=2))

        @block.gpsimd
        def _(pool):
            order = Steps(pool, pool_order, h * 8)

            def rstd(n):
                kind, b = LN[n]
                c.hold(pool, stats_ready, h * 8 + n + 1)
                order.then(pool.tensor_scalar(ve[:, kind], mv[:, kind, :, 1], EPS, None, ALU.add))
                pool.tensor_tensor(rs[:, kind], ve[:, kind], c.mhalf[:, 0:TJ], ALU.pow).then_inc(rstd_ready, 1)

            for n in range(8):
                rstd(n)

            for b in range(B):
                part = c.H1[:, b * TJ:(b + 1) * TJ, :]
                pool.wait_ge(xhat_ready, h * B + b + 1)
                pool.tensor_tensor(part, part, c.bo1[:].unsqueeze(1).broadcast_to([P, TJ, DM]),
                                   ALU.add).then_inc(bias_added, 1)

            def spread_v(i, s):
                pool.tensor_tensor(Vbd[:, s].rearrange("p t (G d) -> p t G d", d=DV),
                                   VT[:, bass.ds(i, 1), :, :].rearrange("p g t d -> p (g t) d").unsqueeze(2).broadcast_to([P, TH, G8, DV]),
                                   c.maskV[:].unsqueeze(1).unsqueeze(3).broadcast_to([P, TH, G8, DV]),
                                   ALU.mult).then_inc(vbd_ready, 1)

            emptied_wait(pool, O0 - 2, h)
            c.hold(pool, *emptied_by(O0 - 1, h))
            pool.memset(attT, 0.0).then_inc(padded, 1)
            for i in range(2):
                spread_v(i, i)

            def normalize(i, s):
                pool.wait_ge(rz_ready, h * GB + i + 1)
                pool.wait_ge(cp_ready, h * GB + i + 1)
                pool.tensor_tensor(PN[:, s, 1], T[:, s, :, H_:NH],
                                   Z[:, s, 1, :].unsqueeze(2).broadcast_to([P, 4 * G8, H_]),
                                   ALU.mult).then_inc(norm1_ready, 1)

            def do_round(i, s, more):
                if more or s == 0:
                    normalize(i + 1, 1 - s)
                if more:
                    pool.wait_ge(pv_ready, h * GB + i + 1)
                    spread_v(i + 2, s)

            normalize(0, 0)
            rounds(pool, do_round)

        @block.scalar
        def _(act):

            def to_hT(b):
                for k in range(KD):
                    act.wait_ge(tp_ready, h * 2 * B + 2 * b + k + 1)
                    g, o = COL["ln1_g"] + k, COL["ln1_b"] + k
                    act.activation(tok[:, k, :, b, :], tp[:, k, :].rearrange("p (t g) -> p t g", t=TJ), ACT.Identity,
                                   bias=c.cols[:, o:o + 1], scale=c.cols[:, g:g + 1]).then_inc(hT_ready, 1)

            def copy(out, in_):
                return act.copy(out, in_)

            for b in range(B):
                to_hT(b)
                for t in range(TJ):
                    n = QK0 + b * TJ + t
                    act.wait_ge(full, h * JOBS + n + 1)
                    copy(QK[:, :, n, :], work[:, n % 6, :].rearrange("p (n d) -> p n d", d=D_)).then_inc(empty_a, 1)
            for n in range(HD0, O0):
                if by_act[n]:
                    act.wait_ge(full, h * JOBS + n + 1)
                    empty(n, copy).then_inc(empty_a, 1)

            def take_q(i, s):
                c.hold(act, empty_d, h * DVES + emptied(V0 - 1))
                copy(Qs[:, s], QT[:, bass.ds(i * G8, G8), :]).then_inc(q_ready, 1)

            for i in range(2):
                take_q(i, i)

            def exponent(i, s):
                act.wait_ge(t_ready, h * GB + i + 1)
                act.activation(T[:, s], T[:, s], ACT.Exp).then_inc(e_ready, 1)

            def take_att(i, s):
                act.wait_ge(cp_ready, h * GB + i + 3)
                copy(attT[:, s, :, 0:H_], CP[s].rearrange("p (t a) -> p t a", a=H_)).then_inc(att_ready, 1)

            def do_round(i, s, more):
                if more:
                    c.hold(act, s_ready, h * GB + i + 1)
                    take_q(i + 2, s)
                if more or s == 0:
                    exponent(i + 1, 1 - s)
                act.wait_ge(pv_ready, h * GB + i + 1)
                copy(O[:, s], PV[s]).then_inc(o_copied, 1)
                if more or s == 0:
                    take_att(i + 1, 1 - s)
                c.hold(act, o_turned, h * GB + i + 1)
                copy(OT[:, :, :, bass.ds(i, 1), :].rearrange("p a r g j -> p (r g) j a"),
                     PV[s].rearrange("p (r j a) -> p r j a", r=4, j=4)[:, :, :, 0:H_]).then_inc(o_ready, 1)

            exponent(0, 0)
            act.wait_ge(padded, h + 1)
            take_att(0, 0)
            rounds(act, do_round)
            for u in range(2):
                for n in range(O0 + 4 * u, O0 + 4 * u + 4):
                    if by_act[n]:
                        act.wait_ge(full, h * JOBS + n + 1)
                        empty(n, copy).then_inc(empty_a, 1)
                emptied_wait(act, O0 + 4 * u + 2, h)
                emptied_wait(act, O0 + 4 * u + 3, h)
                act.activation(SQ[:, u], OK[:, u].rearrange("p G a d -> p (G a d)"), ACT.Square).then_inc(sq_ready, 1)
                act.wait_ge(ss_ready, h * 2 + u + 1)
                act.activation(rr[:, u], ss[:, u], ACT.Sqrt).then_inc(rr_ready, 1)
            for n in range(F0, P0):
                if by_act[n]:
                    act.wait_ge(full, h * JOBS + n + 1)
                    empty(n, copy).then_inc(empty_a, 1)

        @block.tensor
        def _(pe):

            def bank_free(n):
                if n >= 6:
                    emptied_wait(pe, n - 6, h)

            for b in range(B):
                pe.wait_ge(xhat_ready, h * B + b + 1)
                if b:
                    pe.wait_ge(hT_ready, h * 2 * B + 2 * b)
                for k in range(KD):
                    for t in range(TJ):
                        last = pe.transpose(tp[:, k, t * P:(t + 1) * P], xhat[:, t, k * P:(k + 1) * P], c.ident[:])
                    last.then_inc(tp_ready, 1)
                pe.wait_ge(hT_ready, h * 2 * B + 2 * b + 2)
                for t in range(TJ):
                    n = QK0 + b * TJ + t
                    bank_free(n)
                    for k in range(KD):
                        last = pe.matmul(work[:, n % 6, :], tok[:, k, t, b, :], c.w_qk[:, k, :],
                                         start=(k == 0), stop=(k == KD - 1))
                    last.then_inc(full, 1)
            emptied_wait(pe, HD0 - 1, h)
            for n in range(HD0, V0):
                bank_free(n)
                for q in range(4):
                    hd = 4 * (n - HD0) + q
                    last = pe.transpose(work[:, n % 6, q * P:(q + 1) * P], QK[:, hd].rearrange("p t d -> p (t d)"), c.ident[:])
                last.then_inc(full, 1)
            eight = tok.rearrange("p k t (u r) (n g) -> p k t u (r n) g", u=2, g=2)
            for n in range(V0, VT0):
                u, G = (n - V0) // 4, 2 * ((n - V0) % 4)
                bank_free(n)
                for q in range(2):
                    for k in range(KD):
                        last = pe.matmul(work[:, n % 6, q * DM:(q + 1) * DM], eight[:, k, (G + q) % 4, u, :, (G + q) // 4],
                                         c.w_v[:, k, :], start=(k == 0), stop=(k == KD - 1))
                last.then_inc(full, 1)
            for n in range(VT0, O0):
                u, d0 = (n - VT0) // 4, 4 * ((n - VT0) % 4)
                if n in (VT0, VT0 + 4):
                    emptied_wait(pe, V0 + 4 * u + 2, h)
                    emptied_wait(pe, V0 + 4 * u + 3, h)
                bank_free(n)
                v = VS[:, u].rearrange("p G (n d) -> p (G n) d", d=DV)
                for q in range(4):
                    last = pe.transpose(work[:, n % 6, q * P:(q + 1) * P], v[:, :, d0 + q], c.ident[:])
                last.then_inc(full, 1)
            emptied_wait(pe, O0 - 2, h)
            emptied_wait(pe, O0 - 1, h)

            def scores(i, s):
                pe.wait_ge(kbd_ready, h * GB + i + 1)
                c.hold(pe, q_ready, h * GB + i + 1)
                for g in range(G8):
                    for q in range(4):
                        rows = slice(32 * q, 32 * q + 32)
                        j, g2 = g // 2, g % 2
                        last = pe.matmul(SC[NH * j:NH * (j + 1), q, g2 * P:(g2 + 1) * P], Qs[rows, s, g, :],
                                         Kbd[rows, s, g, :], start=True, stop=True)
                last.then_inc(s_ready, 1)

            def combine(i, s):
                pe.wait_ge(norm0_ready, h * GB + i + 1)
                pe.wait_ge(norm1_ready, h * GB + i + 3)
                for q in range(4):
                    for g2 in range(2):
                        for kind in range(2):
                            at = 4 * (2 * q + g2)
                            last = pe.matmul(CP[s][64 * g2:64 * g2 + 64, q * 64:(q + 1) * 64],
                                             PN[:, s, kind, at:at + 4, :].rearrange("p t n -> p (t n)"),
                                             c.combine[:, kind, :], start=(kind == 0), stop=(kind == 1))
                last.then_inc(cp_ready, 1)

            def do_round(i, s, more):
                pe.wait_ge(vbd_ready, h * GB + i + 1)
                pe.wait_ge(att_ready, h * GB + i + 1)
                for t in range(TH):
                    r, j = t // 4, t % 4
                    last = pe.matmul(PV[s][NH * j:NH * (j + 1), r * P:(r + 1) * P], attT[:, s, t, :], Vbd[:, s, t, :],
                                     start=True, stop=True)
                last.then_inc(pv_ready, 1)
                if more:
                    pe.wait_ge(s_free, h * GB + i + 2)
                    scores(i + 2, s)
                if more or s == 0:
                    combine(i + 1, 1 - s)
                pe.wait_ge(o_copied, h * GB + i + 1)
                for r in range(4):
                    last = pe.transpose(PV[s][:, r * P:(r + 1) * P], O[:, s, r * P:(r + 1) * P], c.ident[:])
                last.then_inc(o_turned, 1)

            scores(0, 0)
            pe.wait_ge(s_free, h * GB + 1)
            scores(1, 1)
            combine(0, 0)
            rounds(pe, do_round)
            pe.wait_ge(o_ready, h * GB + GB)
            for n in range(O0, F0):
                u, a = (n - O0) // 4, 4 * ((n - O0) % 4)
                if n >= O0 + 6:
                    bank_free(n)
                for q in range(4):
                    last = pe.transpose(work[:, n % 6, q * P:(q + 1) * P],
                                        OT[:, a + q, 2 * u:2 * u + 2].rearrange("p r g j -> p (r g j)"), c.ident[:])
                last.then_inc(full, 1)
            for n in range(F0, P0):
                u, k, G = (n - F0) // 4, (n - F0) // 2 % 2, 4 * ((n - F0) % 2)
                bank_free(n)
                pe.wait_ge(ok_ready, h * 2 + u + 1)
                for q in range(4):
                    last = pe.transpose(work[:, n % 6, q * P:(q + 1) * P],
                                        OK[:, u, G + q, 8 * k:8 * k + 8, :].rearrange("p a d -> p (a d)"), c.ident[:])
                last.then_inc(full, 1)
            for n in range(P0, JOBS):
                bank_free(n)
                if n in (P0, P0 + 4):
                    u = (n - P0) // 4
                    emptied_wait(pe, F0 + 4 * u + 2, h)
                    emptied_wait(pe, F0 + 4 * u + 3, h)
                for q in range(2):
                    t = 2 * (n - P0) + q
                    for k in range(KD):
                        o = oT[:, k, t % 4, t // 4].rearrange("p n g -> p (n g)")
                        last = pe.matmul(work[:, n % 6, q * DM:(q + 1) * DM], o, c.w_o[:, k, :],
                                         start=(k == 0), stop=(k == KD - 1))
                last.then_inc(full, 1)

        @block.vector
        def _(dve):
            order = Steps(dve, dve_order, h * (8 + 2 * GB))

            def layernorm(n):
                kind, b = LN[n]
                if kind == 1:
                    dve.wait_ge(h1_ready, h * B + b + 1)
                src = [c.X[:, h * TH + (b * TJ + t), :] if kind == 0 else c.H1[:, b * TJ + t, :] for t in range(TJ)]
                for t in range(TJ):
                    last = dve.bn_stats(stats[:, kind, t, :], src[t])
                c.hold(dve, dve_order, order.did(last))
                for t in range(TJ):
                    last = dve.bn_aggr(mv[:, kind, t, :], stats[:, kind, t, :])
                last.then_inc(stats_ready, 1)
                dve.wait_ge(rstd_ready, h * 8 + n + 1)
                if kind == 1 and b:
                    dve.wait_ge(tp_ready, h * 2 * B + 2 * b)
                for t in range(TJ):
                    dst = c.H1[:, b * TJ + t, :] if kind == 0 else xhat[:, t, :]
                    last = dve.tensor_scalar(dst, src[t], mv[:, kind, t, 0:1], rs[:, kind, t:t + 1],
                                             ALU.subtract, ALU.mult)
                last.then_inc(xn_ready if kind == 0 else xhat_ready, 1)
                if kind == 0:
                    part = c.H1[:, b * TJ:(b + 1) * TJ, :]
                    dve.wait_ge(xn_ready, h * B + b + 1)
                    dve.tensor_tensor(part, part, c.rows1[:, b, 1:2, :].broadcast_to([P, TJ, DM]), ALU.mult
                                      ).then_inc(xa_order, 1)
                    dve.wait_ge(xa_order, h * B + b + 1)
                    dve.tensor_tensor(part, part, c.rows1[:, b, 0:1, :].broadcast_to([P, TJ, DM]),
                                      ALU.add).then_inc(h1_ready, 1)

            for n in range(8):
                layernorm(n)
            for n in range(HD0, O0):
                if not by_act[n]:
                    dve.wait_ge(full, h * JOBS + n + 1)
                    empty(n, dve.tensor_copy).then_inc(empty_d, 1)

            def spread_k(i, s):
                dve.tensor_tensor(Kbd[:, s].rearrange("p g (t n) -> p g t n", t=4),
                                  KT[:, bass.ds(i * G8, G8), :].unsqueeze(2).broadcast_to([P, G8, 4, NH]),
                                  c.maskK[:].unsqueeze(1).unsqueeze(3).broadcast_to([P, G8, 4, NH]),
                                  ALU.mult).then_inc(kbd_ready, 1)

            emptied_wait(dve, V0 - 2, h)
            for i in range(2):
                spread_k(i, i)

            def do_round(i, s, more):
                flat = T[:, s].rearrange("p (r g) n -> p r (g n)", r=4)
                at = h * (8 + 2 * GB) + 8 + 2 * i
                dve.wait_ge(s_ready, h * GB + i + 1)
                dve.wait_ge(norm1_ready, h * GB + i + 1)
                dve.tensor_scalar(flat, SC, 0.0, -FMAX, ALU.min, ALU.max).then_inc(dve_order, 1)
                dve.wait_ge(dve_order, at + 1)
                dve.scalar_tensor_tensor(flat, SC, 0.0, flat, ALU.max, ALU.add).then_inc(s_free, 1)
                dve.wait_ge(s_free, h * GB + i + 1)
                dve.tensor_reduce(mx[:, s], T[:, s], AX.X, ALU.max).then_inc(dve_order, 1)
                dve.wait_ge(dve_order, at + 2)
                dve.tensor_scalar(mx[:, s], mx[:, s], FMAX, None, ALU.min).then_inc(c.clamped, 1)
                dve.wait_ge(c.clamped, h * GB + i + 1)
                dve.scalar_tensor_tensor(T[:, s], T[:, s], FMAX, mx[:, s].unsqueeze(2).broadcast_to([P, 4 * G8, NH]),
                                         ALU.min, ALU.subtract).then_inc(t_ready, 1)
                if more:
                    spread_k(i + 2, s)
                dve.wait_ge(e_ready, h * GB + i + 1)
                dve.tensor_reduce(Z[:, s, 0], T[:, s], AX.X, ALU.add).then_inc(c.summed, 1)
                dve.wait_ge(c.summed, h * GB + i + 1)
                dve.reciprocal(Z[:, s, 1], Z[:, s, 0]).then_inc(rz_ready, 1)
                dve.wait_ge(rz_ready, h * GB + i + 1)
                dve.wait_ge(cp_ready, h * GB + i + 1)
                dve.tensor_tensor(PN[:, s, 0], T[:, s, :, 0:H_],
                                  Z[:, s, 1, :].unsqueeze(2).broadcast_to([P, 4 * G8, H_]),
                                  ALU.mult).then_inc(norm0_ready, 1)

            rounds(dve, do_round)
            tail = Steps(dve, tail_order, h * 4)
            for u in range(2):
                for n in range(O0 + 4 * u, O0 + 4 * u + 4):
                    if not by_act[n]:
                        dve.wait_ge(full, h * JOBS + n + 1)
                        empty(n, dve.tensor_copy).then_inc(empty_d, 1)
                dve.wait_ge(sq_ready, h * 2 + u + 1)
                tail.then(dve.tensor_reduce(ss[:, u], SQ[:, u].rearrange("p (n d) -> p n d", d=DV), AX.X, ALU.add))
                dve.tensor_scalar(ss[:, u], ss[:, u], 1.0 / DV, EPS, ALU.mult, ALU.add).then_inc(ss_ready, 1)
                dve.wait_ge(rr_ready, h * 2 + u + 1)
                tail.then(dve.reciprocal(rr[:, u], rr[:, u]))
                o = OK[:, u].rearrange("p G a d -> p (G a) d")
                dve.scalar_tensor_tensor(o, o, 1.0 - LAMBDA_INIT, rr[:, u].unsqueeze(2).broadcast_to([P, P, DV]),
                                         ALU.mult, ALU.mult).then_inc(ok_ready, 1)
            for n in range(F0, P0):
                if not by_act[n]:
                    dve.wait_ge(full, h * JOBS + n + 1)
                    empty(n, dve.tensor_copy).then_inc(empty_d, 1)
            dve.wait_ge(bias_added, h * B + B)
            for n in range(P0, JOBS):
                m = 2 * (n - P0)
                dve.wait_ge(full, h * JOBS + n + 1)
                dve.tensor_tensor(c.H1[:, m:m + 2, :], c.H1[:, m:m + 2, :],
                                  work[:, n % 6, :].rearrange("p (q n) -> p q n", q=2), ALU.add).then_inc(empty_d, 1)


FF = 1024


def mlp(c, h, own):
    nc, d = c.nc, c.d
    c.phase = "ml_"
    MF = FF // P
    w1 = c.sb("w1", [P, KD, FF], ctx=own)
    w2 = c.sb("w2", [P, MF, DM], ctx=own)
    b2 = c.sb("b2", [P, DM], ctx=own)
    stats = c.sb("stats", [P, TJ, 6], ctx=own)
    mv = c.sb("mv", [P, TJ, 2], ctx=own)
    ve = c.sb("ve", [P, TJ], ctx=own)
    rs = c.sb("rs", [P, TJ], ctx=own)
    xhat = c.sb("xhat", [P, 2, TJ, DM], ctx=own)
    hT = c.sb("hT", [P, 2, KD, TJ * P], ctx=own)
    rT = c.sb("rT", [P, 2, MF, TJ * P], ctx=own)
    tp = c.ps("tp", [P, KD, 512], ctx=own)
    f1 = c.ps("f1", [P, 4, 512], ctx=own)
    f2 = c.ps("f2", [P, 2, 2, DM], ctx=own)
    sem = lambda n: c.sem("mlp_" + n)
    w_loaded, stats_ready, rstd_ready, xhat_ready = sem("w_loaded"), sem("stats"), sem("rstd"), sem("xhat")
    tp_ready, hT_ready, f1_ready, rT_ready = sem("tp"), sem("hT"), sem("f1"), sem("rT")
    f2_ready, f2_free = sem("f2"), sem("f2_free")
    dve_order, pool_order, sum_order = sem("dve_order"), sem("pool_order"), sem("sum_order")
    b2_added = sem("b2_added")

    with nc.Block() as block:

        @block.sync
        def _(sp):
            sp.dma_start(w1[:], d["w1"].rearrange("(k p) n -> p k n", p=P)).then_inc(w_loaded, 16)
            sp.dma_start(w2[:], d["w2"].rearrange("(k p) n -> p k n", p=P)).then_inc(w_loaded, 16)
            sp.dma_start(b2[:], d["rows"][ROW["b2_attn"]:ROW["b2_attn"] + 1, :].broadcast_to([P, DM])).then_inc(w_loaded, 16)

        @block.gpsimd
        def _(pool):

            def add_b2(b):
                part = c.H1[:, b * TJ:(b + 1) * TJ, :]
                pool.wait_ge(xhat_ready, h * B + b + 1)
                pool.tensor_tensor(part, part, b2[:].unsqueeze(1).broadcast_to([P, TJ, DM]),
                                   ALU.add).then_inc(b2_added, 1)

            for b in range(B):
                c.hold(pool, stats_ready, h * B + b + 1)
                pool.tensor_scalar(ve[:], mv[:, :, 1], EPS, None, ALU.add).then_inc(pool_order, 1)
                pool.wait_ge(pool_order, h * B + b + 1)
                pool.tensor_tensor(rs[:], ve[:], c.mhalf[:, 0:TJ], ALU.pow).then_inc(rstd_ready, 1)
                if b == 1:
                    pool.wait_ge(w_loaded, h * 48 + 48)
                if b:
                    add_b2(b - 1)
            add_b2(B - 1)

        @block.scalar
        def _(act):
            for b in range(B):
                for k in range(KD):
                    act.wait_ge(tp_ready, h * 2 * B + 2 * b + k + 1)
                    g, o = COL["ln2_g"] + k, COL["ln2_b"] + k
                    act.activation(hT[:, b % 2, k, :], tp[:, k, :], ACT.Identity,
                                   bias=c.cols[:, o:o + 1], scale=c.cols[:, g:g + 1]).then_inc(hT_ready, 1)
                if b >= 2:
                    act.wait_ge(f2_ready, h * 2 * B + 2 * (b - 1))
                for m in range(MF):
                    act.wait_ge(f1_ready, h * B * MF + b * MF + m + 1)
                    col = COL["b1"] + m
                    act.activation(rT[:, b % 2, m, :], f1[:, m % 4, :], ACT.Relu,
                                   bias=c.cols[:, col:col + 1]).then_inc(rT_ready, 1)

        @block.tensor
        def _(pe):

            def up(b):
                pe.wait_ge(xhat_ready, h * B + b + 1)
                if b:
                    pe.wait_ge(hT_ready, h * 2 * B + 2 * b)
                for k in range(KD):
                    for t in range(TJ):
                        last = pe.transpose(tp[:, k, t * P:(t + 1) * P], xhat[:, b % 2, t, k * P:(k + 1) * P], c.ident[:])
                    last.then_inc(tp_ready, 1)
                pe.wait_ge(hT_ready, h * 2 * B + 2 * b + 2)
                for m in range(MF):
                    if b * MF + m >= 4:
                        pe.wait_ge(rT_ready, h * B * MF + b * MF + m - 3)
                    for k in range(KD):
                        last = pe.matmul(f1[:, m % 4, :], w1[:, k, m * P:(m + 1) * P], hT[:, b % 2, k, :],
                                         start=(k == 0), stop=(k == KD - 1))
                    last.then_inc(f1_ready, 1)

            def down(b):
                pe.wait_ge(rT_ready, h * B * MF + (b + 1) * MF)
                for n in range(2):
                    if 2 * b + n >= 2:
                        pe.wait_ge(f2_free, h * 2 * B + 2 * b + n - 1)
                    for q in range(2):
                        t = 2 * n + q
                        for m in range(MF):
                            last = pe.matmul(f2[:, n, q, :], rT[:, b % 2, m, t * P:(t + 1) * P], w2[:, m, :],
                                             start=(m == 0), stop=(m == MF - 1))
                    last.then_inc(f2_ready, 1)

            pe.wait_ge(w_loaded, h * 48 + 48)
            up(0)
            for b in range(B - 1):
                up(b + 1)
                down(b)
            down(B - 1)

        @block.vector
        def _(dve):

            def layernorm(b):
                for t in range(TJ):
                    last = dve.bn_stats(stats[:, t, :], c.H1[:, b * TJ + t, :])
                last.then_inc(dve_order, 1)
                c.hold(dve, dve_order, h * B + b + 1)
                for t in range(TJ):
                    last = dve.bn_aggr(mv[:, t, :], stats[:, t, :])
                last.then_inc(stats_ready, 1)
                dve.wait_ge(rstd_ready, h * B + b + 1)
                if b >= 2:
                    dve.wait_ge(tp_ready, h * 2 * B + 2 * (b - 1))
                for t in range(TJ):
                    last = dve.tensor_scalar(xhat[:, b % 2, t, :], c.H1[:, b * TJ + t, :], mv[:, t, 0:1],
                                             rs[:, t:t + 1], ALU.subtract, ALU.mult)
                last.then_inc(xhat_ready, 1)

            layernorm(0)
            layernorm(1)
            for b in range(B):
                if b + 2 < B:
                    layernorm(b + 2)
                dve.wait_ge(b2_added, h * B + b + 1)
                for n in range(2):
                    m = 2 * b + n
                    y = c.H1[:, 2 * m:2 * m + 2, :]
                    xs = c.X[:, bass.ds(h * TH + 2 * m, 2), :]
                    dve.wait_ge(f2_ready, h * 2 * B + m + 1)
                    dve.tensor_tensor(y, y, f2[:, n], ALU.add).then_inc(f2_free, 1)
                    dve.wait_ge(f2_free, h * 2 * B + m + 1)
                    dve.tensor_tensor(y, y, c.rows1[:, b, 2:3, :].broadcast_to([P, 2, DM]), ALU.mult
                                      ).then_inc(sum_order, 1)
                    dve.wait_ge(sum_order, h * 2 * B + m + 1)
                    dve.tensor_tensor(xs, xs, y, ALU.add)


E_, HM, GR = 8, 512, 16
NT = TILES + E_ - 1


def moe(c, out):
    nc, d = c.nc, c.d
    c.phase = "moe_"
    h_dram = nc.dram_tensor("h_dram", (TILES * P, DM), F32, kind="Internal").ap()
    y_dram = nc.dram_tensor("y_dram", ((TILES + NT) * P, DM), F32, kind="Internal").ap()
    sem = lambda n: c.sem("moe_" + n)
    with ExitStack() as own:
        sb = lambda name, shape, dt=F32: c.sb(name, shape, dt, ctx=own)
        w1 = sb("w1", [P, E_, KD, HM])
        w2 = sb("w2", [P, E_, HM // P, DM])
        b1 = sb("b1", [P, E_, HM])
        b2 = sb("b2", [P, E_, DM])
        token_in = sb("token_in", [P, NT], U32)
        token_out = sb("token_out", [P, NT], U32)
        expert = sb("expert", [1, NT], U32)
        score = sb("score", [P, TILES])
        w_loaded = sem("w_loaded")

        with ExitStack() as st:
            sb1 = lambda name, shape, dt=F32: c.sb(name, shape, dt, ctx=st)
            hrow = sb1("hrow", [P, TILES, DM])
            w_red = sb1("w_red", [P, KD, GR])
            wgT = sb1("wgT", [GR, E_])
            wsq = sb1("wsq", [GR, E_])
            stats = sb1("stats", [P, 2, TJ, 6])
            mv = sb1("mv", [P, 2, TJ, 2])
            ve = sb1("ve", [P, 2, TJ])
            rs = sb1("rs", [P, 2, TJ])
            xhat = sb1("xhat", [P, 2, TJ, DM])
            rows_scaled, rows_ready = sem("rows_scaled"), sem("rows_ready")
            hT = sb1("hT", [P, KD, TJ * P])
            xr = sb1("xr", [GR, TJ * P])
            full1 = sb1("full1", [P, P])
            upper = sb1("upper", [P, P])
            L = sb1("L", [P, TILES, E_])
            O = sb1("O", [P, TILES, E_])
            W = sb1("W", [P, TILES, E_])
            iota = sb1("iota", [P, E_])
            tile_no = sb1("tile_no", [P, NT])
            ends = sb1("ends", [P, NT, E_])
            mx = sb1("mx", [P, TILES])
            tmp = sb1("tmp", [P, TILES])
            cnt = sb1("cnt", [P, 8, E_])
            cnt_i = sb1("cnt_i", [P, E_], I32)
            tile_i = sb1("tile_i", [P, TILES], I32)
            tile_of = sb1("tile_of", [P, TILES])
            row_of = sb1("row_of", [P, TILES])
            in_tile = sb1("in_tile", [P, TILES, NT])
            in_row = xhat[:].rearrange("p s t n -> p s (t n)").rearrange("p s (t r) -> p s t r", r=P)
            number = sb1("number", [P, TILES])
            row_no = sb1("row_no", [P, P])
            pad_no = sb1("pad_no", [P, NT])
            invs = sb1("invs", [NT, P])
            tokens = sb1("tokens", [P, NT])
            in_tile_ready, in_row_ready, in_row_used = sem("in_tile_ready"), sem("in_row_ready"), sem("in_row_used")
            inv_ready, invs_ready, tokens_ready, h_stored = sem("inv"), sem("invs"), sem("tokens"), sem("h_stored")
            tp = c.ps("tp", [P, KD, 512], ctx=st)
            rp = c.ps("rp", [P, 512], ctx=st)
            lp = c.ps("lp", [P, 512], ctx=st)
            pre = c.ps("pre", [P, 512], ctx=st)
            tot = c.ps("tot", [P, 512], ctx=st)
            np_ = c.ps("np", [P, 512], ctx=st)
            r_loaded, stats_ready, rstd_ready, xhat_ready = sem("r_loaded"), sem("stats"), sem("rstd"), sem("xhat")
            tp_ready, hT_ready, rp_ready, xr_ready = sem("tp"), sem("hT"), sem("rp"), sem("xr")
            lp_ready, lp_free, l_done = sem("lp"), sem("lp_free"), sem("l_done")
            ln_order = sem("ln_order")
            dve_order, pool_order = sem("dve_order"), sem("pool_order")
            wsq_ready, norm_ready, sqrt_ready, wg_ready = sem("wsq"), sem("norm"), sem("sqrt"), sem("wg")
            m_ready, exp_ready, o_ready, count_ready = sem("m"), sem("exp"), sem("o"), sem("count")
            const_ready = sem("const")

            with nc.Block() as block:

                @block.sync
                def _(sp):
                    sp.dma_start(w_red[:], d["w_red"].rearrange("(k p) n -> p k n", p=P)).then_inc(r_loaded, 16)
                    sp.dma_start(wgT[:], d["wgT"]).then_inc(r_loaded, 16)
                    for e in range(E_):
                        sp.dma_start(w1[:, e], d["moe_w1"][e].rearrange("(k p) n -> p k n", p=P)).then_inc(w_loaded, 16)
                        sp.dma_start(w2[:, e], d["moe_w2"][e].rearrange("(k p) n -> p k n", p=P)).then_inc(w_loaded, 16)
                    sp.dma_start(b1[:].rearrange("p e n -> p (e n)"), d["moe_b1"].rearrange("e n -> (e n)").unsqueeze(0)
                                 .broadcast_to([P, E_ * HM])).then_inc(w_loaded, 16)
                    sp.dma_start(b2[:].rearrange("p e n -> p (e n)"), d["moe_b2"].rearrange("e n -> (e n)").unsqueeze(0)
                                 .broadcast_to([P, E_ * DM])).then_inc(w_loaded, 16)
                    with sp.Fori(0, 2 * B) as q:
                        sp.wait_ge(rows_ready, q + 1)
                        sp.dma_start(h_dram[bass.ds(q * TJ * P, TJ * P), :].rearrange("(t p) n -> p t n", p=P),
                                     hrow[:, bass.ds(q * TJ, TJ), :]).then_inc(h_stored, 16)
                    sp.wait_ge(h_stored, 16 * 2 * B)

                @block.gpsimd
                def _(pool):
                    pool.memset(full1[:], 1.0).then_inc(const_ready, 1)
                    pool.memset(upper[:], 1.0).then_inc(pool_order, 1)
                    pool.iota(iota[:], pattern=[[1, E_]], base=0, channel_multiplier=0,
                              allow_small_or_imprecise_dtypes=True)
                    pool.iota(tile_no[:], pattern=[[1, NT]], base=0, channel_multiplier=0,
                              allow_small_or_imprecise_dtypes=True)
                    pool.iota(row_no[:], pattern=[[1, P]], base=0, channel_multiplier=0,
                              allow_small_or_imprecise_dtypes=True)
                    pool.iota(number[:], pattern=[[P, TILES]], base=1, channel_multiplier=1,
                              allow_small_or_imprecise_dtypes=True)
                    pool.iota(pad_no[:], pattern=[[P, NT]], base=TILES * P + 1, channel_multiplier=1,
                              allow_small_or_imprecise_dtypes=True)
                    pool.wait_ge(pool_order, 1)
                    pool.affine_select(out=upper[:], in_=upper[:], compare_op=ALU.is_gt, fill=0.0,
                                       base=0, pattern=[[1, P]], channel_multiplier=-1).then_inc(const_ready, 1)
                    def rstd(q, s):
                        c.hold(pool, stats_ready, q + 1)
                        pool.tensor_scalar(ve[:, s], mv[:, s, :, 1], EPS, None, ALU.add).then_inc(pool_order, 1)
                        pool.wait_ge(pool_order, q + 2)
                        pool.tensor_tensor(rs[:, s], ve[:, s], c.mhalf[:, 0:TJ], ALU.pow).then_inc(rstd_ready, 1)

                    with pool.Fori(0, HALVES) as hh:
                        rstd(hh * B, 0)
                        for b in range(B):
                            if b + 1 < B:
                                rstd(hh * B + b + 1, (b + 1) % 2)
                            rows = hrow[:, bass.ds(hh * TH + b * TJ, TJ), :]
                            c.hold(pool, xhat_ready, hh * B + b + 1)
                            pool.tensor_tensor(rows, xhat[:, b % 2], c.rows1[:, b, 4:5, :].broadcast_to([P, TJ, DM]),
                                               ALU.mult).then_inc(rows_scaled, 1)
                            c.hold(pool, rows_scaled, hh * B + b + 3)
                            pool.tensor_tensor(rows, rows, c.rows1[:, b, 3:4, :].broadcast_to([P, TJ, DM]),
                                               ALU.add).then_inc(rows_ready, 1)

                @block.scalar
                def _(act):
                    act.wait_ge(norm_ready, 1)
                    act.activation(wsq[:], np_[0:GR, 0:E_], ACT.Sqrt).then_inc(sqrt_ready, 1)
                    with act.Fori(0, HALVES) as hh:
                        for b in range(B):
                            q = hh * B + b
                            for k in range(KD):
                                act.wait_ge(tp_ready, q * 2 + k + 1)
                                act.activation(hT[:, k, :], tp[:, k, :], ACT.Identity,
                                               bias=c.modT[1][:, 3 * KD + k, b:b + 1],
                                               scale=c.modT[1][:, 4 * KD + k, b:b + 1]).then_inc(hT_ready, 1)
                            act.wait_ge(rp_ready, q + 1)
                            act.copy(xr[:], rp[0:GR, :]).then_inc(xr_ready, 1)
                    act.wait_ge(m_ready, 1)
                    act.activation(W[:], W[:], ACT.Exp).then_inc(exp_ready, 1)

                @block.tensor
                def _(pe):
                    pe.wait_ge(wsq_ready, 1)
                    pe.wait_ge(const_ready, 2)
                    pe.matmul(np_[0:GR, 0:E_], full1[0:GR, 0:GR], wsq[:], start=True, stop=True).then_inc(norm_ready, 1)
                    pe.wait_ge(wg_ready, 1)

                    def turn(q, s):
                        pe.wait_ge(xhat_ready, q + 1)
                        for k in range(KD):
                            for t in range(TJ):
                                last = pe.transpose(tp[:, k, t * P:(t + 1) * P], xhat[:, s, t, k * P:(k + 1) * P],
                                                    c.ident[:])
                            last.then_inc(tp_ready, 1)

                    with pe.Fori(0, HALVES) as hh:
                        turn(hh * B, 0)
                        for b in range(B):
                            q = hh * B + b
                            pe.wait_ge(hT_ready, q * 2 + 2)
                            for k in range(KD):
                                last = pe.matmul(rp[0:GR, :], w_red[:, k, :], hT[:, k, :], start=(k == 0),
                                                 stop=(k == KD - 1))
                            last.then_inc(rp_ready, 1)
                            if b + 1 < B:
                                turn(q + 1, (b + 1) % 2)
                            pe.wait_ge(xr_ready, q + 1)
                            pe.wait_ge(lp_free, q + 1)
                            for t in range(TJ):
                                last = pe.matmul(lp[:, t * E_:(t + 1) * E_], xr[:, t * P:(t + 1) * P], wgT[:],
                                                 start=True, stop=True)
                            last.then_inc(lp_ready, 1)
                    pe.wait_ge(o_ready, 1)
                    o = O[:].rearrange("p t e -> p (t e)")
                    pe.matmul(pre[:, 0:TILES * E_], upper[:], o, start=True, stop=True)
                    pe.matmul(tot[:, 0:TILES * E_], full1[:], o, start=True, stop=True).then_inc(count_ready, 1)
                    pe.wait_ge(in_tile_ready, 1)
                    for t in range(TILES):
                        if t % 8 == 0:
                            pe.wait_ge(in_row_ready, t // 8 + 1)
                        last = pe.matmul(np_[0:NT, 0:P], in_tile[:, t, :], in_row[:, t // 8 % 2, t % 8, :],
                                         start=(t == 0), stop=(t == TILES - 1))
                        if t % 8 == 7:
                            last.then_inc(in_row_used, 1)
                    pe.wait_ge(invs_ready, 1)
                    pe.transpose(rp[:, 0:NT], invs[:], c.ident[0:NT, 0:NT]).then_inc(tokens_ready, 1)

                @block.vector
                def _(dve):
                    order = Steps(dve, dve_order)
                    dve.wait_ge(r_loaded, 32)
                    dve.tensor_tensor(wsq[:], wgT[:], wgT[:], ALU.mult).then_inc(wsq_ready, 1)
                    dve.wait_ge(sqrt_ready, 1)
                    order.then(dve.tensor_scalar(wsq[:], wsq[:], 1e-4, None, ALU.max))
                    order.then(dve.reciprocal(wsq[:], wsq[:]))
                    dve.tensor_tensor(wgT[:], wgT[:], wsq[:], ALU.mult).then_inc(wg_ready, 1)
                    dve.sem_inc(lp_free, 1)

                    dve.sem_inc(rows_scaled, 2)

                    def layernorm(q, s):
                        for t in range(TJ):
                            last = dve.bn_stats(stats[:, s, t, :], c.X[:, q * TJ + t, :])
                        last.then_inc(ln_order, 1)
                        c.hold(dve, ln_order, q + 1)
                        for t in range(TJ):
                            last = dve.bn_aggr(mv[:, s, t, :], stats[:, s, t, :])
                        last.then_inc(stats_ready, 1)
                        dve.wait_ge(rstd_ready, q + 1)
                        dve.wait_ge(rows_scaled, q + 1)
                        for t in range(TJ):
                            last = dve.tensor_scalar(xhat[:, s, t, :], c.X[:, q * TJ + t, :],
                                                     mv[:, s, t, 0:1], rs[:, s, t:t + 1], ALU.subtract, ALU.mult)
                        last.then_inc(xhat_ready, 1)

                    with dve.Fori(0, HALVES) as hh:
                        layernorm(hh * B, 0)
                        for b in range(B):
                            q = hh * B + b
                            if b + 1 < B:
                                layernorm(q + 1, (b + 1) % 2)
                            dve.wait_ge(lp_ready, q + 1)
                            dve.tensor_copy(L[:, bass.ds(q * TJ, TJ), :],
                                            lp[:, 0:TJ * E_].rearrange("p (t e) -> p t e", e=E_)).then_inc(lp_free, 1)
                    dve.wait_ge(lp_free, 2 * B + 1)

                    def over_e(x):
                        return x.unsqueeze(2).broadcast_to([P, TILES, E_])

                    def over_t(x):
                        return x.unsqueeze(1).broadcast_to([P, TILES, E_])

                    order.then(dve.tensor_reduce(mx[:], L[:], AX.X, ALU.max))
                    dve.tensor_tensor(W[:], L[:], over_e(mx[:]), ALU.subtract).then_inc(m_ready, 1)
                    order.then(dve.tensor_tensor(L[:], L[:], over_e(mx[:]), ALU.is_equal))
                    order.then(dve.scalar_tensor_tensor(L[:], L[:], -float(E_), over_t(iota[:]), ALU.mult, ALU.add))
                    order.then(dve.tensor_reduce(mx[:], L[:], AX.X, ALU.min))
                    dve.tensor_tensor(O[:], L[:], over_e(mx[:]), ALU.is_equal).then_inc(o_ready, 1)
                    dve.wait_ge(exp_ready, 1)
                    order.then(dve.tensor_reduce(tmp[:], W[:], AX.X, ALU.add))
                    order.then(dve.reciprocal(score[:], tmp[:]))
                    dve.wait_ge(count_ready, 1)
                    order.then(dve.tensor_copy(W[:], tot[:, 0:TILES * E_].rearrange("p (t e) -> p t e", e=E_)))
                    dve.wait_ge(o_ready, 1)
                    for e in range(E_):
                        order.did(dve.tensor_tensor_scan(L[:, :, e], full1[:, 0:TILES], W[:, :, e], 0.0,
                                                           ALU.mult, ALU.add))
                    dve.wait_ge(dve_order, order.n)
                    order.then(dve.tensor_scalar(cnt[:, 0, :], L[:, TILES - 1, :], float(P - 1), None, ALU.add))
                    order.then(dve.tensor_tensor(L[:], L[:], W[:], ALU.subtract))
                    order.then(dve.tensor_tensor(L[:], L[:], pre[:, 0:TILES * E_].rearrange("p (t e) -> p t e", e=E_),
                                                 ALU.add))
                    order.then(dve.tensor_copy(cnt_i[:], cnt[:, 0, :]))
                    order.then(dve.tensor_scalar(cnt_i[:], cnt_i[:], 7, None, ALU.arith_shift_right))
                    order.then(dve.tensor_copy(cnt[:, 1, :], cnt_i[:]))
                    order.then(dve.tensor_tensor_scan(cnt[:, 2, :], full1[:, 0:E_], cnt[:, 1, :], 0.0, ALU.mult, ALU.add))
                    order.then(dve.tensor_tensor(cnt[:, 3, :], cnt[:, 2, :], cnt[:, 1, :], ALU.subtract))
                    order.then(dve.scalar_tensor_tensor(L[:], over_t(cnt[:, 3, :]), float(P), L[:], ALU.mult, ALU.add))
                    order.then(dve.tensor_tensor(L[:], L[:], O[:], ALU.mult))
                    order.then(dve.tensor_reduce(tmp[:], L[:], AX.X, ALU.add))
                    order.then(dve.tensor_copy(tile_i[:], tmp[:]))
                    order.then(dve.tensor_scalar(tile_i[:], tile_i[:], 7, None, ALU.arith_shift_right))
                    order.then(dve.tensor_copy(tile_of[:], tile_i[:]))
                    order.then(dve.scalar_tensor_tensor(row_of[:], tile_of[:], -float(P), tmp[:], ALU.mult, ALU.add))
                    order.then(dve.tensor_tensor(in_tile[:], tile_of[:].unsqueeze(2).broadcast_to([P, TILES, NT]),
                                                 tile_no[:].unsqueeze(1).broadcast_to([P, TILES, NT]), ALU.is_equal))
                    dve.tensor_tensor(in_tile[:], in_tile[:], number[:].unsqueeze(2).broadcast_to([P, TILES, NT]),
                                      ALU.mult).then_inc(in_tile_ready, 1)
                    dve.wait_ge(rows_ready, 2 * B)
                    for n in range(4):
                        if n >= 2:
                            dve.wait_ge(in_row_used, n - 1)
                        dve.tensor_tensor(in_row[:, n % 2], row_of[:, 8 * n:8 * n + 8].unsqueeze(2).broadcast_to([P, 8, P]),
                                          row_no[:].unsqueeze(1).broadcast_to([P, 8, P]), ALU.is_equal
                                          ).then_inc(in_row_ready, 1)
                    order.then(dve.tensor_tensor(ends[:], cnt[:, 2, :].unsqueeze(1).broadcast_to([P, NT, E_]),
                                                 tile_no[:].unsqueeze(2).broadcast_to([P, NT, E_]), ALU.is_le))
                    order.then(dve.tensor_reduce(tile_no[:], ends[:], AX.X, ALU.add))
                    order.then(dve.tensor_scalar(tile_no[:], tile_no[:], float(E_ - 1), None, ALU.min))
                    dve.tensor_copy(expert[:], tile_no[0:1, :])
                    dve.wait_ge(in_row_used, 4)
                    dve.tensor_copy(invs[:], np_[0:NT, 0:P]).then_inc(invs_ready, 1)
                    dve.wait_ge(tokens_ready, 1)
                    order.then(dve.tensor_scalar(tokens[:], rp[:, 0:NT], -1.0, 0.0, ALU.add, ALU.max))
                    dve.tensor_copy(token_in[:], tokens[:])
                    order.then(dve.scalar_tensor_tensor(in_tile[:, 0, :], rp[:, 0:NT], 0.0, pad_no[:],
                                                        ALU.is_equal, ALU.mult))
                    order.then(dve.scalar_tensor_tensor(in_tile[:, 1, :], rp[:, 0:NT], -1.0, in_tile[:, 0, :],
                                                        ALU.add, ALU.add))
                    dve.tensor_copy(token_out[:], in_tile[:, 1, :])

        with ExitStack() as st:
            sb2 = lambda name, shape, dt=F32: c.sb(name, shape, dt, ctx=st)
            hs = sb2("hs", [P, 3, DM])
            hsT = sb2("hsT", [P, 2, KD, P])
            a = sb2("a", [P, 2, HM])
            aT = sb2("aT", [P, 2, HM // P, P])
            ys = sb2("ys", [P, 3, DM])
            tp = c.ps("tp2", [P, 2, 512], ctx=st)
            up = c.ps("up", [P, 2, HM], ctx=st)
            ap = c.ps("ap", [P, 2, 512], ctx=st)
            dn = c.ps("dn", [P, 2, 512], ctx=st)
            hs_loaded = [sem(f"hs_loaded{i}") for i in range(3)]
            ys_stored = [sem(f"ys_stored{i}") for i in range(3)]
            tp_ready, hsT_ready, up_ready, up_free = sem("tp2"), sem("hsT"), sem("up"), sem("up_free")
            ys_free = sem("ys_free")
            a_ready, ap_ready, aT_ready, dn_ready, ys_ready = sem("a"), sem("ap"), sem("aT"), sem("dn"), sem("ys")

            def tiles(eng, do_tile):
                with eng.Fori(0, NT // 6) as i6:
                    for j in range(6):
                        do_tile(i6 * 6 + j, i6 * 2 + j // 3, j)
                for n in range(NT // 6 * 6, NT):
                    do_tile(n, n // 3, n)

            with nc.Block() as block:

                @block.gpsimd
                def _(pool):

                    def take_in(n):
                        pool.wait_ge(hsT_ready, n + 1)
                        pool.indirect_dma_start(hs[:, n % 3, :], None, h_dram,
                                                bass.IndirectOffsetOnAxis(ap=token_in[:, n:n + 1], axis=0)
                                                ).then_inc(hs_loaded[n % 3], 16)

                    for n in range(3):
                        take_in(n)
                    for n in range(NT):
                        if n + 3 < NT:
                            take_in(n + 3)
                        pool.wait_ge(ys_ready, n + 1)
                        pool.indirect_dma_start(y_dram, bass.IndirectOffsetOnAxis(ap=token_out[:, n:n + 1], axis=0),
                                                ys[:, n % 3, :], None).then_inc(ys_stored[n % 3], 16)

                @block.sync
                def _(sp):
                    for n in range(NT):
                        sp.wait_ge(ys_stored[n % 3], 16 * (n // 3) + 16)
                        sp.sem_inc(ys_free, 1)

                @block.tensor
                def _(pe):
                    pe.wait_ge(w_loaded, 16 * (2 * E_ + 2))

                    def expert_of(n):
                        return pe.value_load(expert[0:1, bass.ds(n, 1)], min_val=0, max_val=E_ - 1)

                    def turn_h(n, turn, j):
                        pe.wait_ge(hs_loaded[j % 3], turn * 16 + 16)
                        for k in range(KD):
                            last = pe.transpose(tp[:, j % 2, k * P:(k + 1) * P], hs[:, j % 3, k * P:(k + 1) * P], c.ident[:])
                        last.then_inc(tp_ready, 1)

                    def go_up(n, j, e):
                        pe.wait_ge(hsT_ready, n + 4)
                        pe.wait_ge(up_free, n + 1)
                        for k in range(KD):
                            last = pe.matmul(up[:, j % 2, :], hsT[:, j % 2, k, :], w1[:, bass.ds(e, 1), k, :],
                                             start=(k == 0), stop=(k == KD - 1))
                        last.then_inc(up_ready, 1)

                    def do_tile(n, turn, j):
                        e = expert_of(n)
                        e_next = expert_of(n + 1) if not isinstance(n, int) or n + 1 < NT else None
                        pe.wait_ge(a_ready, n + 1)
                        for m in range(HM // P):
                            last = pe.transpose(ap[:, j % 2, m * P:(m + 1) * P], a[:, j % 2, m * P:(m + 1) * P], c.ident[:])
                        last.then_inc(ap_ready, 1)
                        if not isinstance(n, int) or n + 2 < NT:
                            turn_h(n + 2, turn + (2 + j % 3) // 3, j + 2)
                        if e_next is not None:
                            go_up(n + 1, j + 1, e_next)
                        pe.wait_ge(aT_ready, n + 1)
                        for m in range(HM // P):
                            last = pe.matmul(dn[:, j % 2, 0:DM], aT[:, j % 2, m, :], w2[:, bass.ds(e, 1), m, :],
                                             start=(m == 0), stop=(m == HM // P - 1))
                        last.then_inc(dn_ready, 1)

                    turn_h(0, 0, 0)
                    turn_h(1, 0, 1)
                    go_up(0, 0, expert_of(0))
                    tiles(pe, do_tile)

                @block.scalar
                def _(act):
                    act.sem_inc(hsT_ready, 3)

                    def turned(n, j):
                        act.wait_ge(tp_ready, n + 1)
                        act.copy(hsT[:, j % 2].rearrange("p k n -> p (k n)"), tp[:, j % 2, 0:DM]).then_inc(hsT_ready, 1)

                    def gelu(n, j):
                        act.wait_ge(up_free, n + 3)
                        act.activation(a[:, j % 2, :], a[:, j % 2, :], ACT.Gelu).then_inc(a_ready, 1)

                    def do_tile(n, turn, j):
                        act.wait_ge(ap_ready, n + 1)
                        act.copy(aT[:, j % 2].rearrange("p m n -> p (m n)"), ap[:, j % 2, :]).then_inc(aT_ready, 1)
                        if not isinstance(n, int) or n + 2 < NT:
                            turned(n + 2, j)
                        if not isinstance(n, int) or n + 1 < NT:
                            gelu(n + 1, j + 1)

                    turned(0, 0)
                    turned(1, 1)
                    gelu(0, 0)
                    tiles(act, do_tile)

                @block.vector
                def _(dve):
                    dve.sem_inc(up_free, 2)
                    dve.sem_inc(ys_free, 3)

                    def expert_of(n):
                        return dve.value_load(expert[0:1, bass.ds(n, 1)], min_val=0, max_val=E_ - 1)

                    def add_b1(n, j):
                        e = expert_of(n)
                        dve.wait_ge(up_ready, n + 1)
                        dve.tensor_tensor(a[:, j % 2, :], up[:, j % 2, :], b1[:, bass.ds(e, 1), :].rearrange(
                            "p o n -> p (o n)"), ALU.add).then_inc(up_free, 1)

                    def do_tile(n, turn, j):
                        if not isinstance(n, int) or n + 1 < NT:
                            add_b1(n + 1, j + 1)
                        e = expert_of(n)
                        dve.wait_ge(dn_ready, n + 1)
                        dve.wait_ge(ys_free, n + 1)
                        dve.tensor_tensor(ys[:, j % 3, :], dn[:, j % 2, 0:DM], b2[:, bass.ds(e, 1), :].rearrange(
                            "p o n -> p (o n)"), ALU.add).then_inc(ys_ready, 1)

                    add_b1(0, 0)
                    tiles(dve, do_tile)

        with ExitStack() as st:
            y = c.sb("y", [P, 2 * B, TJ, DM], ctx=st)
            taken, gated, stored = [sem(f"taken{i}") for i in range(B)], sem("gated"), sem("stored")
            x_ready = [sem("x_ready_pool"), sem("x_ready_dve")]
            with nc.Block() as block:

                def add(eng, q):
                    eng.wait_ge(gated, TJ * (q + 1))
                    xs = c.X[:, q * TJ:(q + 1) * TJ, :]
                    eng.tensor_tensor(xs, xs, y[:, q], ALU.add).then_inc(x_ready[q % 2], 1)

                @block.gpsimd
                def _(pool):
                    for q in range(0, 2 * B, 2):
                        add(pool, q)

                @block.vector
                def _(dve):
                    for q in range(2 * B):
                        dve.wait_ge(taken[q // 2], 16)
                        for t in range(TJ):
                            at = q * TJ + t
                            dve.scalar_tensor_tensor(y[:, q, t, :], y[:, q, t, :], score[:, at:at + 1],
                                                     c.rows1[:, q % B, 5, :], ALU.mult, ALU.mult).then_inc(gated, 1)
                        if q % 2:
                            add(dve, q)

                @block.sync
                def _(sp):
                    for n in range(B):
                        rows = y_dram[2 * n * TJ * P:2 * (n + 1) * TJ * P, :].rearrange("(q t p) n -> p q t n", t=TJ, p=P)
                        sp.dma_start(y[:, 2 * n:2 * n + 2], rows).then_inc(taken[n], 16)
                    for q in range(2 * B):
                        h, b = q // B, q % B
                        sp.wait_ge(x_ready[q % 2], q // 2 + 1)
                        sp.dma_start(out[b, h * TJ * P:(h + 1) * TJ * P, :].rearrange("(t p) n -> p t n", p=P),
                                     c.X[:, q * TJ:(q + 1) * TJ, :]).then_inc(stored, 16)
                    sp.wait_ge(stored, 16 * B * HALVES)


def program(nc, d, out):
    with ExitStack() as ctx:
        c = Core(nc, ctx, d)
        lasting(c)
        c.layer1 = ctx.enter_context(ExitStack())
        attention_constants(c)
        c.layer0 = ctx.enter_context(ExitStack())
        c.gru_own = ctx.enter_context(ExitStack())
        setup(c)
        gru(c)
        c.gru_own.close()
        ffn(c)
        c.layer0.close()
        c.phase = "l1_"
        c.H1 = c.sb("H1", [P, TH, DM], ctx=c.layer1)
        with nc.Fori(0, HALVES) as h:
            with ExitStack() as own:
                attention(c, h, own)
            with ExitStack() as own:
                mlp(c, h, own)
        c.layer1.close()
        moe(c, out)


def lay_out(inputs):
    g = {k: np.asarray(v) for k, v in inputs.items()}
    a = {}
    a["x"] = g["L0_attn_x"]
    a["cT"] = np.stack([g["L0_c"].T, g["L1_c"].T])
    a["wmod"] = np.stack([g["L0_wmod"], g["L1_wmod"]])
    cols = np.zeros((P, NCOL), np.float32)
    src = {"bz_f": "L0_attn_bz_f", "bh_f": "L0_attn_bh_f", "bz_b": "L0_attn_bz_b", "bh_b": "L0_attn_bh_b",
           "bf": "L0_ffn_bf", "bi": "L0_ffn_bi", "bc": "L0_ffn_bc", "in_c": "L0_ffn_in_c",
           "ln1_g": "L1_attn_ln1_g", "ln1_b": "L1_attn_ln1_b", "ln2_g": "L1_attn_ln2_g",
           "ln2_b": "L1_attn_ln2_b", "b1": "L1_attn_b1"}
    for name, key in src.items():
        v = g[key].reshape(-1, P).T
        cols[:, COL[name]:COL[name] + v.shape[1]] = v
    a["cols"] = cols
    a["rows"] = np.stack([g["L0_attn_b_out"], g["L0_ffn_bo"], g["L1_attn_bo"], g["L1_attn_b2"]])
    a["wg"] = np.stack([g["L0_attn_Wz_f"], g["L0_attn_Wh_f"], g["L0_attn_Wz_b"], g["L0_attn_Wh_b"]])
    a["wo0"] = g["L0_attn_W_out"]
    l1 = "L1_attn_"
    heads = lambda w: w.T.reshape(DM, H_, D_, 2).transpose(0, 3, 1, 2).reshape(DM, DM)
    a["w_qk"] = np.concatenate([heads(g[l1 + "Wq"]), heads(g[l1 + "Wk"])], axis=1)
    a["w_v"], a["w_o"] = g[l1 + "Wv"].T, g[l1 + "Wo"].T
    a["lam"] = np.stack([g[l1 + n] for n in ("lq1", "lq2", "lk1", "lk2")])
    a["w1"], a["w2"] = g[l1 + "W1"].T, g[l1 + "W2"].T
    f1 = "L1_ffn_"
    a["w_red"], a["wgT"] = g[f1 + "w_red"], g[f1 + "wg"].T
    a["moe_w1"], a["moe_w2"], a["moe_b1"], a["moe_b2"] = (g[f1 + n] for n in ("W1", "W2", "b1", "b2"))
    p = np.arange(P)[:, None]
    a["maskK"] = np.where(p // D_ % 4 == np.arange(4), D_ ** -0.5, 0.0).astype(np.float32)
    j, kind, head = p // NH, p // H_ % 2, p % H_
    col = np.arange(64)
    a["combine"] = np.stack([(kind == n) & (j == col // H_) & (head == col % H_) for n in range(2)], 1
                            ).astype(np.float32)
    a["maskV"] = (p // H_ == np.arange(G8)).astype(np.float32)
    f = "L0_ffn_"
    a["w_ffn"] = np.stack([g[f + n].T for n in ("wf", "uf", "wi", "ui", "wc", "uc", "wo", "uo")])
    return a


def kernel(**inputs):
    import concourse.bacc as bacc
    from concourse.bass_utils import run_bass_kernel_spmd

    arrays = {f"in_{n}": np.ascontiguousarray(a) for n, a in lay_out(inputs).items()}
    nc = bacc.Bacc("TRN2", target_bir_lowering=False, num_devices=1)
    d = {n[3:]: nc.dram_tensor(n, a.shape, mybir.dt.from_np(a.dtype), kind="ExternalInput").ap()
         for n, a in arrays.items()}
    out = nc.dram_tensor("out", (B, S, DM), F32, kind="ExternalOutput").ap()
    program(nc, d, out)
    r = run_bass_kernel_spmd(nc, [arrays], core_ids=[0])
    return r.results[0]["out"]
```

```python
from contextlib import ExitStack

import numpy as np

import concourse.bass as bass
from concourse import mybir

F32 = mybir.dt.float32
F32R = mybir.dt.float32r
U32 = mybir.dt.uint32
I32 = mybir.dt.int32
ALU = mybir.AluOpType
ACT = mybir.ActivationFunctionType
AX = mybir.AxisListType

P = 128
B, S, DM = 4, 1024, 256
TILES = B * S // P
TB = S // P
HALVES = 2
TJ = TB // HALVES
TH = B * TJ
KD = DM // P
EPS = 1e-5
LAMBDA_INIT = 0.8 - 0.6 * float(np.exp(-0.3 * 1.0))
FMAX = float(np.finfo(np.float32).max)

COL = {}
_n = 0
for _name, _blocks in (("bz_f", 2), ("bh_f", 2), ("bz_b", 2), ("bh_b", 2), ("bf", 2), ("bi", 2), ("bc", 2),
                       ("in_c", 2), ("ln1_g", 2), ("ln1_b", 2), ("ln2_g", 2), ("ln2_b", 2), ("b1", 8)):
    COL[_name] = _n
    _n += _blocks
NCOL = _n
ROW = {n: i for i, n in enumerate(("b_out", "bo_ffn", "bo_attn", "b2_attn"))}
NROW = len(ROW)


def product3(pe, out, lhs, rhs, start, stop):
    pe.matmul(out, lhs[0], rhs[0], start=start, stop=False)
    pe.matmul(out, lhs[0], rhs[1], start=False, stop=False)
    return pe.matmul(out, lhs[1], rhs[0], start=False, stop=stop)


def low_part(eng, low, x, high):
    return eng.tensor_tensor(low, x, high.bitcast(F32), ALU.subtract)


class Steps:

    def __init__(self, eng, sem, base=0):
        self.eng, self.sem, self.base, self.n = eng, sem, base, 0

    def did(self, ins):
        ins.then_inc(self.sem, 1)
        self.n += 1
        return self.base + self.n

    def then(self, ins):
        self.eng.wait_ge(self.sem, self.did(ins))


class Core:

    def __init__(self, nc, ctx, d):
        self.nc, self.ctx, self.d = nc, ctx, d
        self.phase, self.sems = "", []
        self.clamped, self.summed = self.sem("attn_clamped"), self.sem("attn_summed")
        self.passed = self.sem("passed")

    def hold(self, eng, sem, value):
        eng.wait_ge(sem, value)
        eng.sem_inc(self.passed, 1)

    def sem(self, name):
        s = self.nc.alloc_semaphore(name)
        self.sems.append(s)
        return s

    def retire(self, first):
        self.nc.clear_and_free_semaphores(self.sems[first:])
        self.nc.all_engine_barrier()
        del self.sems[first:]

    def sb(self, name, shape, dt=F32, ctx=None):
        return (ctx or self.ctx).enter_context(self.nc.sbuf_tensor(self.phase + name, shape, dt))

    def ps(self, name, shape, dt=F32, ctx=None):
        return (ctx or self.ctx).enter_context(self.nc.psum_tensor(self.phase + name, shape, dt))


COL_PARTS = (tuple((0, j) for j in (0, 1, 3, 4)) + tuple((1, j) for j in (3, 4)))


def gru_stats(c, dve, order, b):
    for t in range(TB):
        last = order.did(dve.bn_stats(c.gru_stats[:, t, :], x_tile(c, b, t)))
    c.hold(dve, order.sem, last)
    for t in range(TB):
        last = dve.bn_aggr(c.gru_mv[:, t, :], c.gru_stats[:, t, :])
    last.then_inc(c.gru_stats_ready, 1)


def gru_normalize(c, dve, b):
    dve.wait_ge(c.gru_rstd_ready, b + 1)
    for t in range(TB):
        last = dve.tensor_scalar(c.gru_xhat[:, t, :], x_tile(c, b, t), c.gru_mv[:, t, 0:1], c.gru_rs[:, t:t + 1],
                                 ALU.subtract, ALU.mult)
        if t % TJ == TJ - 1:
            last.then_inc(c.gru_xhat_ready, 1)


def gru_rstd(c, pool, b):
    c.hold(pool, c.gru_stats_ready, b + 1)
    pool.tensor_scalar(c.gru_ve[:], c.gru_mv[:, :, 1], EPS, None, ALU.add).then_inc(c.gru_pool_order, 1)
    pool.wait_ge(c.gru_pool_order, b + 1)
    pool.tensor_tensor(c.gru_rs[:], c.gru_ve[:], c.mhalf[:, 0:TB], ALU.pow).then_inc(c.gru_rstd_ready, 1)


def gru_turn(c, pe, b, half):
    for n in (2 * half, 2 * half + 1):
        k, q = n // 2, n % 2
        if half == 0:
            pe.wait_ge(c.gru_xhat_ready, b * 2 + q + 1)
        else:
            pe.wait_ge(c.gru_hT_ready, b * 4 + n - 1)
        for t in range(4):
            last = pe.transpose(c.gru_tp[:, n % 2, t * P:(t + 1) * P],
                                c.gru_xhat[:, 4 * q + t, k * P:(k + 1) * P], c.ident[:])
        last.then_inc(c.gru_tp_ready, 1)


def gru_by_feature(c, act, b):
    for n in range(4):
        k, q = n // 2, n % 2
        c.hold(act, c.gru_tp_ready, b * 4 + n + 1)
        if n >= 2:
            c.hold(act, c.gru_h_low, b * 4 + n - 1)
        for dst in (c.gru_hT[:, 0, k, q * 512:(q + 1) * 512], c.gru_h_in[:, n % 2, :]):
            last = act.activation(dst, c.gru_tp[:, n % 2, :], ACT.Identity,
                                  bias=c.modT[0][:, 0 * KD + k, bass.ds(b, 1)],
                                  scale=c.modT[0][:, 1 * KD + k, bass.ds(b, 1)])
        last.then_inc(c.gru_hT_ready, 1)


def gru_h_split(c, dve, b, n):
    k, q = n // 2, n % 2
    at = slice(q * 512, (q + 1) * 512)
    dve.wait_ge(c.gru_hT_ready, b * 4 + n + 1)
    low_part(dve, c.gru_hT[:, 1, k, at], c.gru_h_in[:, n % 2, :], c.gru_hT[:, 0, k, at]).then_inc(c.gru_h_low, 1)


def x_tile(c, b, t):
    return c.X[:, b * TJ + (t // TJ * TH + t % TJ), :]


def lasting(c):
    c.X = c.sb("X", [P, TILES, DM])
    c.cols = c.sb("cols", [P, NCOL])
    c.nbz = c.sb("nbz", [P, 2, KD])
    c.ident = c.sb("ident", [P, P])
    c.mhalf = c.sb("mhalf", [P, TB])
    c.modT = [c.sb(f"modT{l}", [P, 6 * KD, B]) for l in range(2)]
    c.rows1 = c.sb("rows1", [P, B, 6, DM])


def setup(c):
    nc, d = c.nc, c.d
    c.rows0 = c.sb("rows0", [P, B, 2, DM], ctx=c.layer0)
    c.w_ffn = c.sb("w_ffn", [P, 8, KD, DM], ctx=c.layer0)
    c.ffn_w_loaded = c.sem("ffn_w_loaded")
    c.lam_in = c.sb("lam_in", [P, 2, 2, D_], ctx=c.layer0)
    c.lam = c.sb("lam", [P, 4], ctx=c.layer0)
    g = c.gru_own
    c.gru_H = c.sb("gru_H", [P, 4, S], ctx=g)
    wg_in = c.gru_H[:, 0:2, :].rearrange("p a n -> p (a n)").rearrange("p (w k n) -> p w k n", w=4, k=KD)
    c.wg = c.sb("wg", [P, 2, 4, KD, DM], F32R, ctx=g)
    c.wg_high, c.wg_low = c.sem("wg_high"), c.sem("wg_low")
    c.wo = c.sb("wo", [P, 5, DM], ctx=g)
    c.gru_stats, c.gru_mv = c.sb("gru_stats", [P, TB, 6], ctx=g), c.sb("gru_mv", [P, TB, 2], ctx=g)
    c.gru_ve, c.gru_rs = c.sb("gru_ve", [P, TB], ctx=g), c.sb("gru_rs", [P, TB], ctx=g)
    c.gru_xhat = c.sb("gru_xhat", [P, TB, DM], ctx=g)
    c.mod_rows = c.sb("mod_rows", [B, 8, DM], ctx=g)
    c.gru_h_in = c.sb("gru_h_in", [P, 2, 512], ctx=g)
    c.gru_hT = c.sb("gru_hT", [P, 2, KD, S], F32R, ctx=g)
    c.gru_tp = c.ps("gru_tp", [P, 2, 512], ctx=g)
    c.gru_tp_ready, c.gru_hT_ready, c.gru_h_low = c.sem("gru_tp_ready"), c.sem("gru_hT_ready"), c.sem("gru_h_low")
    c.gru_stats_ready, c.gru_rstd_ready = c.sem("gru_stats_ready"), c.sem("gru_rstd_ready")
    c.gru_xhat_ready, c.gru_pool_order = c.sem("gru_xhat_ready"), c.sem("gru_pool_order")
    c.gru_w_loaded, c.rows0_loaded, c.rows1_loaded = c.sem("gru_w_loaded"), c.sem("rows0_loaded"), c.sem("rows1_loaded")
    x_first, c.x_loaded = c.sem("x_first"), c.sem("x_loaded")

    with ExitStack() as own:
        wmod = [c.sb(f"wmod{l}", [P, KD, 6 * DM], ctx=own) for l in range(2)]
        cT = c.sb("cT", [P, 2, KD, B], ctx=own)
        sT = c.sb("sT", [P, 2, KD, B], ctx=own)
        rows = c.mod_rows
        colp = c.ps("colp", [P, len(COL_PARTS), KD, B], ctx=own)
        rowp = c.ps("rowp", [P, 4, 512], ctx=own)
        mod_loaded, wmod1_loaded, silu_ready = c.sem("mod_loaded"), c.sem("wmod1_loaded"), c.sem("silu_ready")
        colp_ready, rowp_ready = c.sem("colp_ready"), c.sem("rowp_ready")
        modT_ready = c.sem("modT_ready")
        dve_order, ident_clear = c.sem("dve_order0"), c.sem("ident_clear")

        with nc.Block() as block:

            def load_x(eng, b, sem):
                for h in range(HALVES):
                    at = h * TH + b * TJ
                    eng.dma_start(c.X[:, at:at + TJ, :], d["x"][b, h * TJ * P:(h + 1) * TJ * P, :].rearrange(
                        "(t p) n -> p t n", p=P)).then_inc(sem, 16)

            @block.sync
            def _(sp):
                sp.dma_start(cT[:], d["cT"].rearrange("l (k p) b -> p l k b", p=P)).then_inc(mod_loaded, 16)
                sp.dma_start(c.cols[:], d["cols"]).then_inc(mod_loaded, 16)
                for l, sem in enumerate((mod_loaded, wmod1_loaded)):
                    sp.dma_start(wmod[l][:], d["wmod"][l].rearrange("(k p) n -> p k n", p=P)).then_inc(sem, 16)
                sp.dma_start(wg_in, d["wg"].rearrange("w (k p) n -> p w k n", p=P)).then_inc(c.gru_w_loaded, 16)
                sp.dma_start(c.wo[:, 0:4, :], d["wo0"].rearrange("(k p) n -> p k n", p=P)).then_inc(c.gru_w_loaded, 16)
                r = d["rows"][ROW["b_out"]:ROW["b_out"] + 1, :]
                sp.dma_start(c.wo[:, 4, :], r.broadcast_to([P, DM])).then_inc(c.gru_w_loaded, 16)
                for b in range(1, B):
                    load_x(sp, b, c.x_loaded)

            @block.gpsimd
            def _(pool):
                pool.memset(c.mhalf[:], -0.5)
                pool.memset(c.ident[:], 0.0).then_inc(ident_clear, 1)
                pool.wait_ge(ident_clear, 1)
                pool.affine_select(out=c.ident[:], in_=c.ident[:], compare_op=ALU.not_equal, fill=1.0,
                                   base=0, pattern=[[-1, P]], channel_multiplier=1).then_inc(ident_clear, 1)
                gru_rstd(c, pool, 0)

            @block.scalar
            def _(act):
                load_x(act, 0, x_first)
                act.wait_ge(mod_loaded, 48)
                act.activation(sT[:], cT[:], ACT.Silu).then_inc(silu_ready, 1)
                act.wait_ge(c.gru_w_loaded, 48)
                act.copy(c.wg[:, 0], wg_in).then_inc(c.wg_high, 1)
                act.wait_ge(modT_ready, 1)
                gru_by_feature(c, act, 0)

            @block.tensor
            def _(pe):
                pe.wait_ge(mod_loaded, 48)
                pe.wait_ge(silu_ready, 1)
                for n, (l, j) in enumerate(COL_PARTS):
                    if (l, j) == (1, 3):
                        pe.wait_ge(wmod1_loaded, 16)
                    for m in range(KD):
                        for k in range(KD):
                            at = (j * KD + m) * P
                            last = pe.matmul(colp[:, n, m, :], wmod[l][:, k, at:at + P], sT[:, l, k, :],
                                             start=(k == 0), stop=(k == KD - 1))
                last.then_inc(colp_ready, 1)
                pe.wait_ge(ident_clear, 2)
                gru_turn(c, pe, 0, 0)
                for n in range(4):
                    if n == 1:
                        gru_turn(c, pe, 0, 1)
                    for q in range(2):
                        l, src = (0, (2, 5)[q]) if n == 0 else (1, 2 * (n - 1) + q)
                        for k in range(KD):
                            last = pe.matmul(rowp[0:B, n, q * DM:(q + 1) * DM], sT[:, l, k, :],
                                             wmod[l][:, k, src * DM:(src + 1) * DM], start=(k == 0), stop=(k == KD - 1))
                    last.then_inc(rowp_ready, 1)

            @block.vector
            def _(dve):
                order = Steps(dve, dve_order)
                dve.wait_ge(x_first, 16 * HALVES)
                gru_stats(c, dve, order, 0)
                gru_normalize(c, dve, 0)
                dve.wait_ge(mod_loaded, 48)
                for q, name in enumerate(("bz_f", "bz_b")):
                    dve.tensor_scalar(c.nbz[:, q, :], c.cols[:, COL[name]:COL[name] + KD], -1.0, None, ALU.mult)
                dve.wait_ge(colp_ready, 1)
                for n, (l, j) in enumerate(COL_PARTS):
                    last = dve.tensor_scalar(c.modT[l][:, j * KD:(j + 1) * KD, :], colp[:, n], float(j in (1, 4)), None,
                                             ALU.add)
                last.then_inc(modT_ready, 1)
                dve.wait_ge(c.wg_high, 1)
                low_part(dve, c.wg[:, 1], wg_in, c.wg[:, 0]).then_inc(c.wg_low, 1)
                for n in range(4):
                    gru_h_split(c, dve, 0, n)
                for n in range(4):
                    dve.wait_ge(rowp_ready, n + 1)
                    dve.tensor_copy(rows[:, 2 * n:2 * n + 2, :], rowp[0:B, n, :].rearrange("p (q n) -> p q n", q=2))


def gru(c):
    nc, d = c.nc, c.d
    c.phase = "gru_"
    with ExitStack() as own:
        wg, wo = c.wg, c.wo
        wo_b = c.sb("wo_b", [P, 5, DM], ctx=own)
        hT = c.gru_hT
        Z = c.sb("Z", [P, 2, S], ctx=own)
        A = c.sb("A", [P, 2, S], ctx=own)
        SG = c.sb("SG", [P, 2, S], ctx=own)
        R = c.sb("R", [P, 2, S], ctx=own)
        H = c.gru_H
        gp = c.ps("gp", [P, 4, 512], ctx=own)
        op = c.ps("op", [P, 2, 2, DM], ctx=own)
        out_bank = [op[:, 0], op[:, 1]] + [gp[:, n, :].rearrange("p (q n) -> p q n", q=2) for n in range(2)]
        gp_ready, gates_ready = c.sem("gru_gp_ready"), c.sem("gru_gates_ready")
        scan_ready, wo_ready = c.sem("gru_scan_ready"), c.sem("gru_wo_ready")
        op_ready, op_free = c.sem("gru_op_ready"), c.sem("gru_op_free")
        dve_order, bias_added = c.sem("gru_dve_order"), c.sem("gru_bias_added")

        rows, rows_dram = c.mod_rows, nc.dram_tensor("mod_rows_dram", (B, 8, DM), F32, kind="Internal").ap()
        mag = c.sb("mag", [B, 2, DM], ctx=own)
        sgn = c.sb("sgn", [B, 2, DM], ctx=own)
        rows_order, rows_ready, rows_stored = c.sem("rows_order"), c.sem("rows_ready"), c.sem("rows_stored")

        def clamp_gate(dve, order, gate):
            order.then(dve.tensor_scalar(mag[:], gate, -1.0, None, ALU.mult))
            order.did(dve.scalar_tensor_tensor(mag[:], gate, 0.25, mag[:], ALU.max, ALU.max))
            order.then(dve.tensor_scalar(sgn[:], gate, 0.0, 2.0, ALU.is_ge, ALU.mult))
            order.then(dve.scalar_tensor_tensor(gate, sgn[:], 1.0, mag[:], ALU.subtract, ALU.mult))

        def batch_rows(eng, do_row):
            with eng.Fori(0, B - 1) as b:
                do_row(b, True)
            do_row(B - 1, False)

        with nc.Block() as block:

            @block.sync
            def _(sp):
                sp.wait_ge(rows_ready, 1)
                sp.dma_start(rows_dram, rows[:]).then_inc(rows_stored, 16)
                sp.wait_ge(rows_stored, 16)
                sp.dma_start(c.rows0[:], rows_dram[:, 0:2, :].unsqueeze(0).broadcast_to([P, B, 2, DM])
                             ).then_inc(c.rows0_loaded, 16)
                sp.dma_start(c.w_ffn[:], d["w_ffn"].rearrange("w (k p) n -> p w k n", p=P)).then_inc(c.ffn_w_loaded, 16)
                load_attention_constants(c, sp)
                sp.dma_start(c.rows1[:], rows_dram[:, 2:8, :].unsqueeze(0).broadcast_to([P, B, 6, DM])
                             ).then_inc(c.rows1_loaded, 16)
                sp.wait_ge(c.rows1_loaded, 16)

            @block.gpsimd
            def _(pool):
                def do_row(b, more):
                    if more:
                        gru_rstd(c, pool, b + 1)
                    pool.wait_ge(c.gru_w_loaded, 48)
                    pool.wait_ge(c.rows0_loaded, 16)
                    pool.wait_ge(op_free, b * 4 + 2)
                    ga = c.rows0[:, bass.ds(b, 1), 0, :]
                    pool.tensor_tensor(wo_b[:], wo[:], ga.broadcast_to([P, 5, DM]), ALU.mult).then_inc(wo_ready, 1)
                    c.hold(pool, wo_ready, b + 1)
                    c.hold(pool, c.gru_xhat_ready, b * 2 + 2)
                    for h in range(HALVES):
                        xs = c.X[:, bass.ds(b * TJ + h * TH, TJ), :]
                        pool.tensor_tensor(xs, xs, wo_b[:, 4:5, :].broadcast_to([P, TJ, DM]), ALU.add
                                           ).then_inc(bias_added, 1)

                batch_rows(pool, do_row)

            @block.scalar
            def _(act):

                def do_row(b, more):
                    for u in range(4):
                        dr, m, s = u // 2, u % 2, u % 2
                        bz, bh = COL[("bz_f", "bz_b")[dr]] + m, COL[("bh_f", "bh_b")[dr]] + m
                        act.wait_ge(scan_ready, b * 4 + u + 1)
                        for n in range(2):
                            cs = slice(n * 512, (n + 1) * 512)
                            act.wait_ge(gp_ready, b * 16 + u * 4 + n * 2 + 1)
                            act.activation(Z[:, s, cs], gp[:, 2 * n, :], ACT.Sigmoid, bias=c.cols[:, bz:bz + 1])
                            act.activation(A[:, s, cs], gp[:, 2 * n, :], ACT.Sigmoid, bias=c.nbz[:, dr, m:m + 1],
                                           scale=-1.0).then_inc(gates_ready, 1)
                            act.wait_ge(gp_ready, b * 16 + u * 4 + n * 2 + 2)
                            act.activation(SG[:, s, cs], gp[:, 2 * n + 1, :], ACT.Sigmoid, bias=c.cols[:, bh:bh + 1])
                            act.activation(R[:, s, cs], gp[:, 2 * n + 1, :], ACT.Relu, bias=c.cols[:, bh:bh + 1]
                                           ).then_inc(gates_ready, 1)
                    if more:
                        gru_by_feature(c, act, b + 1)

                act.sem_inc(gates_ready, 4)
                batch_rows(act, do_row)

            @block.tensor
            def _(pe):

                def do_row(b, more):
                    pe.wait_ge(c.gru_h_low, b * 4 + 4)
                    pe.wait_ge(op_free, b * 4 + 2)
                    for u in range(4):
                        dr, m = u // 2, u % 2
                        for n in range(2):
                            for w in range(2):
                                pe.wait_ge(gates_ready, b * 16 + u * 4 + n * 2 + w + 1)
                                for k in range(KD):
                                    last = product3(pe, gp[:, 2 * n + w, :],
                                                    [wg[:, i, 2 * dr + w, k, m * P:(m + 1) * P] for i in range(2)],
                                                    [hT[:, i, k, n * 512:(n + 1) * 512] for i in range(2)],
                                                    start=(k == 0), stop=(k == KD - 1))
                                last.then_inc(gp_ready, 1)
                    if more:
                        gru_turn(c, pe, b + 1, 0)
                    pe.wait_ge(wo_ready, b + 1)
                    pe.wait_ge(scan_ready, b * 4 + 5)
                    for n in range(4):
                        if n >= 2:
                            pe.wait_ge(gates_ready, b * 16 + 16 + n - 1)
                        for q in range(2):
                            t = 2 * n + q
                            for k in range(3):
                                pe.matmul(out_bank[n][:, q, :], H[:, k, t * P:(t + 1) * P], wo_b[:, k, :],
                                          start=(k == 0 and q == 0), stop=False)
                        if more and n == 1:
                            gru_turn(c, pe, b + 1, 1)
                    pe.wait_ge(scan_ready, b * 4 + 6)
                    for n in range(4):
                        for q in range(2):
                            t = 2 * n + q
                            last = pe.matmul(out_bank[n][:, q, :], H[:, 3, t * P:(t + 1) * P], wo_b[:, 3, :],
                                             start=False, stop=(q == 1))
                        last.then_inc(op_ready, 1)

                pe.wait_ge(c.wg_low, 1)
                batch_rows(pe, do_row)

            @block.vector
            def _(dve):
                dve.sem_inc(scan_ready, 2)
                dve.sem_inc(op_free, 2)
                order = Steps(dve, rows_order)
                clamp_gate(dve, order, rows[:, 0:2, :])
                clamp_gate(dve, order, rows[:, 4:8:3, :])
                for j in (3, 6):
                    order.then(dve.tensor_scalar(rows[:, j, :], rows[:, j, :], 1.0, None, ALU.add))
                dve.sem_inc(rows_ready, 1)
                def do_row(b, more):
                    order = Steps(dve, dve_order, b * 16)
                    for u in range(4):
                        s = u % 2
                        dve.wait_ge(gates_ready, 4 + b * 16 + u * 4 + 4)
                        order.then(dve.scalar_tensor_tensor(SG[:, s, :], SG[:, s, :], 0.5, R[:, s, :], ALU.min, ALU.add))
                        order.then(dve.tensor_tensor(SG[:, s, :], SG[:, s, :], Z[:, s, :], ALU.mult))
                        a, v = A[:, s, :], SG[:, s, :]
                        if u >= 2:
                            a, v = a[:, ::-1], v[:, ::-1]
                        dve.tensor_tensor_scan(H[:, u, :], a, v, 0.0, ALU.mult, ALU.add).then_inc(scan_ready, 1)
                        if more and u == 0:
                            dve.wait_ge(c.x_loaded, 16 * (B - 1) * HALVES)
                            gru_stats(c, dve, order, b + 1)
                        if more and u == 1:
                            dve.wait_ge(c.gru_tp_ready, b * 4 + 4)
                            gru_normalize(c, dve, b + 1)
                    dve.wait_ge(bias_added, b * 2 + 2)
                    for n in range(4):
                        if more and n % 2 == 0:
                            gru_h_split(c, dve, b + 1, n)
                            gru_h_split(c, dve, b + 1, n + 1)
                        dve.wait_ge(op_ready, b * 4 + n + 1)
                        xs = c.X[:, bass.ds(b * TJ + (2 * n // TJ * TH + 2 * n % TJ), 2), :]
                        dve.tensor_tensor(xs, out_bank[n], xs, ALU.add).then_inc(op_free, 1)

                batch_rows(dve, do_row)


def ffn(c):
    nc, d = c.nc, c.d
    c.phase = "ffn_"
    CH = TJ * P // 2
    with ExitStack() as own:
        w = c.sb("w", [P, 2, 8, KD, DM], F32R, ctx=own)
        bo = c.sb("bo_rows", [P, DM], ctx=own)
        stats = c.sb("stats", [P, TJ, 6], ctx=own)
        mv = c.sb("mv", [P, TJ, 2], ctx=own)
        ve = c.sb("ve", [P, TJ], ctx=own)
        rs = c.sb("rs", [P, TJ], ctx=own)
        xhat = c.sb("xhat", [P, TJ, DM], ctx=own)
        h_in = c.sb("h_in", [P, KD, TJ * P], ctx=own)
        hT = c.sb("hT", [P, B, 2, KD, TJ * P], F32R, ctx=own)
        c_in = c.sb("cT_state", [P, KD, TJ * P], ctx=own)
        cT = c.sb("cT", [P, 2, KD, TJ * P], F32R, ctx=own)
        G = c.sb("G", [P, 2, 3, KD, CH], ctx=own)
        Y = c.sb("Y", [P, 4, 2, DM], ctx=own)
        tp = c.ps("tp", [P, KD, 512], ctx=own)
        gp = c.ps("gp", [P, 6, 512], ctx=own)
        w_loaded, stats_ready = c.ffn_w_loaded, c.sem("ffn_stats_ready")
        rstd_ready, xhat_ready = c.sem("ffn_rstd_ready"), c.sem("ffn_xhat_ready")
        tp_ready, hT_ready = c.sem("ffn_tp_ready"), c.sem("ffn_hT_ready")
        gp_ready, gates_ready, c_ready = c.sem("ffn_gp_ready"), c.sem("ffn_gates_ready"), c.sem("ffn_c_ready")
        y_ready, tanh_ready = c.sem("ffn_y_ready"), c.sem("ffn_tanh_ready")
        scaled_ready, biased_ready = c.sem("ffn_scaled_ready"), c.sem("ffn_biased_ready")
        w_high, w_low, w_low_pool = c.sem("ffn_w_high"), c.sem("ffn_w_low"), c.sem("ffn_w_low_pool")
        h_low, c_order, y_free = c.sem("ffn_h_low"), c.sem("ffn_c_order"), c.sem("ffn_y_free")
        dve_order, pool_order = c.sem("ffn_dve_order"), c.sem("ffn_pool_order")

        with nc.Block() as block:

            @block.sync
            def _(sp):
                sp.dma_start(bo[:], d["rows"][ROW["bo_ffn"]:ROW["bo_ffn"] + 1, :].broadcast_to([P, DM])).then_inc(w_loaded, 16)

            @block.gpsimd
            def _(pool):

                def rstd(it):
                    c.hold(pool, stats_ready, it + 1)
                    pool.tensor_scalar(ve[:], mv[:, :, 1], EPS, None, ALU.add).then_inc(pool_order, 1)
                    pool.wait_ge(pool_order, it + 1)
                    pool.tensor_tensor(rs[:], ve[:], c.mhalf[:, 0:TJ], ALU.pow).then_inc(rstd_ready, 1)

                rstd(0)
                pool.wait_ge(w_high, 2)
                low_part(pool, w[:, 1, 4:8], c.w_ffn[:, 4:8], w[:, 0, 4:8]).then_inc(w_low_pool, 1)
                for h in range(HALVES):
                    with pool.Fori(0, B - 1) as b:
                        rstd(b + (h * B + 1))
                    if h + 1 < HALVES:
                        rstd((h + 1) * B)
                    for n in range(8):
                        pool.wait_ge(tanh_ready, h * 8 + n + 1)
                        pool.tensor_tensor(Y[:, n % 4], Y[:, n % 4],
                                           c.rows0[:, n // 2, 1:2, :].broadcast_to([P, 2, DM]),
                                           ALU.mult).then_inc(scaled_ready, 1)

            @block.scalar
            def _(act):

                def evacuate(it, b):
                    for k in range(KD):
                        c.hold(act, tp_ready, it * 2 + k + 2)
                        for dst in (hT[:, b, 0, k, :], h_in[:, k, :]):
                            last = act.activation(dst, tp[:, k, :], ACT.Identity,
                                                  bias=c.modT[0][:, 3 * KD + k, bass.ds(b, 1)],
                                                  scale=c.modT[0][:, 4 * KD + k, bass.ds(b, 1)])
                        last.then_inc(hT_ready, 1)

                def gates(it, ch):
                    for g, (name, f) in enumerate((("bf", ACT.Sigmoid), ("bi", ACT.Sigmoid), ("bc", ACT.Tanh))):
                        act.wait_ge(gp_ready, it * 6 + ch * 3 + g + 1)
                        for m in range(KD):
                            col = COL[name] + m
                            last = act.activation(G[:, ch, g, m, :], gp[:, ch * 3 + g, m * CH:(m + 1) * CH], f,
                                                  bias=c.cols[:, col:col + 1])
                    last.then_inc(gates_ready, 1)

                act.wait_ge(w_loaded, 32)
                for n in range(2):
                    act.copy(w[:, 0, 4 * n:4 * n + 4], c.w_ffn[:, 4 * n:4 * n + 4]).then_inc(w_high, 1)
                evacuate(0, 0)
                for h in range(HALVES):
                    with act.Fori(0, B - 1) as b:
                        gates(b + h * B, 0)
                        evacuate(b + (h * B + 1), b + 1)
                        gates(b + h * B, 1)
                    gates(h * B + B - 1, 0)
                    gates(h * B + B - 1, 1)
                    for n in range(8):
                        if n == 5 and h + 1 < HALVES:
                            evacuate((h + 1) * B, 0)
                        act.wait_ge(biased_ready, h * 8 + n + 1)
                        act.activation(Y[:, n % 4], Y[:, n % 4], ACT.Tanh).then_inc(tanh_ready, 1)
                lambda_on_act(c, act)

            @block.tensor
            def _(pe):

                def transposes(it):
                    pe.wait_ge(xhat_ready, it + 1)
                    for k in range(KD):
                        for t in range(TJ):
                            last = pe.transpose(tp[:, k, t * P:(t + 1) * P], xhat[:, t, k * P:(k + 1) * P], c.ident[:])
                        last.then_inc(tp_ready, 1)

                def gates(h, b, ch):
                    pe.wait_ge(h_low, h * B + b + 1)
                    pe.wait_ge(c_ready, h * 10 + b * 2 + ch + 1)
                    for g in range(3):
                        for m in range(KD):
                            out = gp[:, ch * 3 + g, m * CH:(m + 1) * CH]
                            for k in range(KD):
                                product3(pe, out, [w[:, i, 2 * g, k, m * P:(m + 1) * P] for i in range(2)],
                                         [hT[:, b, i, k, ch * CH:(ch + 1) * CH] for i in range(2)],
                                         start=(k == 0), stop=False)
                            for k in range(KD):
                                last = product3(pe, out, [w[:, i, 2 * g + 1, k, m * P:(m + 1) * P] for i in range(2)],
                                                [cT[:, i, k, ch * CH:(ch + 1) * CH] for i in range(2)],
                                                start=False, stop=(k == KD - 1))
                        last.then_inc(gp_ready, 1)

                pe.sem_inc(tp_ready, 1)
                transposes(0)
                pe.wait_ge(w_low, 1)
                pe.wait_ge(w_low_pool, 1)
                for h in range(HALVES):
                    with pe.Fori(0, B - 1) as b:
                        gates(h, b, 0)
                        transposes(b + (h * B + 1))
                        gates(h, b, 1)
                    gates(h, B - 1, 0)
                    gates(h, B - 1, 1)
                    pe.wait_ge(c_ready, h * 10 + 10)
                    for n in range(8):
                        if n == 4 and h + 1 < HALVES:
                            transposes((h + 1) * B)
                        if n >= 6:
                            pe.wait_ge(biased_ready, h * 8 + n - 5)
                        for q in range(2):
                            out = gp[:, n % 6, q * DM:(q + 1) * DM]
                            b, t = n // 2, 2 * (n % 2) + q
                            for k in range(KD):
                                product3(pe, out, [hT[:, b, i, k, t * P:(t + 1) * P] for i in range(2)],
                                         [w[:, i, 6, k, :] for i in range(2)], start=(k == 0), stop=False)
                            for k in range(KD):
                                last = product3(pe, out, [cT[:, i, k, t * P:(t + 1) * P] for i in range(2)],
                                                [w[:, i, 7, k, :] for i in range(2)], start=False, stop=(k == KD - 1))
                        last.then_inc(y_ready, 1)

            @block.vector
            def _(dve):

                def layernorm(it):
                    for t in range(TJ):
                        dve.bn_stats(stats[:, t, :], c.X[:, it * TJ + t, :]).then_inc(dve_order, 1)
                    c.hold(dve, dve_order, it * TJ + TJ)
                    for t in range(TJ):
                        last = dve.bn_aggr(mv[:, t, :], stats[:, t, :])
                    last.then_inc(stats_ready, 1)
                    dve.wait_ge(rstd_ready, it + 1)
                    dve.wait_ge(tp_ready, it * 2 + 1)
                    for t in range(TJ):
                        last = dve.tensor_scalar(xhat[:, t, :], c.X[:, it * TJ + t, :], mv[:, t, 0:1],
                                                 rs[:, t:t + 1], ALU.subtract, ALU.mult)
                    last.then_inc(xhat_ready, 1)

                def update(h, b, ch):
                    order = Steps(dve, c_order, h * PER_HALF + 4 + b * 6 + ch * 3)
                    cols = slice(ch * CH, (ch + 1) * CH)
                    state = c_in[:, :, cols]
                    dve.wait_ge(gates_ready, h * 2 * B + b * 2 + ch + 1)
                    dve.tensor_tensor(G[:, ch, 2], G[:, ch, 1], G[:, ch, 2], ALU.mult)
                    order.then(dve.tensor_tensor(state, G[:, ch, 0], state, ALU.mult))
                    order.then(dve.tensor_tensor(state, state, G[:, ch, 2], ALU.add))
                    order.then(dve.tensor_copy(cT[:, 0, :, cols], state))
                    low_part(dve, cT[:, 1, :, cols], state, cT[:, 0, :, cols]).then_inc(c_ready, 1)

                def h_split(h, b):
                    dve.wait_ge(hT_ready, h * 2 * B + 2 * b + 2)
                    low_part(dve, hT[:, b, 1], h_in[:], hT[:, b, 0]).then_inc(h_low, 1)

                PER_HALF = 4 + 6 * B

                def add_bias(h, n):
                    dve.wait_ge(y_ready, h * 8 + n + 1)
                    dve.wait_ge(y_free, h * 8 + n + 1)
                    dve.tensor_tensor(Y[:, n % 4], gp[:, n % 6, :].rearrange("p (q n) -> p q n", q=2),
                                      bo[:].unsqueeze(1).broadcast_to([P, 2, DM]), ALU.add).then_inc(biased_ready, 1)

                def finish(h, n):
                    xs = c.X[:, h * TH + 2 * n:h * TH + 2 * n + 2, :]
                    dve.wait_ge(scaled_ready, h * 8 + n + 1)
                    dve.tensor_tensor(xs, xs, Y[:, n % 4], ALU.add).then_inc(y_free, 1)

                dve.sem_inc(y_free, 4)
                layernorm(0)
                dve.wait_ge(w_high, 1)
                low_part(dve, w[:, 1, 0:4], c.w_ffn[:, 0:4], w[:, 0, 0:4]).then_inc(w_low, 1)
                for h in range(HALVES):
                    order = Steps(dve, c_order, h * PER_HALF)
                    for ch in range(2):
                        cols = slice(ch * CH, (ch + 1) * CH)
                        order.then(dve.tensor_copy(c_in[:, :, cols], c.cols[:, COL["in_c"]:COL["in_c"] + KD].unsqueeze(2)
                                                   .broadcast_to([P, KD, CH])))
                        order.then(dve.tensor_copy(cT[:, 0, :, cols], c_in[:, :, cols]))
                        low_part(dve, cT[:, 1, :, cols], c_in[:, :, cols], cT[:, 0, :, cols]).then_inc(c_ready, 1)
                    if h == 0:
                        h_split(0, 0)
                    with dve.Fori(0, B - 1) as b:
                        layernorm(b + (h * B + 1))
                        update(h, b, 0)
                        h_split(h, b + 1)
                        update(h, b, 1)
                    update(h, B - 1, 0)
                    update(h, B - 1, 1)
                    if h + 1 < HALVES:
                        layernorm((h + 1) * B)
                    for n in range(8):
                        add_bias(h, n)
                        if n >= 2:
                            finish(h, n - 2)
                        if n == 6 and h + 1 < HALVES:
                            h_split(h + 1, 0)
                    if h + 1 == HALVES:
                        lambda_on_dve(c, dve)
                    finish(h, 6)
                    finish(h, 7)


H_, D_, DV = 16, 8, 16
NH = 2 * H_
GB = 16
G8 = P // GB


def attention_constants(c):
    c.w_qk = c.sb("w_qk", [P, KD, 2 * DM], ctx=c.layer1)
    c.w_v = c.sb("w_v", [P, KD, DM], ctx=c.layer1)
    c.w_o = c.sb("w_o", [P, KD, DM], ctx=c.layer1)
    c.bo1 = c.sb("bo1", [P, DM], ctx=c.layer1)
    c.maskK = c.sb("maskK", [P, 4], ctx=c.layer1)
    c.maskV = c.sb("maskV", [P, G8], ctx=c.layer1)
    c.combine = c.sb("combine", [P, 2, 64], ctx=c.layer1)
    c.at_loaded, c.lam_order, c.lam_exp = c.sem("at_loaded"), c.sem("lam_order"), c.sem("lam_exp")
    c.credit = {n: c.sem("attn_" + n) for n in ("norm1_ready", "cp_ready")}


def load_attention_constants(c, sp):
    d = c.d
    for dst, src in ((c.w_qk, d["w_qk"].rearrange("(k p) n -> p k n", p=P)),
                     (c.w_v, d["w_v"].rearrange("(k p) n -> p k n", p=P)),
                     (c.w_o, d["w_o"].rearrange("(k p) n -> p k n", p=P)),
                     (c.bo1, d["rows"][ROW["bo_attn"]:ROW["bo_attn"] + 1, :].broadcast_to([P, DM])),
                     (c.maskK, d["maskK"]), (c.maskV, d["maskV"]), (c.combine, d["combine"])):
        sp.dma_start(dst[:], src).then_inc(c.at_loaded, 16)
    sp.dma_start(c.lam_in[:].rearrange("p a b n -> p (a b n)"),
                 d["lam"].rearrange("a n -> (a n)").unsqueeze(0).broadcast_to([P, 4 * D_])).then_inc(c.at_loaded, 16)


def lambda_on_act(c, act):
    act.wait_ge(c.lam_order, 2)
    act.activation(c.lam[:, 2:4], c.lam[:, 0:2], ACT.Exp).then_inc(c.lam_exp, 1)


def lambda_on_dve(c, dve):
    order = Steps(dve, c.lam_order)
    dve.sem_inc(c.credit["norm1_ready"], 2)
    dve.sem_inc(c.credit["cp_ready"], 2)
    dve.wait_ge(c.at_loaded, 16 * 8)
    order.then(dve.tensor_tensor(c.lam_in[:, 0], c.lam_in[:, 0], c.lam_in[:, 1], ALU.mult))
    order.then(dve.tensor_reduce(c.lam[:, 0:2], c.lam_in[:, 0], AX.X, ALU.add))
    dve.wait_ge(c.lam_exp, 1)
    order.then(dve.scalar_tensor_tensor(c.lam[:, 0:1], c.lam[:, 3:4], LAMBDA_INIT, c.lam[:, 2:3],
                                        ALU.subtract, ALU.subtract))
    dve.tensor_scalar(c.combine[:, 1, :], c.combine[:, 1, :], c.lam[:, 0:1], None, ALU.mult)


def attention(c, h, own):
    nc = c.nc
    c.phase = "at_"
    AREA = TH * DM
    area0 = c.sb("area0", [P, AREA], ctx=own)
    area1 = c.sb("area1", [P, 2 * AREA], ctx=own)
    area2 = c.sb("area2", [P, 2 * AREA], ctx=own)
    tok = area0[:].rearrange("p (k t r g) -> p k t r g", k=KD, t=TJ, r=B)
    OT = area0[:].rearrange("p (a r g j) -> p a r g j", a=H_, r=4, g=GB)
    QK = area1[:].rearrange("p (n t d) -> p n t d", n=2 * NH, t=TH)
    VS = area1[:, 0:AREA].rearrange("p (u G n) -> p u G n", u=2, G=G8)
    VT = area1[:, AREA:].rearrange("p (g t d) -> p g t d", g=GB, t=TH)
    PN = area1[:, 0:AREA // 2].rearrange("p (s k n a) -> p s k n a", s=2, k=2, a=H_)
    attT = area1[:, AREA // 2:AREA * 3 // 4].rearrange("p (s t a) -> p s t a", s=2, t=TH)
    O = area1[:, AREA * 3 // 4:AREA].rearrange("p (s n) -> p s n", s=2)
    OK = area1[:, 0:AREA].rearrange("p (u G a d) -> p u G a d", u=2, G=G8, a=H_)
    QT = area2[:, 0:AREA].rearrange("p (g n) -> p g n", n=NH)
    KT = area2[:, AREA:].rearrange("p (g n) -> p g n", n=NH)
    oT = area2[:, 0:AREA].rearrange("p (k t r n g) -> p k t r n g", k=KD, t=4, r=4, g=2)
    SQ = area2[:, AREA:].rearrange("p (u n) -> p u n", u=2)

    stats = c.sb("stats", [P, 2, TJ, 6], ctx=own)
    mv = c.sb("mv", [P, 2, TJ, 2], ctx=own)
    ve = c.sb("ve", [P, 2, TJ], ctx=own)
    rs = c.sb("rs", [P, 2, TJ], ctx=own)
    xhat = area2[:, 0:TJ * DM].rearrange("p (t n) -> p t n", t=TJ)
    Kbd = c.sb("Kbd", [P, 2, G8, P], ctx=own)
    Qs = c.sb("Qs", [P, 2, G8, NH], ctx=own)
    Vbd = c.sb("Vbd", [P, 2, TH, P], ctx=own)
    T = c.sb("T", [P, 2, 4 * G8, NH], ctx=own)
    mx = c.sb("mx", [P, 2, 4 * G8], ctx=own)
    Z = c.sb("Z", [P, 2, 2, 4 * G8], ctx=own)
    ss = c.sb("ss", [P, 2, P], ctx=own)
    rr = c.sb("rr", [P, 2, P], ctx=own)
    work = c.ps("work", [P, 6, 512], ctx=own)
    tp = c.ps("tp", [P, KD, 512], ctx=own)
    SC = work[:, 0:4, 0:G8 * NH]
    CP = [work[:, 4, 0:4 * 64], tp[:, 0, 0:4 * 64]]
    PV = [work[:, 5], tp[:, 1]]

    QK0, HD0, V0, VT0, O0, F0, JOBS = 0, 16, 32, 40, 48, 56, 72
    F = [range(F0 + 8 * u, F0 + 8 * u + 4) for u in range(2)]
    PR = [range(F0 + 8 * u + 4, F0 + 8 * u + 8) for u in range(2)]
    by_act = [n < HD0 or (n % 2 == 0 and n < F0) or n in F[0] or n in F[1] for n in range(JOBS)]
    ACTS, DVES = sum(by_act), JOBS - sum(by_act)

    def emptied(n):
        return sum(1 for m in range(n + 1) if by_act[m] == by_act[n])

    sem = lambda n: c.sem("attn_" + n)
    stats_ready, rstd_ready = sem("stats_ready"), sem("rstd_ready")
    xn_ready, h1_ready, xhat_ready = sem("xn_ready"), sem("h1_ready"), sem("xhat_ready")
    bias_added = sem("bias_added")
    tp_ready, hT_ready = sem("tp_ready"), sem("hT_ready")
    full, empty_a, empty_d = sem("bank_full"), sem("bank_empty_act"), sem("bank_empty_dve")
    kbd_ready, q_ready, vbd_ready = sem("kbd_ready"), sem("q_ready"), sem("vbd_ready")
    s_ready, s_free, t_ready, e_ready, rz_ready = sem("s_ready"), sem("s_free"), sem("t_ready"), sem("e_ready"), sem("rz_ready")
    norm0_ready, norm1_ready, cp_ready = sem("norm0_ready"), c.credit["norm1_ready"], c.credit["cp_ready"]
    att_ready, pv_ready, o_ready = sem("att_ready"), sem("pv_ready"), sem("o_ready")
    padded, o_copied, o_turned = sem("padded"), sem("o_copied"), sem("o_turned")
    sq_ready, ss_ready, rr_ready, ok_ready = sem("sq_ready"), sem("ss_ready"), sem("rr_ready"), sem("ok_ready")
    dve_order, pool_order, tail_order = sem("dve_order"), sem("pool_order"), sem("tail_order")

    def emptied_by(n, hh):
        return (empty_a, hh * ACTS + emptied(n)) if by_act[n] else (empty_d, hh * DVES + emptied(n))

    def emptied_wait(eng, n, hh):
        eng.wait_ge(*emptied_by(n, hh))

    def rounds(eng, do_round):
        with eng.Fori(0, GB // 2 - 1) as i2:
            for s in range(2):
                do_round(i2 * 2 + s, s, True)
        for s in range(2):
            do_round(GB - 2 + s, s, False)

    LN = [(0, 0), (1, 0), (0, 1), (1, 1), (0, 2), (1, 2), (0, 3), (1, 3)]

    with nc.Block() as block:

        def empty(n, copy):
            bank = work[:, n % 6, :]
            if n < V0:
                q, j = ((QT, n - HD0) if n < HD0 + 8 else (KT, n - HD0 - 8))
                return copy(q[:, :, 4 * j:4 * j + 4].rearrange("p g n -> p n g"),
                            bank.rearrange("p (n g) -> p n g", n=4))
            if n < VT0:
                u, G = (n - V0) // 4, 2 * ((n - V0) % 4)
                return copy(VS[:, u, G:G + 2, :], bank.rearrange("p (G n) -> p G n", G=2))
            if n < O0:
                u, d0 = (n - VT0) // 4, 4 * ((n - VT0) % 4)
                v = bank.rearrange("p (d r g j) -> p d r g j", d=4, r=2, g=GB)
                for r in range(2):
                    at = 8 * u + 4 * r
                    last = copy(VT[:, :, at:at + 4, d0:d0 + 4].rearrange("p g j d -> p d g j"), v[:, :, r])
                return last
            if n < F0:
                u, a = (n - O0) // 4, 4 * ((n - O0) % 4)
                return copy(OK[:, u, :, a:a + 4, :].rearrange("p G a d -> p a G d"),
                            bank.rearrange("p (a G d) -> p a G d", a=4, G=G8))
            u, k, g2 = (n - F0) // 8, (n - F0) // 2 % 2, (n - F0) % 2
            return copy(oT[:, k, :, 2 * u:2 * u + 2, :, g2], bank.rearrange("p (t r n) -> p t r n", t=4, r=2))

        @block.gpsimd
        def _(pool):
            order = Steps(pool, pool_order, h * 8)

            def rstd(n):
                kind, b = LN[n]
                c.hold(pool, stats_ready, h * 8 + n + 1)
                order.then(pool.tensor_scalar(ve[:, kind], mv[:, kind, :, 1], EPS, None, ALU.add))
                pool.tensor_tensor(rs[:, kind], ve[:, kind], c.mhalf[:, 0:TJ], ALU.pow).then_inc(rstd_ready, 1)

            for n in range(8):
                rstd(n)

            for b in range(B):
                part = c.H1[:, b * TJ:(b + 1) * TJ, :]
                pool.wait_ge(xhat_ready, h * B + b + 1)
                pool.tensor_tensor(part, part, c.bo1[:].unsqueeze(1).broadcast_to([P, TJ, DM]),
                                   ALU.add).then_inc(bias_added, 1)

            def spread_v(i, s):
                pool.tensor_tensor(Vbd[:, s].rearrange("p t (G d) -> p t G d", d=DV),
                                   VT[:, bass.ds(i, 1), :, :].rearrange("p g t d -> p (g t) d").unsqueeze(2).broadcast_to([P, TH, G8, DV]),
                                   c.maskV[:].unsqueeze(1).unsqueeze(3).broadcast_to([P, TH, G8, DV]),
                                   ALU.mult).then_inc(vbd_ready, 1)

            emptied_wait(pool, O0 - 2, h)
            c.hold(pool, *emptied_by(O0 - 1, h))
            pool.memset(attT, 0.0).then_inc(padded, 1)
            for i in range(2):
                spread_v(i, i)

            def normalize(i, s):
                pool.wait_ge(rz_ready, h * GB + i + 1)
                pool.wait_ge(cp_ready, h * GB + i + 1)
                pool.tensor_tensor(PN[:, s, 1], T[:, s, :, H_:NH],
                                   Z[:, s, 1, :].unsqueeze(2).broadcast_to([P, 4 * G8, H_]),
                                   ALU.mult).then_inc(norm1_ready, 1)

            def do_round(i, s, more):
                if more or s == 0:
                    normalize(i + 1, 1 - s)
                if more:
                    pool.wait_ge(pv_ready, h * GB + i + 1)
                    spread_v(i + 2, s)

            normalize(0, 0)
            rounds(pool, do_round)

        @block.scalar
        def _(act):

            def to_hT(b):
                for k in range(KD):
                    act.wait_ge(tp_ready, h * 2 * B + 2 * b + k + 1)
                    g, o = COL["ln1_g"] + k, COL["ln1_b"] + k
                    act.activation(tok[:, k, :, b, :], tp[:, k, :].rearrange("p (t g) -> p t g", t=TJ), ACT.Identity,
                                   bias=c.cols[:, o:o + 1], scale=c.cols[:, g:g + 1]).then_inc(hT_ready, 1)

            def copy(out, in_):
                return act.copy(out, in_)

            for b in range(B):
                to_hT(b)
                for t in range(TJ):
                    n = QK0 + b * TJ + t
                    act.wait_ge(full, h * JOBS + n + 1)
                    copy(QK[:, :, n, :], work[:, n % 6, :].rearrange("p (n d) -> p n d", d=D_)).then_inc(empty_a, 1)
            for n in range(HD0, O0):
                if by_act[n]:
                    act.wait_ge(full, h * JOBS + n + 1)
                    empty(n, copy).then_inc(empty_a, 1)

            def take_q(i, s):
                c.hold(act, empty_d, h * DVES + emptied(V0 - 1))
                copy(Qs[:, s], QT[:, bass.ds(i * G8, G8), :]).then_inc(q_ready, 1)

            for i in range(2):
                take_q(i, i)

            def exponent(i, s):
                act.wait_ge(t_ready, h * GB + i + 1)
                act.activation(T[:, s], T[:, s], ACT.Exp).then_inc(e_ready, 1)

            def take_att(i, s):
                act.wait_ge(cp_ready, h * GB + i + 3)
                copy(attT[:, s, :, 0:H_], CP[s].rearrange("p (t a) -> p t a", a=H_)).then_inc(att_ready, 1)

            def do_round(i, s, more):
                if more:
                    c.hold(act, s_ready, h * GB + i + 1)
                    take_q(i + 2, s)
                if more or s == 0:
                    exponent(i + 1, 1 - s)
                act.wait_ge(pv_ready, h * GB + i + 1)
                copy(O[:, s], PV[s]).then_inc(o_copied, 1)
                if more or s == 0:
                    take_att(i + 1, 1 - s)
                c.hold(act, o_turned, h * GB + i + 1)
                copy(OT[:, :, :, bass.ds(i, 1), :].rearrange("p a r g j -> p (r g) j a"),
                     PV[s].rearrange("p (r j a) -> p r j a", r=4, j=4)[:, :, :, 0:H_]).then_inc(o_ready, 1)

            exponent(0, 0)
            act.wait_ge(padded, h + 1)
            take_att(0, 0)
            rounds(act, do_round)
            def root(u):
                act.wait_ge(ss_ready, h * 2 + u + 1)
                act.activation(rr[:, u], ss[:, u], ACT.Sqrt).then_inc(rr_ready, 1)

            def empty_f(u):
                for n in F[u]:
                    act.wait_ge(full, h * JOBS + n + 1)
                    empty(n, copy).then_inc(empty_a, 1)

            for u in range(2):
                for n in range(O0 + 4 * u, O0 + 4 * u + 4):
                    if by_act[n]:
                        act.wait_ge(full, h * JOBS + n + 1)
                        empty(n, copy).then_inc(empty_a, 1)
                emptied_wait(act, O0 + 4 * u + 2, h)
                emptied_wait(act, O0 + 4 * u + 3, h)
                act.activation(SQ[:, u], OK[:, u].rearrange("p G a d -> p (G a d)"), ACT.Square).then_inc(sq_ready, 1)
                if u == 0:
                    root(0)
            empty_f(0)
            root(1)
            empty_f(1)

        @block.tensor
        def _(pe):

            def bank_free(n):
                if n >= 6:
                    emptied_wait(pe, n - 6, h)

            for b in range(B):
                pe.wait_ge(xhat_ready, h * B + b + 1)
                if b:
                    pe.wait_ge(hT_ready, h * 2 * B + 2 * b)
                for k in range(KD):
                    for t in range(TJ):
                        last = pe.transpose(tp[:, k, t * P:(t + 1) * P], xhat[:, t, k * P:(k + 1) * P], c.ident[:])
                    last.then_inc(tp_ready, 1)
                pe.wait_ge(hT_ready, h * 2 * B + 2 * b + 2)
                for t in range(TJ):
                    n = QK0 + b * TJ + t
                    bank_free(n)
                    for k in range(KD):
                        last = pe.matmul(work[:, n % 6, :], tok[:, k, t, b, :], c.w_qk[:, k, :],
                                         start=(k == 0), stop=(k == KD - 1))
                    last.then_inc(full, 1)
            emptied_wait(pe, HD0 - 1, h)
            for n in range(HD0, V0):
                bank_free(n)
                for q in range(4):
                    hd = 4 * (n - HD0) + q
                    last = pe.transpose(work[:, n % 6, q * P:(q + 1) * P], QK[:, hd].rearrange("p t d -> p (t d)"), c.ident[:])
                last.then_inc(full, 1)
            eight = tok.rearrange("p k t (u r) (n g) -> p k t u (r n) g", u=2, g=2)
            for n in range(V0, VT0):
                u, G = (n - V0) // 4, 2 * ((n - V0) % 4)
                bank_free(n)
                for q in range(2):
                    for k in range(KD):
                        last = pe.matmul(work[:, n % 6, q * DM:(q + 1) * DM], eight[:, k, (G + q) % 4, u, :, (G + q) // 4],
                                         c.w_v[:, k, :], start=(k == 0), stop=(k == KD - 1))
                last.then_inc(full, 1)
            for n in range(VT0, O0):
                u, d0 = (n - VT0) // 4, 4 * ((n - VT0) % 4)
                if n in (VT0, VT0 + 4):
                    emptied_wait(pe, V0 + 4 * u + 2, h)
                    emptied_wait(pe, V0 + 4 * u + 3, h)
                bank_free(n)
                v = VS[:, u].rearrange("p G (n d) -> p (G n) d", d=DV)
                for q in range(4):
                    last = pe.transpose(work[:, n % 6, q * P:(q + 1) * P], v[:, :, d0 + q], c.ident[:])
                last.then_inc(full, 1)
            emptied_wait(pe, O0 - 2, h)
            emptied_wait(pe, O0 - 1, h)

            def scores(i, s):
                pe.wait_ge(kbd_ready, h * GB + i + 1)
                c.hold(pe, q_ready, h * GB + i + 1)
                for g in range(G8):
                    for q in range(4):
                        rows = slice(32 * q, 32 * q + 32)
                        j, g2 = g // 2, g % 2
                        last = pe.matmul(SC[NH * j:NH * (j + 1), q, g2 * P:(g2 + 1) * P], Qs[rows, s, g, :],
                                         Kbd[rows, s, g, :], start=True, stop=True)
                last.then_inc(s_ready, 1)

            def combine(i, s):
                pe.wait_ge(norm0_ready, h * GB + i + 1)
                pe.wait_ge(norm1_ready, h * GB + i + 3)
                for q in range(4):
                    for g2 in range(2):
                        for kind in range(2):
                            at = 4 * (2 * q + g2)
                            last = pe.matmul(CP[s][64 * g2:64 * g2 + 64, q * 64:(q + 1) * 64],
                                             PN[:, s, kind, at:at + 4, :].rearrange("p t n -> p (t n)"),
                                             c.combine[:, kind, :], start=(kind == 0), stop=(kind == 1))
                last.then_inc(cp_ready, 1)

            def do_round(i, s, more):
                pe.wait_ge(vbd_ready, h * GB + i + 1)
                pe.wait_ge(att_ready, h * GB + i + 1)
                for t in range(TH):
                    r, j = t // 4, t % 4
                    last = pe.matmul(PV[s][NH * j:NH * (j + 1), r * P:(r + 1) * P], attT[:, s, t, :], Vbd[:, s, t, :],
                                     start=True, stop=True)
                last.then_inc(pv_ready, 1)
                if more:
                    pe.wait_ge(s_free, h * GB + i + 2)
                    scores(i + 2, s)
                if more or s == 0:
                    combine(i + 1, 1 - s)
                pe.wait_ge(o_copied, h * GB + i + 1)
                for r in range(4):
                    last = pe.transpose(PV[s][:, r * P:(r + 1) * P], O[:, s, r * P:(r + 1) * P], c.ident[:])
                last.then_inc(o_turned, 1)

            scores(0, 0)
            pe.wait_ge(s_free, h * GB + 1)
            scores(1, 1)
            combine(0, 0)
            rounds(pe, do_round)
            pe.wait_ge(o_ready, h * GB + GB)
            for n in range(O0, F0):
                u, a = (n - O0) // 4, 4 * ((n - O0) % 4)
                if n >= O0 + 6:
                    bank_free(n)
                for q in range(4):
                    last = pe.transpose(work[:, n % 6, q * P:(q + 1) * P],
                                        OT[:, a + q, 2 * u:2 * u + 2].rearrange("p r g j -> p (r g j)"), c.ident[:])
                last.then_inc(full, 1)
            for u in range(2):
                pe.wait_ge(ok_ready, h * 2 + u + 1)
                for n in F[u]:
                    k, G = (n - F0) // 2 % 2, 4 * ((n - F0) % 2)
                    bank_free(n)
                    for q in range(4):
                        last = pe.transpose(work[:, n % 6, q * P:(q + 1) * P],
                                            OK[:, u, G + q, 8 * k:8 * k + 8, :].rearrange("p a d -> p (a d)"), c.ident[:])
                    last.then_inc(full, 1)
                emptied_wait(pe, F[u][3], h)
                for n in PR[u]:
                    bank_free(n)
                    for q in range(2):
                        t = 8 * u + 2 * (n - PR[u][0]) + q
                        for k in range(KD):
                            o = oT[:, k, t % 4, t // 4].rearrange("p n g -> p (n g)")
                            last = pe.matmul(work[:, n % 6, q * DM:(q + 1) * DM], o, c.w_o[:, k, :],
                                             start=(k == 0), stop=(k == KD - 1))
                    last.then_inc(full, 1)

        @block.vector
        def _(dve):
            order = Steps(dve, dve_order, h * (8 + 2 * GB))

            def layernorm(n):
                kind, b = LN[n]
                if kind == 1:
                    dve.wait_ge(h1_ready, h * B + b + 1)
                src = [c.X[:, h * TH + (b * TJ + t), :] if kind == 0 else c.H1[:, b * TJ + t, :] for t in range(TJ)]
                for t in range(TJ):
                    last = dve.bn_stats(stats[:, kind, t, :], src[t])
                c.hold(dve, dve_order, order.did(last))
                for t in range(TJ):
                    last = dve.bn_aggr(mv[:, kind, t, :], stats[:, kind, t, :])
                last.then_inc(stats_ready, 1)
                if kind == 0:
                    dst = [c.H1[:, b * TJ + t, :] for t in range(TJ)]
                    c.hold(dve, stats_ready, h * 8 + n + 1)
                    for t in range(TJ):
                        last = dve.scalar_tensor_tensor(dst[t], src[t], mv[:, kind, t, 0:1], c.rows1[:, b, 1, :],
                                                        ALU.subtract, ALU.mult)
                    last.then_inc(xn_ready, 1)
                    dve.wait_ge(rstd_ready, h * 8 + n + 1)
                    dve.wait_ge(xn_ready, h * B + b + 1)
                    for t in range(TJ):
                        last = dve.scalar_tensor_tensor(dst[t], dst[t], rs[:, kind, t:t + 1], c.rows1[:, b, 0, :],
                                                        ALU.mult, ALU.add)
                    last.then_inc(h1_ready, 1)
                    return
                dve.wait_ge(rstd_ready, h * 8 + n + 1)
                if b:
                    dve.wait_ge(tp_ready, h * 2 * B + 2 * b)
                for t in range(TJ):
                    last = dve.tensor_scalar(xhat[:, t, :], src[t], mv[:, kind, t, 0:1], rs[:, kind, t:t + 1],
                                             ALU.subtract, ALU.mult)
                last.then_inc(xhat_ready, 1)

            for n in range(8):
                layernorm(n)
            for n in range(HD0, O0):
                if not by_act[n]:
                    dve.wait_ge(full, h * JOBS + n + 1)
                    empty(n, dve.tensor_copy).then_inc(empty_d, 1)

            def spread_k(i, s):
                dve.tensor_tensor(Kbd[:, s].rearrange("p g (t n) -> p g t n", t=4),
                                  KT[:, bass.ds(i * G8, G8), :].unsqueeze(2).broadcast_to([P, G8, 4, NH]),
                                  c.maskK[:].unsqueeze(1).unsqueeze(3).broadcast_to([P, G8, 4, NH]),
                                  ALU.mult).then_inc(kbd_ready, 1)

            emptied_wait(dve, V0 - 2, h)
            for i in range(2):
                spread_k(i, i)

            def do_round(i, s, more):
                flat = T[:, s].rearrange("p (r g) n -> p r (g n)", r=4)
                at = h * (8 + 2 * GB) + 8 + 2 * i
                dve.wait_ge(s_ready, h * GB + i + 1)
                dve.wait_ge(norm1_ready, h * GB + i + 1)
                dve.tensor_scalar(flat, SC, 0.0, -FMAX, ALU.min, ALU.max).then_inc(dve_order, 1)
                dve.wait_ge(dve_order, at + 1)
                dve.scalar_tensor_tensor(flat, SC, 0.0, flat, ALU.max, ALU.add).then_inc(s_free, 1)
                dve.wait_ge(s_free, h * GB + i + 1)
                dve.tensor_reduce(mx[:, s], T[:, s], AX.X, ALU.max).then_inc(dve_order, 1)
                dve.wait_ge(dve_order, at + 2)
                dve.tensor_scalar(mx[:, s], mx[:, s], FMAX, None, ALU.min).then_inc(c.clamped, 1)
                dve.wait_ge(c.clamped, h * GB + i + 1)
                dve.scalar_tensor_tensor(T[:, s], T[:, s], FMAX, mx[:, s].unsqueeze(2).broadcast_to([P, 4 * G8, NH]),
                                         ALU.min, ALU.subtract).then_inc(t_ready, 1)
                if more:
                    spread_k(i + 2, s)
                dve.wait_ge(e_ready, h * GB + i + 1)
                dve.tensor_reduce(Z[:, s, 0], T[:, s], AX.X, ALU.add).then_inc(c.summed, 1)
                dve.wait_ge(c.summed, h * GB + i + 1)
                dve.reciprocal(Z[:, s, 1], Z[:, s, 0]).then_inc(rz_ready, 1)
                dve.wait_ge(rz_ready, h * GB + i + 1)
                dve.wait_ge(cp_ready, h * GB + i + 1)
                dve.tensor_tensor(PN[:, s, 0], T[:, s, :, 0:H_],
                                  Z[:, s, 1, :].unsqueeze(2).broadcast_to([P, 4 * G8, H_]),
                                  ALU.mult).then_inc(norm0_ready, 1)

            rounds(dve, do_round)
            tail = Steps(dve, tail_order, h * 4)
            for u in range(2):
                for n in range(O0 + 4 * u, O0 + 4 * u + 4):
                    if not by_act[n]:
                        dve.wait_ge(full, h * JOBS + n + 1)
                        empty(n, dve.tensor_copy).then_inc(empty_d, 1)
                dve.wait_ge(sq_ready, h * 2 + u + 1)
                tail.then(dve.tensor_reduce(ss[:, u], SQ[:, u].rearrange("p (n d) -> p n d", d=DV), AX.X, ALU.add))
                dve.tensor_scalar(ss[:, u], ss[:, u], 1.0 / DV, EPS, ALU.mult, ALU.add).then_inc(ss_ready, 1)
                dve.wait_ge(rr_ready, h * 2 + u + 1)
                tail.then(dve.reciprocal(rr[:, u], rr[:, u]))
                o = OK[:, u].rearrange("p G a d -> p (G a) d")
                dve.scalar_tensor_tensor(o, o, 1.0 - LAMBDA_INIT, rr[:, u].unsqueeze(2).broadcast_to([P, P, DV]),
                                         ALU.mult, ALU.mult).then_inc(ok_ready, 1)
            dve.wait_ge(bias_added, h * B + B)
            for u in range(2):
                for n in PR[u]:
                    m = 8 * u + 2 * (n - PR[u][0])
                    dve.wait_ge(full, h * JOBS + n + 1)
                    dve.tensor_tensor(c.H1[:, m:m + 2, :], c.H1[:, m:m + 2, :],
                                      work[:, n % 6, :].rearrange("p (q n) -> p q n", q=2), ALU.add).then_inc(empty_d, 1)


FF = 1024


def mlp(c, h, own):
    nc, d = c.nc, c.d
    c.phase = "ml_"
    MF = FF // P
    w1 = c.sb("w1", [P, 2, KD, FF], F32R, ctx=own)
    w2 = c.sb("w2", [P, 2, MF, DM], F32R, ctx=own)
    b2 = c.sb("b2", [P, DM], ctx=own)
    stats = c.sb("stats", [P, TJ, 6], ctx=own)
    mv = c.sb("mv", [P, TJ, 2], ctx=own)
    ve = c.sb("ve", [P, TJ], ctx=own)
    rs = c.sb("rs", [P, TJ], ctx=own)
    XN, HN, RN = TJ * DM, KD * TJ * P, 3 * TJ * P
    place = c.sb("place", [P, XN + KD * FF + MF * DM], ctx=own)
    xhat = place[:, 0:2 * XN].rearrange("p (s t n) -> p s t n", s=2, t=TJ)
    h_in = place[:, 2 * XN:2 * XN + HN].rearrange("p (k n) -> p k n", k=KD)
    r_in = place[:, 2 * XN + HN:2 * XN + HN + RN].rearrange("p (s n) -> p s n", s=3)
    w1_in = place[:, XN:XN + KD * FF].rearrange("p (k n) -> p k n", k=KD)
    w2_in = place[:, XN + KD * FF:].rearrange("p (k n) -> p k n", k=MF)
    hT = c.sb("hT", [P, 2, KD, TJ * P], F32R, ctx=own)
    rT = c.sb("rT", [P, 2, 2, MF, TJ * P], F32R, ctx=own)
    tp = c.ps("tp", [P, KD, 512], ctx=own)
    f1 = c.ps("f1", [P, 4, 512], ctx=own)
    f2 = c.ps("f2", [P, 2, 2, DM], ctx=own)
    sem = lambda n: c.sem("mlp_" + n)
    w1_loaded, w2_loaded, stats_ready, rstd_ready, xhat_ready = sem("w1_loaded"), sem("w2_loaded"), sem("stats"), sem("rstd"), sem("xhat")
    tp_ready, hT_ready, f1_ready, rT_ready = sem("tp"), sem("hT"), sem("f1"), sem("rT")
    f2_ready, f2_free = sem("f2"), sem("f2_free")
    dve_order, pool_order, sum_order = sem("dve_order"), sem("pool_order"), sem("sum_order")
    b2_added, h_low, r_low = sem("b2_added"), sem("h_low"), sem("r_low")
    w_high, w1_low, w2_low = sem("w_high"), sem("w1_low"), sem("w2_low")

    with nc.Block() as block:

        @block.sync
        def _(sp):
            sp.dma_start(w1_in, d["w1"].rearrange("(k p) n -> p k n", p=P)).then_inc(w1_loaded, 16)
            sp.dma_start(w2_in, d["w2"].rearrange("(k p) n -> p k n", p=P)).then_inc(w2_loaded, 16)
            sp.dma_start(b2[:], d["rows"][ROW["b2_attn"]:ROW["b2_attn"] + 1, :].broadcast_to([P, DM])).then_inc(w2_loaded, 16)

        @block.gpsimd
        def _(pool):

            def add_b2(b):
                part = c.H1[:, b * TJ:(b + 1) * TJ, :]
                pool.wait_ge(xhat_ready, h * B + b + 1)
                pool.tensor_tensor(part, part, b2[:].unsqueeze(1).broadcast_to([P, TJ, DM]),
                                   ALU.add).then_inc(b2_added, 1)

            for b in range(B):
                c.hold(pool, stats_ready, h * B + b + 1)
                pool.tensor_scalar(ve[:], mv[:, :, 1], EPS, None, ALU.add).then_inc(pool_order, 1)
                pool.wait_ge(pool_order, h * B + b + 1)
                pool.tensor_tensor(rs[:], ve[:], c.mhalf[:, 0:TJ], ALU.pow).then_inc(rstd_ready, 1)
                if b:
                    add_b2(b - 1)
            add_b2(B - 1)

        @block.scalar
        def _(act):
            act.wait_ge(w1_loaded, h * 16 + 16)
            act.copy(w1[:, 0], w1_in).then_inc(w_high, 1)
            act.wait_ge(w1_low, h + 1)
            for b in range(B):
                for k in range(KD):
                    act.wait_ge(tp_ready, h * 2 * B + 2 * b + k + 1)
                    g, o = COL["ln2_g"] + k, COL["ln2_b"] + k
                    for dst in (hT[:, 0, k, :], h_in[:, k, :]):
                        last = act.activation(dst, tp[:, k, :], ACT.Identity, bias=c.cols[:, o:o + 1],
                                              scale=c.cols[:, g:g + 1])
                    last.then_inc(hT_ready, 1)
                if b == 0:
                    act.wait_ge(w2_loaded, h * 32 + 32)
                    act.copy(w2[:, 0], w2_in).then_inc(w_high, 1)
                    act.wait_ge(w2_low, h + 1)
                if b >= 2:
                    act.wait_ge(f2_ready, h * 2 * B + 2 * (b - 1))
                for m in range(MF):
                    n = b * MF + m
                    act.wait_ge(f1_ready, h * B * MF + n + 1)
                    if n >= 3:
                        act.wait_ge(r_low, h * B * MF + n - 2)
                    col = COL["b1"] + m
                    act.activation(rT[:, b % 2, 0, m, :], f1[:, m % 4, :], ACT.Relu, bias=c.cols[:, col:col + 1])
                    act.activation(r_in[:, n % 3, :], f1[:, m % 4, :], ACT.Relu,
                                   bias=c.cols[:, col:col + 1]).then_inc(rT_ready, 1)

        @block.tensor
        def _(pe):

            def up(b):
                pe.wait_ge(xhat_ready, h * B + b + 1)
                if b:
                    pe.wait_ge(hT_ready, h * 2 * B + 2 * b)
                for k in range(KD):
                    for t in range(TJ):
                        last = pe.transpose(tp[:, k, t * P:(t + 1) * P], xhat[:, b % 2, t, k * P:(k + 1) * P], c.ident[:])
                    last.then_inc(tp_ready, 1)
                if b >= 2:
                    down(b - 2)
                pe.wait_ge(w1_low, h + 1)
                pe.wait_ge(h_low, h * B + b + 1)
                for m in range(MF):
                    if b * MF + m >= 4:
                        pe.wait_ge(rT_ready, h * B * MF + b * MF + m - 3)
                    for k in range(KD):
                        last = product3(pe, f1[:, m % 4, :], [w1[:, i, k, m * P:(m + 1) * P] for i in range(2)],
                                        [hT[:, i, k, :] for i in range(2)], start=(k == 0), stop=(k == KD - 1))
                    last.then_inc(f1_ready, 1)

            def down(b):
                pe.wait_ge(w2_low, h + 1)
                pe.wait_ge(r_low, h * B * MF + (b + 1) * MF)
                for n in range(2):
                    if 2 * b + n >= 2:
                        pe.wait_ge(f2_free, h * 2 * B + 2 * b + n - 1)
                    for q in range(2):
                        t = 2 * n + q
                        for m in range(MF):
                            last = product3(pe, f2[:, n, q, :],
                                            [rT[:, b % 2, i, m, t * P:(t + 1) * P] for i in range(2)],
                                            [w2[:, i, m, :] for i in range(2)], start=(m == 0), stop=(m == MF - 1))
                    last.then_inc(f2_ready, 1)

            for b in range(B):
                up(b)
            down(B - 2)
            down(B - 1)

        @block.vector
        def _(dve):

            def layernorm(b):
                for t in range(TJ):
                    last = dve.bn_stats(stats[:, t, :], c.H1[:, b * TJ + t, :])
                last.then_inc(dve_order, 1)
                c.hold(dve, dve_order, h * B + b + 1)
                for t in range(TJ):
                    last = dve.bn_aggr(mv[:, t, :], stats[:, t, :])
                last.then_inc(stats_ready, 1)
                dve.wait_ge(rstd_ready, h * B + b + 1)
                if b >= 2:
                    dve.wait_ge(tp_ready, h * 2 * B + 2 * (b - 1))
                for t in range(TJ):
                    last = dve.tensor_scalar(xhat[:, b % 2, t, :], c.H1[:, b * TJ + t, :], mv[:, t, 0:1],
                                             rs[:, t:t + 1], ALU.subtract, ALU.mult)
                last.then_inc(xhat_ready, 1)

            def h_split(b):
                dve.wait_ge(hT_ready, h * 2 * B + 2 * b + 2)
                low_part(dve, hT[:, 1], h_in, hT[:, 0]).then_inc(h_low, 1)

            def r_split(b):
                for m in range(MF):
                    dve.wait_ge(rT_ready, h * B * MF + b * MF + m + 1)
                    low_part(dve, rT[:, b % 2, 1, m, :], r_in[:, (b * MF + m) % 3, :], rT[:, b % 2, 0, m, :]).then_inc(r_low, 1)

            layernorm(0)
            dve.wait_ge(w_high, h * 2 + 1)
            low_part(dve, w1[:, 1], w1_in, w1[:, 0]).then_inc(w1_low, 1)
            def finish(b):
                dve.wait_ge(b2_added, h * B + b + 1)
                for n in range(2):
                    m = 2 * b + n
                    y = c.H1[:, 2 * m:2 * m + 2, :]
                    xs = c.X[:, bass.ds(h * TH + 2 * m, 2), :]
                    dve.wait_ge(f2_ready, h * 2 * B + m + 1)
                    dve.tensor_tensor(y, y, f2[:, n], ALU.add).then_inc(f2_free, 1)
                    dve.wait_ge(f2_free, h * 2 * B + m + 1)
                    dve.tensor_tensor(y, y, c.rows1[:, b, 2:3, :].broadcast_to([P, 2, DM]), ALU.mult
                                      ).then_inc(sum_order, 1)
                    dve.wait_ge(sum_order, h * 2 * B + m + 1)
                    dve.tensor_tensor(xs, xs, y, ALU.add)

            h_split(0)
            dve.wait_ge(w_high, h * 2 + 2)
            low_part(dve, w2[:, 1], w2_in, w2[:, 0]).then_inc(w2_low, 1)
            dve.wait_ge(w1_low, h + 1)
            layernorm(1)
            for b in range(B):
                r_split(b)
                if b + 1 < B:
                    h_split(b + 1)
                if b + 2 < B:
                    layernorm(b + 2)
                if b:
                    finish(b - 1)
            finish(B - 1)


E_, HM, GR = 8, 512, 16
NT = TILES + E_ - 1


def moe(c, out):
    nc, d = c.nc, c.d
    c.phase = "moe_"
    h_dram = nc.dram_tensor("h_dram", (TILES * P, DM), F32, kind="Internal").ap()
    y_dram = nc.dram_tensor("y_dram", ((TILES + NT) * P, DM), F32, kind="Internal").ap()
    sem = lambda n: c.sem("moe_" + n)
    with ExitStack() as own:
        sb = lambda name, shape, dt=F32: c.sb(name, shape, dt, ctx=own)
        w1 = sb("w1", [P, E_, KD, HM])
        w2 = sb("w2", [P, E_, HM // P, DM])
        b1 = sb("b1", [P, E_, HM])
        b2 = sb("b2", [P, E_, DM])
        token_in = sb("token_in", [P, NT], U32)
        token_out = sb("token_out", [P, NT], U32)
        expert = sb("expert", [1, NT], U32)
        score = sb("score", [P, TILES])
        w_loaded = sem("w_loaded")

        with ExitStack() as st:
            sb1 = lambda name, shape, dt=F32: c.sb(name, shape, dt, ctx=st)
            hrow = sb1("hrow", [P, TILES, DM])
            w_red = sb1("w_red", [P, KD, GR])
            wgT = sb1("wgT", [GR, E_])
            wsq = sb1("wsq", [GR, E_])
            stats = sb1("stats", [P, 2, TJ, 6])
            mv = sb1("mv", [P, 2, TJ, 2])
            ve = sb1("ve", [P, 2, TJ])
            rs = sb1("rs", [P, 2, TJ])
            xhat = sb1("xhat", [P, 2, TJ, DM])
            rows_scaled, rows_ready = sem("rows_scaled"), sem("rows_ready")
            hT = sb1("hT", [P, KD, TJ * P])
            xr = sb1("xr", [GR, TJ * P])
            full1 = sb1("full1", [P, P])
            upper = sb1("upper", [P, P])
            L = sb1("L", [P, TILES, E_])
            O = sb1("O", [P, TILES, E_])
            W = sb1("W", [P, TILES, E_])
            iota = sb1("iota", [P, E_])
            tile_no = sb1("tile_no", [P, NT])
            ends = sb1("ends", [P, NT, E_])
            mx = sb1("mx", [P, TILES])
            tmp = sb1("tmp", [P, TILES])
            cnt = sb1("cnt", [P, 8, E_])
            cnt_i = sb1("cnt_i", [P, E_], I32)
            tile_i = sb1("tile_i", [P, TILES], I32)
            tile_of = sb1("tile_of", [P, TILES])
            row_of = sb1("row_of", [P, TILES])
            in_tile = sb1("in_tile", [P, TILES, NT])
            in_row = xhat[:].rearrange("p s t n -> p s (t n)").rearrange("p s (t r) -> p s t r", r=P)
            number = sb1("number", [P, TILES])
            row_no = sb1("row_no", [P, P])
            pad_no = sb1("pad_no", [P, NT])
            invs = sb1("invs", [NT, P])
            tokens = sb1("tokens", [P, NT])
            in_tile_ready, in_row_ready, in_row_used = sem("in_tile_ready"), sem("in_row_ready"), sem("in_row_used")
            inv_ready, invs_ready, tokens_ready, h_stored = sem("inv"), sem("invs"), sem("tokens"), sem("h_stored")
            tp = c.ps("tp", [P, KD, 512], ctx=st)
            rp = c.ps("rp", [P, 512], ctx=st)
            lp = c.ps("lp", [P, 512], ctx=st)
            pre = c.ps("pre", [P, 512], ctx=st)
            tot = c.ps("tot", [P, 512], ctx=st)
            np_ = c.ps("np", [P, 512], ctx=st)
            r_loaded, stats_ready, rstd_ready, xhat_ready = sem("r_loaded"), sem("stats"), sem("rstd"), sem("xhat")
            tp_ready, hT_ready, rp_ready, xr_ready = sem("tp"), sem("hT"), sem("rp"), sem("xr")
            lp_ready, lp_free, l_done = sem("lp"), sem("lp_free"), sem("l_done")
            ln_order = sem("ln_order")
            dve_order, pool_order = sem("dve_order"), sem("pool_order")
            wsq_ready, norm_ready, sqrt_ready, wg_ready = sem("wsq"), sem("norm"), sem("sqrt"), sem("wg")
            m_ready, exp_ready, o_ready, count_ready = sem("m"), sem("exp"), sem("o"), sem("count")
            const_ready = sem("const")

            with nc.Block() as block:

                @block.sync
                def _(sp):
                    sp.dma_start(w_red[:], d["w_red"].rearrange("(k p) n -> p k n", p=P)).then_inc(r_loaded, 16)
                    sp.dma_start(wgT[:], d["wgT"]).then_inc(r_loaded, 16)
                    for e in range(E_):
                        sp.dma_start(w1[:, e], d["moe_w1"][e].rearrange("(k p) n -> p k n", p=P)).then_inc(w_loaded, 16)
                        sp.dma_start(w2[:, e], d["moe_w2"][e].rearrange("(k p) n -> p k n", p=P)).then_inc(w_loaded, 16)
                    sp.dma_start(b1[:].rearrange("p e n -> p (e n)"), d["moe_b1"].rearrange("e n -> (e n)").unsqueeze(0)
                                 .broadcast_to([P, E_ * HM])).then_inc(w_loaded, 16)
                    sp.dma_start(b2[:].rearrange("p e n -> p (e n)"), d["moe_b2"].rearrange("e n -> (e n)").unsqueeze(0)
                                 .broadcast_to([P, E_ * DM])).then_inc(w_loaded, 16)
                    with sp.Fori(0, 2 * B) as q:
                        sp.wait_ge(rows_ready, q + 1)
                        sp.dma_start(h_dram[bass.ds(q * TJ * P, TJ * P), :].rearrange("(t p) n -> p t n", p=P),
                                     hrow[:, bass.ds(q * TJ, TJ), :]).then_inc(h_stored, 16)
                    sp.wait_ge(h_stored, 16 * 2 * B)

                @block.gpsimd
                def _(pool):
                    pool.memset(full1[:], 1.0).then_inc(const_ready, 1)
                    pool.memset(upper[:], 1.0).then_inc(pool_order, 1)
                    pool.iota(iota[:], pattern=[[1, E_]], base=0, channel_multiplier=0,
                              allow_small_or_imprecise_dtypes=True)
                    pool.iota(tile_no[:], pattern=[[1, NT]], base=0, channel_multiplier=0,
                              allow_small_or_imprecise_dtypes=True)
                    pool.iota(row_no[:], pattern=[[1, P]], base=0, channel_multiplier=0,
                              allow_small_or_imprecise_dtypes=True)
                    pool.iota(number[:], pattern=[[P, TILES]], base=1, channel_multiplier=1,
                              allow_small_or_imprecise_dtypes=True)
                    pool.iota(pad_no[:], pattern=[[P, NT]], base=TILES * P + 1, channel_multiplier=1,
                              allow_small_or_imprecise_dtypes=True)
                    pool.wait_ge(pool_order, 1)
                    pool.affine_select(out=upper[:], in_=upper[:], compare_op=ALU.is_gt, fill=0.0,
                                       base=0, pattern=[[1, P]], channel_multiplier=-1).then_inc(const_ready, 1)
                    def rstd(q, s):
                        c.hold(pool, stats_ready, q + 1)
                        pool.tensor_scalar(ve[:, s], mv[:, s, :, 1], EPS, None, ALU.add).then_inc(pool_order, 1)
                        pool.wait_ge(pool_order, q + 2)
                        pool.tensor_tensor(rs[:, s], ve[:, s], c.mhalf[:, 0:TJ], ALU.pow).then_inc(rstd_ready, 1)

                    with pool.Fori(0, HALVES) as hh:
                        rstd(hh * B, 0)
                        for b in range(B):
                            if b + 1 < B:
                                rstd(hh * B + b + 1, (b + 1) % 2)
                            rows = hrow[:, bass.ds(hh * TH + b * TJ, TJ), :]
                            c.hold(pool, xhat_ready, hh * B + b + 1)
                            pool.tensor_tensor(rows, xhat[:, b % 2], c.rows1[:, b, 4:5, :].broadcast_to([P, TJ, DM]),
                                               ALU.mult).then_inc(rows_scaled, 1)
                            c.hold(pool, rows_scaled, hh * B + b + 3)
                            pool.tensor_tensor(rows, rows, c.rows1[:, b, 3:4, :].broadcast_to([P, TJ, DM]),
                                               ALU.add).then_inc(rows_ready, 1)

                @block.scalar
                def _(act):
                    act.wait_ge(norm_ready, 1)
                    act.activation(wsq[:], np_[0:GR, 0:E_], ACT.Sqrt).then_inc(sqrt_ready, 1)
                    with act.Fori(0, HALVES) as hh:
                        for b in range(B):
                            q = hh * B + b
                            for k in range(KD):
                                act.wait_ge(tp_ready, q * 2 + k + 1)
                                act.activation(hT[:, k, :], tp[:, k, :], ACT.Identity,
                                               bias=c.modT[1][:, 3 * KD + k, b:b + 1],
                                               scale=c.modT[1][:, 4 * KD + k, b:b + 1]).then_inc(hT_ready, 1)
                            act.wait_ge(rp_ready, q + 1)
                            act.copy(xr[:], rp[0:GR, :]).then_inc(xr_ready, 1)
                    act.wait_ge(m_ready, 1)
                    act.activation(W[:], W[:], ACT.Exp).then_inc(exp_ready, 1)

                @block.tensor
                def _(pe):
                    pe.wait_ge(wsq_ready, 1)
                    pe.wait_ge(const_ready, 2)
                    pe.matmul(np_[0:GR, 0:E_], full1[0:GR, 0:GR], wsq[:], start=True, stop=True).then_inc(norm_ready, 1)
                    pe.wait_ge(wg_ready, 1)

                    def turn(q, s):
                        pe.wait_ge(xhat_ready, q + 1)
                        for k in range(KD):
                            for t in range(TJ):
                                last = pe.transpose(tp[:, k, t * P:(t + 1) * P], xhat[:, s, t, k * P:(k + 1) * P],
                                                    c.ident[:])
                            last.then_inc(tp_ready, 1)

                    with pe.Fori(0, HALVES) as hh:
                        turn(hh * B, 0)
                        for b in range(B):
                            q = hh * B + b
                            pe.wait_ge(hT_ready, q * 2 + 2)
                            for k in range(KD):
                                last = pe.matmul(rp[0:GR, :], w_red[:, k, :], hT[:, k, :], start=(k == 0),
                                                 stop=(k == KD - 1))
                            last.then_inc(rp_ready, 1)
                            if b + 1 < B:
                                turn(q + 1, (b + 1) % 2)
                            pe.wait_ge(xr_ready, q + 1)
                            pe.wait_ge(lp_free, q + 1)
                            for t in range(TJ):
                                last = pe.matmul(lp[:, t * E_:(t + 1) * E_], xr[:, t * P:(t + 1) * P], wgT[:],
                                                 start=True, stop=True)
                            last.then_inc(lp_ready, 1)
                    pe.wait_ge(o_ready, 1)
                    o = O[:].rearrange("p t e -> p (t e)")
                    pe.matmul(pre[:, 0:TILES * E_], upper[:], o, start=True, stop=True)
                    pe.matmul(tot[:, 0:TILES * E_], full1[:], o, start=True, stop=True).then_inc(count_ready, 1)
                    pe.wait_ge(in_tile_ready, 1)
                    for t in range(TILES):
                        if t % 8 == 0:
                            pe.wait_ge(in_row_ready, t // 8 + 1)
                        last = pe.matmul(np_[0:NT, 0:P], in_tile[:, t, :], in_row[:, t // 8 % 2, t % 8, :],
                                         start=(t == 0), stop=(t == TILES - 1))
                        if t % 8 == 7:
                            last.then_inc(in_row_used, 1)
                    pe.wait_ge(invs_ready, 1)
                    pe.transpose(rp[:, 0:NT], invs[:], c.ident[0:NT, 0:NT]).then_inc(tokens_ready, 1)

                @block.vector
                def _(dve):
                    order = Steps(dve, dve_order)
                    dve.wait_ge(r_loaded, 32)
                    dve.tensor_tensor(wsq[:], wgT[:], wgT[:], ALU.mult).then_inc(wsq_ready, 1)
                    dve.wait_ge(sqrt_ready, 1)
                    order.then(dve.tensor_scalar(wsq[:], wsq[:], 1e-4, None, ALU.max))
                    order.then(dve.reciprocal(wsq[:], wsq[:]))
                    dve.tensor_tensor(wgT[:], wgT[:], wsq[:], ALU.mult).then_inc(wg_ready, 1)
                    dve.sem_inc(lp_free, 1)

                    dve.sem_inc(rows_scaled, 2)

                    def layernorm(q, s):
                        for t in range(TJ):
                            last = dve.bn_stats(stats[:, s, t, :], c.X[:, q * TJ + t, :])
                        last.then_inc(ln_order, 1)
                        c.hold(dve, ln_order, q + 1)
                        for t in range(TJ):
                            last = dve.bn_aggr(mv[:, s, t, :], stats[:, s, t, :])
                        last.then_inc(stats_ready, 1)
                        dve.wait_ge(rstd_ready, q + 1)
                        dve.wait_ge(rows_scaled, q + 1)
                        for t in range(TJ):
                            last = dve.tensor_scalar(xhat[:, s, t, :], c.X[:, q * TJ + t, :],
                                                     mv[:, s, t, 0:1], rs[:, s, t:t + 1], ALU.subtract, ALU.mult)
                        last.then_inc(xhat_ready, 1)

                    with dve.Fori(0, HALVES) as hh:
                        layernorm(hh * B, 0)
                        for b in range(B):
                            q = hh * B + b
                            if b + 1 < B:
                                layernorm(q + 1, (b + 1) % 2)
                            dve.wait_ge(lp_ready, q + 1)
                            dve.tensor_copy(L[:, bass.ds(q * TJ, TJ), :],
                                            lp[:, 0:TJ * E_].rearrange("p (t e) -> p t e", e=E_)).then_inc(lp_free, 1)
                    dve.wait_ge(lp_free, 2 * B + 1)

                    def over_e(x):
                        return x.unsqueeze(2).broadcast_to([P, TILES, E_])

                    def over_t(x):
                        return x.unsqueeze(1).broadcast_to([P, TILES, E_])

                    order.then(dve.tensor_reduce(mx[:], L[:], AX.X, ALU.max))
                    dve.tensor_tensor(W[:], L[:], over_e(mx[:]), ALU.subtract).then_inc(m_ready, 1)
                    order.then(dve.tensor_tensor(L[:], L[:], over_e(mx[:]), ALU.is_equal))
                    order.then(dve.scalar_tensor_tensor(L[:], L[:], -float(E_), over_t(iota[:]), ALU.mult, ALU.add))
                    order.then(dve.tensor_reduce(mx[:], L[:], AX.X, ALU.min))
                    dve.tensor_tensor(O[:], L[:], over_e(mx[:]), ALU.is_equal).then_inc(o_ready, 1)
                    dve.wait_ge(exp_ready, 1)
                    order.then(dve.tensor_reduce(tmp[:], W[:], AX.X, ALU.add))
                    order.then(dve.reciprocal(score[:], tmp[:]))
                    dve.wait_ge(count_ready, 1)
                    order.then(dve.tensor_copy(W[:], tot[:, 0:TILES * E_].rearrange("p (t e) -> p t e", e=E_)))
                    dve.wait_ge(o_ready, 1)
                    for e in range(E_):
                        order.did(dve.tensor_tensor_scan(L[:, :, e], full1[:, 0:TILES], W[:, :, e], 0.0,
                                                           ALU.mult, ALU.add))
                    dve.wait_ge(dve_order, order.n)
                    order.then(dve.tensor_scalar(cnt[:, 0, :], L[:, TILES - 1, :], float(P - 1), None, ALU.add))
                    order.then(dve.tensor_tensor(L[:], L[:], W[:], ALU.subtract))
                    order.then(dve.tensor_tensor(L[:], L[:], pre[:, 0:TILES * E_].rearrange("p (t e) -> p t e", e=E_),
                                                 ALU.add))
                    order.then(dve.tensor_copy(cnt_i[:], cnt[:, 0, :]))
                    order.then(dve.tensor_scalar(cnt_i[:], cnt_i[:], 7, None, ALU.arith_shift_right))
                    order.then(dve.tensor_copy(cnt[:, 1, :], cnt_i[:]))
                    order.then(dve.tensor_tensor_scan(cnt[:, 2, :], full1[:, 0:E_], cnt[:, 1, :], 0.0, ALU.mult, ALU.add))
                    order.then(dve.tensor_tensor(cnt[:, 3, :], cnt[:, 2, :], cnt[:, 1, :], ALU.subtract))
                    order.then(dve.scalar_tensor_tensor(L[:], over_t(cnt[:, 3, :]), float(P), L[:], ALU.mult, ALU.add))
                    order.then(dve.tensor_tensor(L[:], L[:], O[:], ALU.mult))
                    order.then(dve.tensor_reduce(tmp[:], L[:], AX.X, ALU.add))
                    order.then(dve.tensor_copy(tile_i[:], tmp[:]))
                    order.then(dve.tensor_scalar(tile_i[:], tile_i[:], 7, None, ALU.arith_shift_right))
                    order.then(dve.tensor_copy(tile_of[:], tile_i[:]))
                    order.then(dve.scalar_tensor_tensor(row_of[:], tile_of[:], -float(P), tmp[:], ALU.mult, ALU.add))
                    order.then(dve.tensor_tensor(in_tile[:], tile_of[:].unsqueeze(2).broadcast_to([P, TILES, NT]),
                                                 tile_no[:].unsqueeze(1).broadcast_to([P, TILES, NT]), ALU.is_equal))
                    dve.tensor_tensor(in_tile[:], in_tile[:], number[:].unsqueeze(2).broadcast_to([P, TILES, NT]),
                                      ALU.mult).then_inc(in_tile_ready, 1)
                    dve.wait_ge(rows_ready, 2 * B)
                    for n in range(4):
                        if n >= 2:
                            dve.wait_ge(in_row_used, n - 1)
                        dve.tensor_tensor(in_row[:, n % 2], row_of[:, 8 * n:8 * n + 8].unsqueeze(2).broadcast_to([P, 8, P]),
                                          row_no[:].unsqueeze(1).broadcast_to([P, 8, P]), ALU.is_equal
                                          ).then_inc(in_row_ready, 1)
                    order.then(dve.tensor_tensor(ends[:], cnt[:, 2, :].unsqueeze(1).broadcast_to([P, NT, E_]),
                                                 tile_no[:].unsqueeze(2).broadcast_to([P, NT, E_]), ALU.is_le))
                    order.then(dve.tensor_reduce(tile_no[:], ends[:], AX.X, ALU.add))
                    order.then(dve.tensor_scalar(tile_no[:], tile_no[:], float(E_ - 1), None, ALU.min))
                    dve.tensor_copy(expert[:], tile_no[0:1, :])
                    dve.wait_ge(in_row_used, 4)
                    dve.tensor_copy(invs[:], np_[0:NT, 0:P]).then_inc(invs_ready, 1)
                    dve.wait_ge(tokens_ready, 1)
                    order.then(dve.tensor_scalar(tokens[:], rp[:, 0:NT], -1.0, 0.0, ALU.add, ALU.max))
                    dve.tensor_copy(token_in[:], tokens[:])
                    order.then(dve.scalar_tensor_tensor(in_tile[:, 0, :], rp[:, 0:NT], 0.0, pad_no[:],
                                                        ALU.is_equal, ALU.mult))
                    order.then(dve.scalar_tensor_tensor(in_tile[:, 1, :], rp[:, 0:NT], -1.0, in_tile[:, 0, :],
                                                        ALU.add, ALU.add))
                    dve.tensor_copy(token_out[:], in_tile[:, 1, :])

        with ExitStack() as st:
            sb2 = lambda name, shape, dt=F32: c.sb(name, shape, dt, ctx=st)
            hs = sb2("hs", [P, 3, DM])
            hsT = sb2("hsT", [P, 2, KD, P])
            a = sb2("a", [P, 2, HM])
            aT = sb2("aT", [P, 2, HM // P, P])
            ys = sb2("ys", [P, 3, DM])
            tp = c.ps("tp2", [P, 2, 512], ctx=st)
            up = c.ps("up", [P, 2, HM], ctx=st)
            ap = c.ps("ap", [P, 2, 512], ctx=st)
            dn = c.ps("dn", [P, 2, 512], ctx=st)
            hs_loaded = [sem(f"hs_loaded{i}") for i in range(3)]
            ys_stored = [sem(f"ys_stored{i}") for i in range(3)]
            tp_ready, hsT_ready, up_ready, up_free = sem("tp2"), sem("hsT"), sem("up"), sem("up_free")
            ys_free = sem("ys_free")
            a_ready, ap_ready, aT_ready, dn_ready, ys_ready = sem("a"), sem("ap"), sem("aT"), sem("dn"), sem("ys")

            def tiles(eng, do_tile):
                with eng.Fori(0, NT // 6) as i6:
                    for j in range(6):
                        do_tile(i6 * 6 + j, i6 * 2 + j // 3, j)
                for n in range(NT // 6 * 6, NT):
                    do_tile(n, n // 3, n)

            with nc.Block() as block:

                @block.gpsimd
                def _(pool):

                    def take_in(n):
                        pool.wait_ge(hsT_ready, n + 1)
                        pool.indirect_dma_start(hs[:, n % 3, :], None, h_dram,
                                                bass.IndirectOffsetOnAxis(ap=token_in[:, n:n + 1], axis=0)
                                                ).then_inc(hs_loaded[n % 3], 16)

                    for n in range(3):
                        take_in(n)
                    for n in range(NT):
                        if n + 3 < NT:
                            take_in(n + 3)
                        pool.wait_ge(ys_ready, n + 1)
                        pool.indirect_dma_start(y_dram, bass.IndirectOffsetOnAxis(ap=token_out[:, n:n + 1], axis=0),
                                                ys[:, n % 3, :], None).then_inc(ys_stored[n % 3], 16)

                @block.sync
                def _(sp):
                    for n in range(NT):
                        sp.wait_ge(ys_stored[n % 3], 16 * (n // 3) + 16)
                        sp.sem_inc(ys_free, 1)

                @block.tensor
                def _(pe):
                    pe.wait_ge(w_loaded, 16 * (2 * E_ + 2))

                    def expert_of(n):
                        return pe.value_load(expert[0:1, bass.ds(n, 1)], min_val=0, max_val=E_ - 1)

                    def turn_h(n, turn, j):
                        pe.wait_ge(hs_loaded[j % 3], turn * 16 + 16)
                        for k in range(KD):
                            last = pe.transpose(tp[:, j % 2, k * P:(k + 1) * P], hs[:, j % 3, k * P:(k + 1) * P], c.ident[:])
                        last.then_inc(tp_ready, 1)

                    def go_up(n, j, e):
                        pe.wait_ge(hsT_ready, n + 4)
                        pe.wait_ge(up_free, n + 1)
                        for k in range(KD):
                            last = pe.matmul(up[:, j % 2, :], hsT[:, j % 2, k, :], w1[:, bass.ds(e, 1), k, :],
                                             start=(k == 0), stop=(k == KD - 1))
                        last.then_inc(up_ready, 1)

                    def do_tile(n, turn, j):
                        e = expert_of(n)
                        e_next = expert_of(n + 1) if not isinstance(n, int) or n + 1 < NT else None
                        pe.wait_ge(a_ready, n + 1)
                        for m in range(HM // P):
                            last = pe.transpose(ap[:, j % 2, m * P:(m + 1) * P], a[:, j % 2, m * P:(m + 1) * P], c.ident[:])
                        last.then_inc(ap_ready, 1)
                        if not isinstance(n, int) or n + 2 < NT:
                            turn_h(n + 2, turn + (2 + j % 3) // 3, j + 2)
                        if e_next is not None:
                            go_up(n + 1, j + 1, e_next)
                        pe.wait_ge(aT_ready, n + 1)
                        for m in range(HM // P):
                            last = pe.matmul(dn[:, j % 2, 0:DM], aT[:, j % 2, m, :], w2[:, bass.ds(e, 1), m, :],
                                             start=(m == 0), stop=(m == HM // P - 1))
                        last.then_inc(dn_ready, 1)

                    turn_h(0, 0, 0)
                    turn_h(1, 0, 1)
                    go_up(0, 0, expert_of(0))
                    tiles(pe, do_tile)

                @block.scalar
                def _(act):
                    act.sem_inc(hsT_ready, 3)

                    def turned(n, j):
                        act.wait_ge(tp_ready, n + 1)
                        act.copy(hsT[:, j % 2].rearrange("p k n -> p (k n)"), tp[:, j % 2, 0:DM]).then_inc(hsT_ready, 1)

                    def gelu(n, j):
                        act.wait_ge(up_free, n + 3)
                        act.activation(a[:, j % 2, :], a[:, j % 2, :], ACT.Gelu).then_inc(a_ready, 1)

                    def do_tile(n, turn, j):
                        act.wait_ge(ap_ready, n + 1)
                        act.copy(aT[:, j % 2].rearrange("p m n -> p (m n)"), ap[:, j % 2, :]).then_inc(aT_ready, 1)
                        if not isinstance(n, int) or n + 2 < NT:
                            turned(n + 2, j)
                        if not isinstance(n, int) or n + 1 < NT:
                            gelu(n + 1, j + 1)

                    turned(0, 0)
                    turned(1, 1)
                    gelu(0, 0)
                    tiles(act, do_tile)

                @block.vector
                def _(dve):
                    dve.sem_inc(up_free, 2)
                    dve.sem_inc(ys_free, 3)

                    def expert_of(n):
                        return dve.value_load(expert[0:1, bass.ds(n, 1)], min_val=0, max_val=E_ - 1)

                    def add_b1(n, j):
                        e = expert_of(n)
                        dve.wait_ge(up_ready, n + 1)
                        dve.tensor_tensor(a[:, j % 2, :], up[:, j % 2, :], b1[:, bass.ds(e, 1), :].rearrange(
                            "p o n -> p (o n)"), ALU.add).then_inc(up_free, 1)

                    def do_tile(n, turn, j):
                        if not isinstance(n, int) or n + 1 < NT:
                            add_b1(n + 1, j + 1)
                        e = expert_of(n)
                        dve.wait_ge(dn_ready, n + 1)
                        dve.wait_ge(ys_free, n + 1)
                        dve.tensor_tensor(ys[:, j % 3, :], dn[:, j % 2, 0:DM], b2[:, bass.ds(e, 1), :].rearrange(
                            "p o n -> p (o n)"), ALU.add).then_inc(ys_ready, 1)

                    add_b1(0, 0)
                    tiles(dve, do_tile)

        with ExitStack() as st:
            y = c.sb("y", [P, 2 * B, TJ, DM], ctx=st)
            taken, gated, stored = [sem(f"taken{i}") for i in range(B)], sem("gated"), sem("stored")
            x_ready = [sem("x_ready_pool"), sem("x_ready_dve")]
            with nc.Block() as block:

                def add(eng, q):
                    eng.wait_ge(gated, TJ * (q + 1))
                    xs = c.X[:, q * TJ:(q + 1) * TJ, :]
                    eng.tensor_tensor(xs, xs, y[:, q], ALU.add).then_inc(x_ready[q % 2], 1)

                @block.gpsimd
                def _(pool):
                    for q in range(0, 2 * B, 2):
                        add(pool, q)

                @block.vector
                def _(dve):
                    for q in range(2 * B):
                        dve.wait_ge(taken[q // 2], 16)
                        for t in range(TJ):
                            at = q * TJ + t
                            dve.scalar_tensor_tensor(y[:, q, t, :], y[:, q, t, :], score[:, at:at + 1],
                                                     c.rows1[:, q % B, 5, :], ALU.mult, ALU.mult).then_inc(gated, 1)
                        if q % 2:
                            add(dve, q)

                @block.sync
                def _(sp):
                    for n in range(B):
                        rows = y_dram[2 * n * TJ * P:2 * (n + 1) * TJ * P, :].rearrange("(q t p) n -> p q t n", t=TJ, p=P)
                        sp.dma_start(y[:, 2 * n:2 * n + 2], rows).then_inc(taken[n], 16)
                    for q in range(2 * B):
                        h, b = q // B, q % B
                        sp.wait_ge(x_ready[q % 2], q // 2 + 1)
                        sp.dma_start(out[b, h * TJ * P:(h + 1) * TJ * P, :].rearrange("(t p) n -> p t n", p=P),
                                     c.X[:, q * TJ:(q + 1) * TJ, :]).then_inc(stored, 16)
                    sp.wait_ge(stored, 16 * B * HALVES)


def program(nc, d, out):
    with ExitStack() as ctx:
        c = Core(nc, ctx, d)
        lasting(c)
        c.layer1 = ctx.enter_context(ExitStack())
        attention_constants(c)
        c.layer0 = ctx.enter_context(ExitStack())
        c.gru_own = ctx.enter_context(ExitStack())
        first = len(c.sems)
        setup(c)
        gru(c)
        c.gru_own.close()
        ffn(c)
        c.retire(first)
        c.layer0.close()
        c.phase = "l1_"
        c.H1 = c.sb("H1", [P, TH, DM], ctx=c.layer1)
        with nc.Fori(0, HALVES) as h:
            with ExitStack() as own:
                attention(c, h, own)
            with ExitStack() as own:
                mlp(c, h, own)
        c.layer1.close()
        moe(c, out)


def lay_out(inputs):
    g = {k: np.asarray(v) for k, v in inputs.items()}
    a = {}
    a["x"] = g["L0_attn_x"]
    a["cT"] = np.stack([g["L0_c"].T, g["L1_c"].T])
    a["wmod"] = np.stack([g["L0_wmod"], g["L1_wmod"]])
    cols = np.zeros((P, NCOL), np.float32)
    src = {"bz_f": "L0_attn_bz_f", "bh_f": "L0_attn_bh_f", "bz_b": "L0_attn_bz_b", "bh_b": "L0_attn_bh_b",
           "bf": "L0_ffn_bf", "bi": "L0_ffn_bi", "bc": "L0_ffn_bc", "in_c": "L0_ffn_in_c",
           "ln1_g": "L1_attn_ln1_g", "ln1_b": "L1_attn_ln1_b", "ln2_g": "L1_attn_ln2_g",
           "ln2_b": "L1_attn_ln2_b", "b1": "L1_attn_b1"}
    for name, key in src.items():
        v = g[key].reshape(-1, P).T
        cols[:, COL[name]:COL[name] + v.shape[1]] = v
    a["cols"] = cols
    a["rows"] = np.stack([g["L0_attn_b_out"], g["L0_ffn_bo"], g["L1_attn_bo"], g["L1_attn_b2"]])
    a["wg"] = np.stack([g["L0_attn_Wz_f"], g["L0_attn_Wh_f"], g["L0_attn_Wz_b"], g["L0_attn_Wh_b"]])
    a["wo0"] = g["L0_attn_W_out"]
    l1 = "L1_attn_"
    heads = lambda w: w.T.reshape(DM, H_, D_, 2).transpose(0, 3, 1, 2).reshape(DM, DM)
    a["w_qk"] = np.concatenate([heads(g[l1 + "Wq"]), heads(g[l1 + "Wk"])], axis=1)
    a["w_v"], a["w_o"] = g[l1 + "Wv"].T, g[l1 + "Wo"].T
    a["lam"] = np.stack([g[l1 + n] for n in ("lq1", "lq2", "lk1", "lk2")])
    a["w1"], a["w2"] = g[l1 + "W1"].T, g[l1 + "W2"].T
    f1 = "L1_ffn_"
    a["w_red"], a["wgT"] = g[f1 + "w_red"], g[f1 + "wg"].T
    a["moe_w1"], a["moe_w2"], a["moe_b1"], a["moe_b2"] = (g[f1 + n] for n in ("W1", "W2", "b1", "b2"))
    p = np.arange(P)[:, None]
    a["maskK"] = np.where(p // D_ % 4 == np.arange(4), D_ ** -0.5, 0.0).astype(np.float32)
    j, kind, head = p // NH, p // H_ % 2, p % H_
    col = np.arange(64)
    a["combine"] = np.stack([(kind == n) & (j == col // H_) & (head == col % H_) for n in range(2)], 1
                            ).astype(np.float32)
    a["maskV"] = (p // H_ == np.arange(G8)).astype(np.float32)
    f = "L0_ffn_"
    a["w_ffn"] = np.stack([g[f + n].T for n in ("wf", "uf", "wi", "ui", "wc", "uc", "wo", "uo")])
    return a


def kernel(**inputs):
    import concourse.bacc as bacc
    from concourse.bass_utils import run_bass_kernel_spmd

    arrays = {f"in_{n}": np.ascontiguousarray(a) for n, a in lay_out(inputs).items()}
    nc = bacc.Bacc("TRN2", target_bir_lowering=False, num_devices=1)
    d = {n[3:]: nc.dram_tensor(n, a.shape, mybir.dt.from_np(a.dtype), kind="ExternalInput").ap()
         for n, a in arrays.items()}
    out = nc.dram_tensor("out", (B, S, DM), F32, kind="ExternalOutput").ap()
    program(nc, d, out)
    r = run_bass_kernel_spmd(nc, [arrays], core_ids=[0])
    return r.results[0]["out"]
```
